# Optimizing a Trainium2 kernel written in Bass

```python
import numpy as np
import jax
import jax.numpy as jnp

def _softmax(x, axis=-1):
    return jax.nn.softmax(x, axis=axis)

def _gelu(x):
    return jax.nn.gelu(x, approximate=True)

def _silu(x):
    return jax.nn.silu(x)

def _sigmoid(x):
    return jax.nn.sigmoid(x)

def _layernorm(x, axis=-1, eps=1e-05):
    m = jnp.mean(x, axis=axis, keepdims=True)
    v = jnp.var(x, axis=axis, keepdims=True)
    return (x - m) / jnp.sqrt(v + eps)

def _scatter_add(tgt, idx, src, axis=0):
    return tgt.at[idx].add(src)

def _segment_sum(src, seg, n):
    return jax.ops.segment_sum(src, seg, n)
kernel_name = 'mk_decoder_postln_d1_seqx_r8_453534'

def setup_inputs(seed: int=0):
    np.random.seed(seed)
    _w = jnp.asarray

    def _rec_inputs():
        import jax
        import jax.numpy as jnp
        _rk = jax.random.key(seed)
        x = -0.0002928 + 1 * jax.random.normal(jax.random.fold_in(_rk, 1), (2, 512, 128), jnp.float32)
        _lenS = 512 - jax.random.randint(jax.random.fold_in(_rk, 7), (2,), 0, max(1, 512 // 4) + 1, jnp.int32)
        _lenS2 = 32 - jax.random.randint(jax.random.fold_in(_rk, 8), (2,), 0, max(1, 32 // 4) + 1, jnp.int32)
        _ctx_1024P = jax.random.normal(jax.random.fold_in(_rk, 11), (2, 16, 128), jnp.float32)
        _ctx_1024c = jax.random.dirichlet(jax.random.fold_in(_rk, 511), 0.3 * jnp.ones((16,), jnp.float32), (2, 32))
        _ctx_1024t = jnp.einsum('bsk,bkd->bsd', _ctx_1024c, _ctx_1024P)
        _ctx_1024t = _ctx_1024t * jax.lax.rsqrt(jnp.mean(jnp.square(_ctx_1024t)) + 1e-12) * 0.953939
        ctx_1024 = -1.39393e-06 + 0.999914 * (_ctx_1024t + 0.3 * jax.random.normal(jax.random.fold_in(_rk, 611), (2, 32, 128), jnp.float32))
        return (x, ctx_1024)
    x, ctx_1024 = _rec_inputs()

    def _L0_attn_setup():
        import jax, jax.numpy as jnp
        import numpy as np
        D_MODEL = 128
        D_INNER = 256
        D_STATE = 16
        D_CONV = 4
        DT_RANK = 64
        N_EXPERTS = 8
        TOP_K = 2
        FFN = 512
        EPS = 1e-05

        def rmsnorm(x, w):
            return x * jax.lax.rsqrt(jnp.mean(x * x, axis=-1, keepdims=True) + EPS) * w

        def mamba_block(x, in_proj_w, conv_w, conv_b, x_proj_w, dt_proj_w, dt_proj_b, A_log, D_skip, out_proj_w):
            B, L, _ = x.shape
            xz = x @ in_proj_w
            xi, z = jnp.split(xz, 2, axis=-1)
            xc = jax.lax.conv_general_dilated(xi.transpose(0, 2, 1), conv_w, window_strides=(1,), padding=[(D_CONV - 1, 0)], feature_group_count=D_INNER, dimension_numbers=('NCH', 'OIH', 'NCH'))
            xi = jax.nn.silu(xc.transpose(0, 2, 1) + conv_b)
            dbc = xi @ x_proj_w
            delta = jax.nn.softplus(dbc[..., :DT_RANK] @ dt_proj_w + dt_proj_b)
            Bm = dbc[..., DT_RANK:DT_RANK + D_STATE]
            Cm = dbc[..., DT_RANK + D_STATE:]
            A = -jnp.exp(A_log)

            def step(h, inp):
                d_t, B_t, C_t, x_t = inp
                dA = jnp.exp(d_t[..., None] * A)
                h = dA * h + (d_t * x_t)[..., None] * B_t[:, None, :]
                y = jnp.einsum('ben,bn->be', h, C_t)
                return (h, y)
            h0 = jnp.zeros((B, D_INNER, D_STATE), dtype=x.dtype)
            xs = (delta.transpose(1, 0, 2), Bm.transpose(1, 0, 2), Cm.transpose(1, 0, 2), xi.transpose(1, 0, 2))
            _, ys = jax.lax.scan(step, h0, xs)
            y = ys.transpose(1, 0, 2) + D_skip * xi
            y = y * jax.nn.silu(z)
            return y @ out_proj_w

        def moe_block(x, router_w, Wg, Wu, Wd):
            B, L, D = x.shape
            hs = x.reshape(-1, D)
            router_logits = hs @ router_w
            rw = jax.nn.softmax(router_logits.astype(jnp.float32), axis=-1)
            top_w, sel = jax.lax.top_k(rw, TOP_K)
            top_w = top_w.astype(hs.dtype)
            out = jnp.zeros_like(hs)
            for e in range(N_EXPERTS):
                w_e = jnp.where(sel == e, top_w, 0.0).sum(axis=-1)
                ye = jax.nn.silu(hs @ Wg[e]) * (hs @ Wu[e]) @ Wd[e]
                out = out + w_e[:, None] * ye
            return (out.reshape(B, L, D), router_logits)
        key = jax.random.key(seed)
        ks = jax.random.split(key, 16)
        s = 0.02
        inp = {'hidden_states': jax.random.normal(ks[0], (2, 256, D_MODEL), jnp.float32), 'rms1_w': jnp.ones((D_MODEL,), jnp.float32), 'rms2_w': jnp.ones((D_MODEL,), jnp.float32), 'in_proj_w': jax.random.normal(ks[1], (D_MODEL, 2 * D_INNER), jnp.float32) * s, 'conv_w': jax.random.normal(ks[2], (D_INNER, 1, D_CONV), jnp.float32) * s, 'conv_b': jnp.zeros((D_INNER,), jnp.float32), 'x_proj_w': jax.random.normal(ks[3], (D_INNER, DT_RANK + 2 * D_STATE), jnp.float32) * s, 'dt_proj_w': jax.random.normal(ks[4], (DT_RANK, D_INNER), jnp.float32) * s, 'dt_proj_b': jnp.zeros((D_INNER,), jnp.float32), 'A_log': jnp.log(jnp.tile(jnp.arange(1, D_STATE + 1, dtype=jnp.float32), (D_INNER, 1))), 'D_skip': jnp.ones((D_INNER,), jnp.float32), 'out_proj_w': jax.random.normal(ks[5], (D_INNER, D_MODEL), jnp.float32) * s, 'router_w': jax.random.normal(ks[6], (D_MODEL, N_EXPERTS), jnp.float32) * s, 'Wg': jax.random.normal(ks[7], (N_EXPERTS, D_MODEL, FFN), jnp.float32) * s, 'Wu': jax.random.normal(ks[8], (N_EXPERTS, D_MODEL, FFN), jnp.float32) * s, 'Wd': jax.random.normal(ks[9], (N_EXPERTS, FFN, D_MODEL), jnp.float32) * s}
        return inp
    _L0_attn_all = _L0_attn_setup()
    _L0_attn_in = {k: v for k, v in _L0_attn_all.items() if k in ('rms1_w', 'rms2_w', 'in_proj_w', 'conv_w', 'conv_b', 'x_proj_w', 'dt_proj_w', 'dt_proj_b', 'A_log', 'D_skip', 'out_proj_w', 'router_w', 'Wg', 'Wu', 'Wd')}
    del _L0_attn_all

    def _L0_xattn_setup():
        import jax, jax.numpy as jnp
        import numpy as np
        E = 128
        H = 16
        D = E // H
        NUM_BUCKETS = 32
        MAX_DISTANCE = 128

        def _relative_position_bucket(rel, num_buckets=NUM_BUCKETS, max_distance=MAX_DISTANCE):
            nb = num_buckets // 2
            buckets = (rel > 0).astype(jnp.int32) * nb
            rel = jnp.abs(rel)
            max_exact = nb // 2
            is_small = rel < max_exact
            rel_f = jnp.maximum(rel, 1).astype(jnp.float32)
            large = max_exact + (jnp.log(rel_f / max_exact) / np.log(max_distance / max_exact) * (nb - max_exact)).astype(jnp.int32)
            large = jnp.minimum(large, nb - 1)
            return buckets + jnp.where(is_small, rel, large)
        key = jax.random.key(seed)
        ks = jax.random.split(key, 6)
        B, S, K = (2, 256, 256)
        w = 0.02
        return {'hidden_states': jax.random.normal(ks[0], (B, S, E), jnp.float32), 'key_value_states': jax.random.normal(ks[1], (B, K, E), jnp.float32), 'Wq': jax.random.normal(ks[2], (E, E), jnp.float32) * w, 'Wkv': jax.random.normal(ks[3], (E, 2 * E), jnp.float32) * w, 'Wo': jax.random.normal(ks[4], (E, E), jnp.float32) * w, 'rel_bias': jax.random.normal(ks[5], (NUM_BUCKETS, H), jnp.float32) * w}
    _L0_xattn_all = _L0_xattn_setup()
    _L0_xattn_in = {k: v for k, v in _L0_xattn_all.items() if k in ('Wq', 'Wkv', 'Wo', 'rel_bias')}
    del _L0_xattn_all

    def _L0_ffn_setup():
        import jax, jax.numpy as jnp
        import numpy as np
        DIM = 128
        DEPTH = 6
        HEADS = 16
        DIM_HEAD = 64
        WINDOW = 32
        INNER = HEADS * DIM_HEAD
        DIM_INNER = int(DIM * 4 * 2 / 3)
        QK_SCALE = 8.0

        def shift_tokens(t):
            a, s = jnp.split(t, 2, -1)
            s = jnp.pad(s, ((0, 0), (1, 0), (0, 0)))[:, :-1]
            return jnp.concatenate([a, s], -1)

        def l2norm(t):
            return t / jnp.maximum(jnp.linalg.norm(t, axis=-1, keepdims=True), 1e-12)

        def rotate_half(x):
            x1, x2 = jnp.split(x, 2, -1)
            return jnp.concatenate([-x2, x1], -1)

        def rotary_tables(n):
            half = jnp.arange(0, DIM_HEAD, 2, dtype=jnp.float32)
            inv_freq = 1.0 / 10000.0 ** (half / DIM_HEAD)
            t = jnp.arange(n, dtype=jnp.float32)
            freqs = t[:, None] * inv_freq[None, :]
            freqs = jnp.concatenate([freqs, freqs], -1)
            base_scale = (half + 0.4 * DIM_HEAD) / (1.4 * DIM_HEAD)
            power = (t - n // 2) / (WINDOW // 2)
            scale = base_scale[None, :] ** power[:, None]
            scale = jnp.concatenate([scale, scale], -1)
            return (freqs, scale)

        def local_attention(q, k, v):
            b, h, n, d = q.shape
            w = WINDOW
            nw = n // w
            bq = q.reshape(b, h, nw, w, d)
            bk = k.reshape(b, h, nw, w, d)
            bv = v.reshape(b, h, nw, w, d)

            def look(t):
                p = jnp.pad(t, ((0, 0), (0, 0), (1, 0), (0, 0), (0, 0)))
                return jnp.concatenate([p[:, :, :nw], p[:, :, 1:]], axis=3)
            bk2, bv2 = (look(bk), look(bv))
            seq = jnp.arange(n).reshape(nw, w)
            seq_p = jnp.pad(seq, ((1, 0), (0, 0)), constant_values=-1)
            jt = jnp.concatenate([seq_p[:nw], seq_p[1:]], axis=1)
            it = seq[:, :, None]
            jb = jt[:, None, :]
            mask = (it < jb) | (it > jb + w) | (jb == -1)
            sim = jnp.einsum('bhwie,bhwje->bhwij', bq, bk2) * QK_SCALE
            sim = jnp.where(mask, -jnp.finfo(sim.dtype).max, sim)
            attn = jax.nn.softmax(sim, -1)
            out = jnp.einsum('bhwij,bhwje->bhwie', attn, bv2)
            return out.reshape(b, h, n, d)

        def attn_layer(x, Wqkv, qs, ksc, Wo):
            b, n, _ = x.shape
            qkv = x @ Wqkv
            q, k, v = jnp.split(qkv, 3, -1)
            sh = lambda t: t.reshape(b, n, HEADS, DIM_HEAD).transpose(0, 2, 1, 3)
            q, k, v = (sh(q), sh(k), sh(v))
            q = l2norm(q) * qs
            k = l2norm(k) * ksc
            freqs, scale = rotary_tables(n)
            cos, sin = (jnp.cos(freqs), jnp.sin(freqs))
            q = q * cos * scale + rotate_half(q) * sin * scale
            inv = 1.0 / scale
            k = k * cos * inv + rotate_half(k) * sin * inv
            out = local_attention(q, k, v)
            out = out.transpose(0, 2, 1, 3).reshape(b, n, INNER)
            return out @ Wo

        def ffn_layer(x, g, bln, W1, b1, W2, b2):
            mu = x.mean(-1, keepdims=True)
            var = ((x - mu) ** 2).mean(-1, keepdims=True)
            xn = (x - mu) / jnp.sqrt(var + 1e-05) * g + bln
            hg = xn @ W1 + b1
            a, gate = jnp.split(hg, 2, -1)
            return a * jax.nn.gelu(gate, approximate=False) @ W2 + b2
        key = jax.random.key(seed)
        ks = jax.random.split(key, 8)
        B, N = (2, 256)
        init = lambda k, shape: jax.random.normal(k, shape, jnp.float32) * 0.02
        return {'x': jax.random.normal(ks[0], (B, N, DIM), jnp.float32), 'Wqkv': init(ks[1], (DEPTH, DIM, 3 * INNER)), 'q_scale': jnp.ones((DEPTH, DIM_HEAD), jnp.float32), 'k_scale': jnp.ones((DEPTH, DIM_HEAD), jnp.float32), 'Wo': init(ks[2], (DEPTH, INNER, DIM)), 'ln_g': jnp.ones((DEPTH, DIM), jnp.float32), 'ln_b': jnp.zeros((DEPTH, DIM), jnp.float32), 'W1': init(ks[3], (DEPTH, DIM, 2 * DIM_INNER)), 'b1': jnp.zeros((DEPTH, 2 * DIM_INNER), jnp.float32), 'W2': init(ks[4], (DEPTH, DIM_INNER, DIM)), 'b2': jnp.zeros((DEPTH, DIM), jnp.float32)}
    _L0_ffn_all = _L0_ffn_setup()
    _L0_ffn_in = {k: v for k, v in _L0_ffn_all.items() if k in ('Wqkv', 'q_scale', 'k_scale', 'Wo', 'ln_g', 'ln_b', 'W1', 'b1', 'W2', 'b2')}
    del _L0_ffn_all
    return {'x': x, 'ctx_1024': ctx_1024, 'L0_attn_rms1_w': _L0_attn_in['rms1_w'], 'L0_attn_rms2_w': _L0_attn_in['rms2_w'], 'L0_attn_in_proj_w': _L0_attn_in['in_proj_w'], 'L0_attn_conv_w': _L0_attn_in['conv_w'], 'L0_attn_conv_b': _L0_attn_in['conv_b'], 'L0_attn_x_proj_w': _L0_attn_in['x_proj_w'], 'L0_attn_dt_proj_w': _L0_attn_in['dt_proj_w'], 'L0_attn_dt_proj_b': _L0_attn_in['dt_proj_b'], 'L0_attn_A_log': _L0_attn_in['A_log'], 'L0_attn_D_skip': _L0_attn_in['D_skip'], 'L0_attn_out_proj_w': _L0_attn_in['out_proj_w'], 'L0_attn_router_w': _L0_attn_in['router_w'], 'L0_attn_Wg': _L0_attn_in['Wg'], 'L0_attn_Wu': _L0_attn_in['Wu'], 'L0_attn_Wd': _L0_attn_in['Wd'], 'L0_xattn_Wq': _L0_xattn_in['Wq'], 'L0_xattn_Wkv': _L0_xattn_in['Wkv'], 'L0_xattn_Wo': _L0_xattn_in['Wo'], 'L0_xattn_rel_bias': _L0_xattn_in['rel_bias'], 'L0_ffn_Wqkv': _L0_ffn_in['Wqkv'], 'L0_ffn_q_scale': _L0_ffn_in['q_scale'], 'L0_ffn_k_scale': _L0_ffn_in['k_scale'], 'L0_ffn_Wo': _L0_ffn_in['Wo'], 'L0_ffn_ln_g': _L0_ffn_in['ln_g'], 'L0_ffn_ln_b': _L0_ffn_in['ln_b'], 'L0_ffn_W1': _L0_ffn_in['W1'], 'L0_ffn_b1': _L0_ffn_in['b1'], 'L0_ffn_W2': _L0_ffn_in['W2'], 'L0_ffn_b2': _L0_ffn_in['b2']}

def reference(x, ctx_1024, L0_attn_rms1_w, L0_attn_rms2_w, L0_attn_in_proj_w, L0_attn_conv_w, L0_attn_conv_b, L0_attn_x_proj_w, L0_attn_dt_proj_w, L0_attn_dt_proj_b, L0_attn_A_log, L0_attn_D_skip, L0_attn_out_proj_w, L0_attn_router_w, L0_attn_Wg, L0_attn_Wu, L0_attn_Wd, L0_xattn_Wq, L0_xattn_Wkv, L0_xattn_Wo, L0_xattn_rel_bias, L0_ffn_Wqkv, L0_ffn_q_scale, L0_ffn_k_scale, L0_ffn_Wo, L0_ffn_ln_g, L0_ffn_ln_b, L0_ffn_W1, L0_ffn_b1, L0_ffn_W2, L0_ffn_b2):
    import jax
    import jax.numpy as jnp

    def _L0_attn_ref(hidden_states, rms1_w, rms2_w, in_proj_w, conv_w, conv_b, x_proj_w, dt_proj_w, dt_proj_b, A_log, D_skip, out_proj_w, router_w, Wg, Wu, Wd):
        import jax, jax.numpy as jnp
        import numpy as np
        D_MODEL = 128
        D_INNER = 256
        D_STATE = 16
        D_CONV = 4
        DT_RANK = 64
        N_EXPERTS = 8
        TOP_K = 2
        FFN = 512
        EPS = 1e-05

        def rmsnorm(x, w):
            return x * jax.lax.rsqrt(jnp.mean(x * x, axis=-1, keepdims=True) + EPS) * w

        def mamba_block(x, in_proj_w, conv_w, conv_b, x_proj_w, dt_proj_w, dt_proj_b, A_log, D_skip, out_proj_w):
            B, L, _ = x.shape
            xz = x @ in_proj_w
            xi, z = jnp.split(xz, 2, axis=-1)
            xc = jax.lax.conv_general_dilated(xi.transpose(0, 2, 1), conv_w, window_strides=(1,), padding=[(D_CONV - 1, 0)], feature_group_count=D_INNER, dimension_numbers=('NCH', 'OIH', 'NCH'))
            xi = jax.nn.silu(xc.transpose(0, 2, 1) + conv_b)
            dbc = xi @ x_proj_w
            delta = jax.nn.softplus(dbc[..., :DT_RANK] @ dt_proj_w + dt_proj_b)
            Bm = dbc[..., DT_RANK:DT_RANK + D_STATE]
            Cm = dbc[..., DT_RANK + D_STATE:]
            A = -jnp.exp(A_log)

            def step(h, inp):
                d_t, B_t, C_t, x_t = inp
                dA = jnp.exp(d_t[..., None] * A)
                h = dA * h + (d_t * x_t)[..., None] * B_t[:, None, :]
                y = jnp.einsum('ben,bn->be', h, C_t)
                return (h, y)
            h0 = jnp.zeros((B, D_INNER, D_STATE), dtype=x.dtype)
            xs = (delta.transpose(1, 0, 2), Bm.transpose(1, 0, 2), Cm.transpose(1, 0, 2), xi.transpose(1, 0, 2))
            _, ys = jax.lax.scan(step, h0, xs)
            y = ys.transpose(1, 0, 2) + D_skip * xi
            y = y * jax.nn.silu(z)
            return y @ out_proj_w

        def moe_block(x, router_w, Wg, Wu, Wd):
            B, L, D = x.shape
            hs = x.reshape(-1, D)
            router_logits = hs @ router_w
            rw = jax.nn.softmax(router_logits.astype(jnp.float32), axis=-1)
            top_w, sel = jax.lax.top_k(rw, TOP_K)
            top_w = top_w.astype(hs.dtype)
            out = jnp.zeros_like(hs)
            for e in range(N_EXPERTS):
                w_e = jnp.where(sel == e, top_w, 0.0).sum(axis=-1)
                ye = jax.nn.silu(hs @ Wg[e]) * (hs @ Wu[e]) @ Wd[e]
                out = out + w_e[:, None] * ye
            return (out.reshape(B, L, D), router_logits)
        residual = hidden_states
        h = rmsnorm(hidden_states, rms1_w)
        h = mamba_block(h, in_proj_w, conv_w, conv_b, x_proj_w, dt_proj_w, dt_proj_b, A_log, D_skip, out_proj_w)
        h = residual + h
        residual = h
        h = rmsnorm(h, rms2_w)
        h, router_logits = moe_block(h, router_w, Wg, Wu, Wd)
        h = residual + h
        return h

    def _L0_xattn_ref(hidden_states, key_value_states, Wq, Wkv, Wo, rel_bias):
        import jax, jax.numpy as jnp
        import numpy as np
        E = 128
        H = 16
        D = E // H
        NUM_BUCKETS = 32
        MAX_DISTANCE = 128

        def _relative_position_bucket(rel, num_buckets=NUM_BUCKETS, max_distance=MAX_DISTANCE):
            nb = num_buckets // 2
            buckets = (rel > 0).astype(jnp.int32) * nb
            rel = jnp.abs(rel)
            max_exact = nb // 2
            is_small = rel < max_exact
            rel_f = jnp.maximum(rel, 1).astype(jnp.float32)
            large = max_exact + (jnp.log(rel_f / max_exact) / np.log(max_distance / max_exact) * (nb - max_exact)).astype(jnp.int32)
            large = jnp.minimum(large, nb - 1)
            return buckets + jnp.where(is_small, rel, large)
        B, S, _ = hidden_states.shape
        K = key_value_states.shape[1]
        q = (hidden_states @ Wq).reshape(B, S, H, D).transpose(0, 2, 1, 3)
        kv = (key_value_states @ Wkv).reshape(B, K, 2, H, D)
        k = kv[:, :, 0].transpose(0, 2, 1, 3)
        v = kv[:, :, 1].transpose(0, 2, 1, 3)
        scores = jnp.einsum('bhsd,bhkd->bhsk', q, k)
        rel = jnp.arange(K)[None, :] - jnp.arange(S)[:, None]
        buckets = _relative_position_bucket(rel)
        bias = rel_bias[buckets].transpose(2, 0, 1)[None]
        scores = scores + bias
        attn = jax.nn.softmax(scores.astype(jnp.float32), axis=-1).astype(scores.dtype)
        out = jnp.einsum('bhsk,bhkd->bshd', attn, v).reshape(B, S, E)
        return out @ Wo

    def _L0_ffn_ref(x, Wqkv, q_scale, k_scale, Wo, ln_g, ln_b, W1, b1, W2, b2):
        import jax, jax.numpy as jnp
        import numpy as np
        DIM = 128
        DEPTH = 6
        HEADS = 16
        DIM_HEAD = 64
        WINDOW = 32
        INNER = HEADS * DIM_HEAD
        DIM_INNER = int(DIM * 4 * 2 / 3)
        QK_SCALE = 8.0

        def shift_tokens(t):
            a, s = jnp.split(t, 2, -1)
            s = jnp.pad(s, ((0, 0), (1, 0), (0, 0)))[:, :-1]
            return jnp.concatenate([a, s], -1)

        def l2norm(t):
            return t / jnp.maximum(jnp.linalg.norm(t, axis=-1, keepdims=True), 1e-12)

        def rotate_half(x):
            x1, x2 = jnp.split(x, 2, -1)
            return jnp.concatenate([-x2, x1], -1)

        def rotary_tables(n):
            half = jnp.arange(0, DIM_HEAD, 2, dtype=jnp.float32)
            inv_freq = 1.0 / 10000.0 ** (half / DIM_HEAD)
            t = jnp.arange(n, dtype=jnp.float32)
            freqs = t[:, None] * inv_freq[None, :]
            freqs = jnp.concatenate([freqs, freqs], -1)
            base_scale = (half + 0.4 * DIM_HEAD) / (1.4 * DIM_HEAD)
            power = (t - n // 2) / (WINDOW // 2)
            scale = base_scale[None, :] ** power[:, None]
            scale = jnp.concatenate([scale, scale], -1)
            return (freqs, scale)

        def local_attention(q, k, v):
            b, h, n, d = q.shape
            w = WINDOW
            nw = n // w
            bq = q.reshape(b, h, nw, w, d)
            bk = k.reshape(b, h, nw, w, d)
            bv = v.reshape(b, h, nw, w, d)

            def look(t):
                p = jnp.pad(t, ((0, 0), (0, 0), (1, 0), (0, 0), (0, 0)))
                return jnp.concatenate([p[:, :, :nw], p[:, :, 1:]], axis=3)
            bk2, bv2 = (look(bk), look(bv))
            seq = jnp.arange(n).reshape(nw, w)
            seq_p = jnp.pad(seq, ((1, 0), (0, 0)), constant_values=-1)
            jt = jnp.concatenate([seq_p[:nw], seq_p[1:]], axis=1)
            it = seq[:, :, None]
            jb = jt[:, None, :]
            mask = (it < jb) | (it > jb + w) | (jb == -1)
            sim = jnp.einsum('bhwie,bhwje->bhwij', bq, bk2) * QK_SCALE
            sim = jnp.where(mask, -jnp.finfo(sim.dtype).max, sim)
            attn = jax.nn.softmax(sim, -1)
            out = jnp.einsum('bhwij,bhwje->bhwie', attn, bv2)
            return out.reshape(b, h, n, d)

        def attn_layer(x, Wqkv, qs, ksc, Wo):
            b, n, _ = x.shape
            qkv = x @ Wqkv
            q, k, v = jnp.split(qkv, 3, -1)
            sh = lambda t: t.reshape(b, n, HEADS, DIM_HEAD).transpose(0, 2, 1, 3)
            q, k, v = (sh(q), sh(k), sh(v))
            q = l2norm(q) * qs
            k = l2norm(k) * ksc
            freqs, scale = rotary_tables(n)
            cos, sin = (jnp.cos(freqs), jnp.sin(freqs))
            q = q * cos * scale + rotate_half(q) * sin * scale
            inv = 1.0 / scale
            k = k * cos * inv + rotate_half(k) * sin * inv
            out = local_attention(q, k, v)
            out = out.transpose(0, 2, 1, 3).reshape(b, n, INNER)
            return out @ Wo

        def ffn_layer(x, g, bln, W1, b1, W2, b2):
            mu = x.mean(-1, keepdims=True)
            var = ((x - mu) ** 2).mean(-1, keepdims=True)
            xn = (x - mu) / jnp.sqrt(var + 1e-05) * g + bln
            hg = xn @ W1 + b1
            a, gate = jnp.split(hg, 2, -1)
            return a * jax.nn.gelu(gate, approximate=False) @ W2 + b2
        for i in range(DEPTH):
            x = attn_layer(shift_tokens(x), Wqkv[i], q_scale[i], k_scale[i], Wo[i]) + x
            x = ffn_layer(shift_tokens(x), ln_g[i], ln_b[i], W1[i], b1[i], W2[i], b2[i]) + x
        return x
    x = _layernorm(x + _L0_attn_ref(x, L0_attn_rms1_w, L0_attn_rms2_w, L0_attn_in_proj_w, L0_attn_conv_w, L0_attn_conv_b, L0_attn_x_proj_w, L0_attn_dt_proj_w, L0_attn_dt_proj_b, L0_attn_A_log, L0_attn_D_skip, L0_attn_out_proj_w, L0_attn_router_w, L0_attn_Wg, L0_attn_Wu, L0_attn_Wd), axis=-1)
    x = _layernorm(x + _L0_xattn_ref(x, ctx_1024, L0_xattn_Wq, L0_xattn_Wkv, L0_xattn_Wo, L0_xattn_rel_bias), axis=-1)
    x = _layernorm(x + _L0_ffn_ref(x, L0_ffn_Wqkv, L0_ffn_q_scale, L0_ffn_k_scale, L0_ffn_Wo, L0_ffn_ln_g, L0_ffn_ln_b, L0_ffn_W1, L0_ffn_b1, L0_ffn_W2, L0_ffn_b2), axis=-1)
    return x

_drawn_inputs = setup_inputs


def setup_inputs(seed=0):
    import zlib

    import numpy as np

    out = dict(_drawn_inputs(seed))
    spreads = {'L0_attn_rms1_w': (1.0, 0.6),
     'L0_attn_rms2_w': (1.0, 0.6),
     'L0_attn_conv_b': (0.0, 0.8),
     'L0_attn_dt_proj_b': (0.0, 0.8),
     'L0_attn_D_skip': (1.0, 0.6),
     'L0_ffn_q_scale': (1.0, 0.6),
     'L0_ffn_k_scale': (1.0, 0.6),
     'L0_ffn_ln_g': (1.0, 0.6),
     'L0_ffn_ln_b': (0.0, 0.8),
     'L0_ffn_b1': (0.0, 0.8),
     'L0_ffn_b2': (0.0, 0.1)}
    factors = {'L0_attn_in_proj_w': 8.0,
     'L0_attn_conv_w': 8.0,
     'L0_attn_x_proj_w': 8.0,
     'L0_attn_dt_proj_w': 8.0,
     'L0_attn_A_log': 8.0,
     'L0_attn_out_proj_w': 8.0,
     'L0_attn_router_w': 8.0,
     'L0_attn_Wg': 8.0,
     'L0_attn_Wu': 8.0,
     'L0_attn_Wd': 8.0,
     'L0_xattn_Wq': 24.939,
     'L0_xattn_rel_bias': 64.0,
     'L0_ffn_W1': 3.682,
     'L0_ffn_W2': 3.614}
    for name, (base, spread) in spreads.items():
        noise = np.random.default_rng([zlib.crc32(name.encode()), seed]).standard_normal(out[name].shape)
        drawn = base * np.exp(spread * noise) if base else spread * noise
        out[name] = jnp.asarray(drawn.astype(out[name].dtype))
    for name, factor in factors.items():
        out[name] = (out[name] * factor).astype(out[name].dtype)
    return out
```

```python
import numpy as np
import concourse.bass as bass
from concourse import mybir
from contextlib import ExitStack

F32 = mybir.dt.float32
BF16 = mybir.dt.bfloat16
ACT = mybir.ActivationFunctionType
ALU = mybir.AluOpType
AX = mybir.AxisListType.X

P = 128
BATCH = 2
SEQ = 512
DIM = 128
LAYERS = 6
HEADS = 16
DH = 64
WIN = 32
DT_RANK = 64
STATES = 16
EXPERTS = 8
KEYS = 32
BUCKETS = 32
SPAN = SEQ + KEYS
HID = int(DIM * 4 * 2 / 3)
QK_SCALE = 8.0
SS_SCALE = 65536.0
HALF_SWAP = [(i + 16) % 32 for i in range(32)]


class Flow:

    def __init__(self, sem, per):
        self.sem = sem
        self.per = per

    def at(self, turn, n):
        return self.sem, turn * self.per + n


def at_layer(ap, turn):
    one = ap[bass.ds(turn, 1)]
    return one.rearrange("o p n -> (o p) n" if len(ap.shape) == 3 else "o p m n -> (o p) m n")


def expert(ap, turn, e):
    one = ap[bass.ds(turn * 2 + e, 1)]
    return one.rearrange("o p n -> (o p) n" if len(ap.shape) == 3 else "o p m n -> (o p) m n")


def norm_steps(nc, ctx):
    return {what: Flow(ctx.enter_context(nc.semaphore(f"norm_{what}")), 2)
            for what in ("mean", "centred", "square", "var", "ln", "rstd", "scaled")}


def build_mamba(nc, ctx, x, h1, d, C):
    def sb(name, shape, dt=F32):
        return ctx.enter_context(nc.sbuf_tensor("ma_" + name, shape, dt))

    def flow(name, per=0):
        return Flow(C["sems"].enter_context(nc.semaphore("ma_" + name)), per)

    ps = C["psum"]
    in_w = sb("in_w", [P, 4, P])
    xdt_w = sb("xdt_w", [P, 2, DT_RANK])
    xbc_w = sb("xbc_w", [P, 2, 96])
    dt_w = sb("dt_w", [DT_RANK, 2, P])
    out_w = sb("out_w", [P, 2, P])
    chan = sb("chan", [P, 2, 7])
    a_log = sb("a_log", [P, 2, STATES])
    rms_w = sb("rms_w", [P, 1])
    select = sb("select", [96, 2 * STATES, P], BF16)
    xsq = sb("xsq", [P, 2, SEQ])
    rn = sb("rn", [P, 2, SEQ])
    hn = sb("hn", [P, 2, SEQ])
    xi = sb("xi", [P, 2, 2, 3 + SEQ])
    sz = sb("sz", [P, 2, 2, SEQ])
    conv = sb("conv", [P, 2, 2, 2, SEQ])
    xc = sb("xc", [P, 2, 2, SEQ])
    dt = sb("dt", [DT_RANK, 2, SEQ])
    part = sb("part", [96, 3, 2, SEQ], BF16)
    rest = sb("rest", [96, 3, 2, SEQ])
    bc3 = sb("bc3", [96, 2, SEQ], BF16)
    pre = sb("pre", [P, 2, 2, SEQ])
    mag = sb("mag", [P, 2, 2, SEQ])
    delta = sb("delta", [P, 2, 2, SEQ])
    u = sb("u", [P, 2, 2, SEQ])
    a_neg = sb("a_neg", [P, 2, STATES])
    decay = sb("decay", [P, 4, 2, SEQ])
    bc = sb("bc", [P, 2, 2, SEQ])
    dbx = sb("dbx", [P, 4, SEQ])
    state = sb("state", [P, 2, SEQ])
    hc = sb("hc", [P, 4, SEQ])

    loaded, loaded2 = flow("loaded"), flow("loaded2")
    pads = flow("pads")
    xsq_done, ms_done, ln_done, r_done, hn_done = flow("xsq_done"), flow("ms_done"), flow("ln_done"), flow("r_done"), flow("hn_done")
    in_done, in_copied = flow("in_done"), flow("in_copied")
    conv_done, xc_done = flow("conv_done"), flow("xc_done")
    proj_done, dt_copied, split_done = flow("proj_done"), flow("dt_copied"), flow("split_done")
    dtp_done, pre_done, mag_done, sp_exp, sp_ln, delta_done, u_done = (flow(n) for n in (
        "dtp_done", "pre_done", "mag_done", "sp_exp", "sp_ln", "delta_done", "u_done"))
    aexp_done, aneg_done = flow("aexp_done"), flow("aneg_done")
    bc_done, bc_copied, decay_done, dbx_done, scan_done, hc_done, sum_done = (flow(n) for n in (
        "bc_done", "bc_copied", "decay_done", "dbx_done", "scan_done", "hc_done", "sum_done"))
    skip_done, gated_done, out_done, h1_done = flow("skip_done"), flow("gated_done"), flow("out_done"), flow("h1_done")

    def w(eng, f, n):
        if n > 0:
            eng.wait_ge(f.sem, n)

    block = ctx.enter_context(nc.Block())
    STEPS = [(k, b) for k in range(2) for b in range(2)]

    @block.sync
    def _(sp):
        sp.dma_start(rms_w[:], d["rms1"]).then_inc(loaded.sem, 16)
        sp.dma_start(in_w[:], d["in_w"]).then_inc(loaded.sem, 16)
        for dst, src in ((chan, "chan"), (a_log, "a_log"), (xdt_w, "xdt_w"), (xbc_w, "xbc_w"), (dt_w, "dt_w"), (out_w, "out_w"), (select, "select")):
            sp.dma_start(dst[:], d[src]).then_inc(loaded2.sem, 16)

    @block.tensor
    def _(pe):
        w(pe, C["const_in"], C["const_n"])
        for b in range(2):
            w(pe, xsq_done, b + 1)
            nc.tensor.matmul(ps[:, b, :], C["mean_ones"], xsq[:, b, :], start=True, stop=True).then_inc(ms_done.sem, 1)
        w(pe, loaded, 32)
        for b in range(2):
            w(pe, hn_done, b + 1)
            for m in range(4):
                nc.tensor.matmul(ps[:, (2 + 4 * b + m) % 8, :], in_w[:, m, :], hn[:, b, :], start=True, stop=True).then_inc(in_done.sem, 1)
        w(pe, loaded2, 112)
        w(pe, in_copied, 8)
        for b in range(2):
            w(pe, xc_done, 2 + b + 1)
            for k in range(2):
                nc.tensor.matmul(ps[0:DT_RANK, b, :], xdt_w[:, k, :], xc[:, k, b, :], start=(k == 0), stop=(k == 1))
            for k in range(2):
                last = nc.tensor.matmul(ps[0:96, 2 + b, :], xbc_w[:, k, :], xc[:, k, b, :], start=(k == 0), stop=(k == 1))
            last.then_inc(proj_done.sem, 1)
        for n, (k, b) in enumerate(STEPS):
            w(pe, dt_copied, b + 1)
            nc.tensor.matmul(ps[:, 4 + n, :], dt_w[:, k, :], dt[:, b, :], start=True, stop=True).then_inc(dtp_done.sem, 1)

        def broadcast(i):
            n, b = divmod(i, 2)
            w(pe, bc_copied, i - 1)
            for s in range(2):
                last = nc.tensor.matmul(ps[:, 4 + 2 * (i % 2) + s, :], select[:, STATES * s + n, :], bc3[:, b, :], start=True, stop=True)
            last.then_inc(bc_done.sem, 1)

        w(pe, split_done, 2)
        w(pe, mag_done, 4)
        broadcast(0)
        broadcast(1)
        w(pe, dt_copied, 2)
        for i in range(2 * STATES):
            n, b = divmod(i, 2)
            for k in range(2):
                j = 2 * i + k
                w(pe, hc_done, j + 1)
                nc.tensor.matmul(ps[:, 2 * k + b, :], C["ident"], hc[:, j % 4, :], start=(n == 0), stop=(n == STATES - 1)).then_inc(sum_done.sem, 1)
            if i + 2 < 2 * STATES:
                broadcast(i + 2)
        for b in range(2):
            w(pe, gated_done, 2 * b + 2)
            for k in range(2):
                last = nc.tensor.matmul(ps[:, 4 + b, :], out_w[:, k, :], xc[:, k, b, :], start=(k == 0), stop=(k == 1))
            last.then_inc(out_done.sem, 1)

    @block.scalar
    def _(ac):
        A = nc.scalar.activation
        nc.scalar.preload_act_table_set("natural_log_exp_and_others")
        w(ac, C["const_in"], C["const_n"])
        w(ac, C["fill"], C["fill_n"])
        for b in range(2):
            A(xsq[:, b, :], x[:, b, :], ACT.Square).then_inc(xsq_done.sem, 1)
        for b in range(2):
            w(ac, ms_done, b + 1)
            A(rn[:, b, :], ps[:, b, :], ACT.Ln, bias=C["eps"]).then_inc(ln_done.sem, 1)
            w(ac, ln_done, b + 1)
            A(rn[:, b, :], rn[:, b, :], ACT.Exp, scale=-0.5).then_inc(r_done.sem, 1)
        for b in range(2):
            for m in range(2):
                w(ac, in_done, 4 * b + m + 1)
                A(xi[:, m, b, 3:], ps[:, (2 + 4 * b + m) % 8, :], ACT.Copy).then_inc(in_copied.sem, 1)
        for b in range(2):
            for m in range(2, 4):
                w(ac, in_done, 4 * b + m + 1)
                A(sz[:, m - 2, b, :], ps[:, (2 + 4 * b + m) % 8, :], ACT.Silu).then_inc(in_copied.sem, 1)
        for b in range(2):
            for k in range(2):
                w(ac, conv_done, 8 * b + 4 * k + 4)
                A(xc[:, k, b, :], conv[:, 1, k, b, :], ACT.Silu, bias=chan[:, k, 4:5]).then_inc(xc_done.sem, 1)
        nc.scalar.preload_act_table_set("natural_log_exp_and_others")
        A(a_neg[:], a_log[:], ACT.Exp).then_inc(aexp_done.sem, 1)
        for b in range(2):
            w(ac, proj_done, b + 1)
            A(dt[:, b, :], ps[0:DT_RANK, b, :], ACT.Copy).then_inc(dt_copied.sem, 1)
        for n, (k, b) in enumerate(STEPS):
            w(ac, mag_done, n + 1)
            A(mag[:, k, b, :], mag[:, k, b, :], ACT.Exp).then_inc(sp_exp.sem, 1)
        for n, (k, b) in enumerate(STEPS):
            w(ac, sp_exp, n + 1)
            A(mag[:, k, b, :], mag[:, k, b, :], ACT.Ln, bias=C["one"]).then_inc(sp_ln.sem, 1)

        def copy_bc(i):
            w(ac, bc_done, i + 1)
            w(ac, hc_done, 2 * (i - 1))
            A(bc[:, i % 2], ps[:, 4 + 2 * (i % 2):6 + 2 * (i % 2), :], ACT.Copy).then_inc(bc_copied.sem, 1)

        w(ac, aneg_done, 1)
        w(ac, delta_done, 4)
        for n in range(STATES):
            for k in range(2):
                w(ac, scan_done, 4 * (n - 1))
                A(decay[:, 2 * (n % 2) + k], delta[:, k], ACT.Exp, scale=a_neg[:, k, n:n + 1]).then_inc(decay_done.sem, 1)
                copy_bc(2 * n + k)

    @block.vector
    def _(dv):
        v = nc.vector
        v.memset(xi[:, :, :, 0:3], 0.0).then_inc(pads.sem, 1)
        w(dv, C["const_in"], C["const_n"])
        w(dv, loaded, 32)
        for b in range(2):
            w(dv, r_done, b + 1)
            v.scalar_tensor_tensor(hn[:, b, :], x[:, b, :], rms_w[:, 0:1], rn[:, b, :], ALU.mult, ALU.mult).then_inc(hn_done.sem, 1)
        w(dv, loaded2, 112)
        w(dv, pads, 1)
        for b in range(2):
            for k in range(2):
                w(dv, in_copied, 2 * b + k + 1)
                v.tensor_scalar(conv[:, 0, k, b, :], xi[:, k, b, 0:SEQ], chan[:, k, 0:1], None, ALU.mult).then_inc(conv_done.sem, 1)
                for i in range(1, 4):
                    w(dv, conv_done, 8 * b + 4 * k + i)
                    v.scalar_tensor_tensor(conv[:, i % 2, k, b, :], xi[:, k, b, i:i + SEQ], chan[:, k, i:i + 1],
                                           conv[:, (i + 1) % 2, k, b, :], ALU.mult, ALU.add).then_inc(conv_done.sem, 1)
        w(dv, aexp_done, 1)
        v.tensor_scalar(a_neg[:], a_neg[:], -1.0, None, ALU.mult).then_inc(aneg_done.sem, 1)
        step = flow("split_step")
        at = 0
        for b in range(2):
            w(dv, proj_done, b + 1)
            v.tensor_copy(rest[:, 0, b, :], ps[0:96, 2 + b, :]).then_inc(step.sem, 1)
            for i in range(3):
                at += 1
                w(dv, step, at)
                v.tensor_copy(part[:, i, b, :], rest[:, i, b, :]).then_inc(step.sem, 1)
                at += 1
                w(dv, step, at)
                if i < 2:
                    v.tensor_tensor(rest[:, i + 1, b, :], rest[:, i, b, :], part[:, i, b, :], ALU.subtract).then_inc(step.sem, 1)
            for i in range(3):
                last = v.tensor_copy(bc3[32 * i:32 * i + 32, b, :], part[32 * i:32 * i + 32, i, b, :])
            last.then_inc(split_done.sem, 1)
        for n, (k, b) in enumerate(STEPS):
            w(dv, dtp_done, n + 1)
            v.tensor_scalar(pre[:, k, b, :], ps[:, 4 + n, :], chan[:, k, 5:6], None, ALU.add).then_inc(pre_done.sem, 1)
            w(dv, pre_done, n + 1)
            v.scalar_tensor_tensor(mag[:, k, b, :], pre[:, k, b, :], -1.0, pre[:, k, b, :], ALU.mult, ALU.min).then_inc(mag_done.sem, 1)
        for n, (k, b) in enumerate(STEPS):
            w(dv, sp_ln, n + 1)
            v.scalar_tensor_tensor(delta[:, k, b, :], pre[:, k, b, :], 0.0, mag[:, k, b, :], ALU.max, ALU.add).then_inc(delta_done.sem, 1)
            w(dv, delta_done, n + 1)
            w(dv, xc_done, 4)
            v.tensor_tensor(u[:, k, b, :], delta[:, k, b, :], xc[:, k, b, :], ALU.mult).then_inc(u_done.sem, 1)

        def times_c(j):
            w(dv, scan_done, j + 1)
            w(dv, sum_done, j - 3)
            v.tensor_tensor(hc[:, j % 4, :], state[:, j % 2, :], bc[:, j // 2 % 2, 1, :], ALU.mult).then_inc(hc_done.sem, 1)

        for j in range(4 * STATES):
            n, b, k = j // 4, j // 2 % 2, j % 2
            w(dv, dbx_done, j + 1)
            w(dv, decay_done, 2 * n + k + 1)
            w(dv, hc_done, j - 1)
            v.tensor_tensor_scan(state[:, j % 2, :], decay[:, 2 * (n % 2) + k, b, :], dbx[:, j % 4, :], 0.0, ALU.mult, ALU.add).then_inc(scan_done.sem, 1)
            if j >= 1:
                times_c(j - 1)
        times_c(4 * STATES - 1)
        for n, (b, k) in enumerate(STEPS):
            w(dv, sum_done, 4 * STATES)
            v.scalar_tensor_tensor(u[:, k, b, :], xc[:, k, b, :], chan[:, k, 6:7], ps[:, 2 * k + b, :], ALU.mult, ALU.add).then_inc(skip_done.sem, 1)
            w(dv, skip_done, n + 1)
            w(dv, in_copied, 8)
            v.tensor_tensor(xc[:, k, b, :], u[:, k, b, :], sz[:, k, b, :], ALU.mult).then_inc(gated_done.sem, 1)
        for b in range(2):
            w(dv, out_done, b + 1)
            v.tensor_tensor(h1[:, b, :], ps[:, 4 + b, :], x[:, b, :], ALU.add).then_inc(h1_done.sem, 1)
        w(dv, h1_done, 2)

    @block.gpsimd
    def _(pool):
        w(pool, u_done, 4)
        for j in range(4 * STATES):
            i, b, k = j // 2, j // 2 % 2, j % 2
            w(pool, bc_copied, i + 1)
            w(pool, scan_done, j - 3)
            nc.gpsimd.tensor_tensor(dbx[:, j % 4, :], u[:, k, b, :], bc[:, i % 2, 0, :], ALU.mult).then_inc(dbx_done.sem, 1)


def normalise(nc, who, eng, s, b, src, dst, work, rows, C, w):
    centred, ln = work
    if who == "pe_mean":
        nc.tensor.matmul(rows[0], C["mean_ones"], src, start=True, stop=True).then_inc(s["mean"].sem, 1)
    elif who == "dve_centre":
        eng.wait_ge(*s["mean"].at(s["use"], b + 1))
        nc.vector.tensor_tensor(centred[:, b, :], src, rows[0], ALU.subtract).then_inc(s["centred"].sem, 1)
    elif who == "act_square":
        eng.wait_ge(*s["centred"].at(s["use"], b + 1))
        nc.scalar.activation(ln[:, b, :], centred[:, b, :], ACT.Square).then_inc(s["square"].sem, 1)
    elif who == "pe_var":
        eng.wait_ge(*s["square"].at(s["use"], b + 1))
        nc.tensor.matmul(rows[1], C["mean_ones"], ln[:, b, :], start=True, stop=True).then_inc(s["var"].sem, 1)
    elif who == "act_rstd":
        eng.wait_ge(*s["var"].at(s["use"], b + 1))
        nc.scalar.activation(ln[:, b, :], rows[1], ACT.Ln, bias=C["eps"]).then_inc(s["ln"].sem, 1)
        eng.wait_ge(*s["ln"].at(s["use"], b + 1))
        nc.scalar.activation(ln[:, b, :], ln[:, b, :], ACT.Exp, scale=-0.5).then_inc(s["rstd"].sem, 1)
    elif who == "dve_scale":
        eng.wait_ge(*s["rstd"].at(s["use"], b + 1))
        nc.vector.tensor_tensor(dst, centred[:, b, :], ln[:, b, :], ALU.mult).then_inc(s["scaled"].sem, 1)


def build_moe(nc, ctx, x, h1, x1, d, C):
    def sb(name, shape, dt=F32):
        return ctx.enter_context(nc.sbuf_tensor("mo_" + name, shape, dt))

    def flow(name, per=0):
        return Flow(C["sems"].enter_context(nc.semaphore("mo_" + name)), per)

    ps = C["psum"]
    rms_w = sb("rms_w", [P, 1])
    router = sb("router", [P, EXPERTS])
    pick = sb("pick", [EXPERTS, EXPERTS, P])
    order = sb("order", [P, 8, EXPERTS])
    hsq = sb("hsq", [P, 2, SEQ])
    rn = sb("rn", [P, 2, SEQ])
    hn = sb("hn", [P, 2, SEQ])
    G = [sb(f"gate{i}", [P, 8, EXPERTS]) for i in range(7)]
    col = sb("col", [P, 8, 6])
    wT = sb("wT", [EXPERTS, 2, SEQ])
    w_all = sb("w_all", [P, EXPERTS, 2, SEQ])
    wg = sb("wg", [P, 2, 4 * P])
    wu = sb("wu", [P, 2, 4 * P])
    wd = sb("wd", [P, 2, 4, P])
    sg = sb("sg", [P, 2, SEQ])
    hid = sb("hid", [P, 8, SEQ])
    wy = sb("wy", [P, 2, SEQ])
    total = sb("total", [P, 2, SEQ])

    loaded = flow("loaded")
    hsq_done, ms_done, ln_done, r_done, hn_done = (flow(n) for n in ("hsq_done", "ms_done", "ln_done", "r_done", "hn_done"))
    logit_done, gexp_done, gate_step, weight_done = (flow(n) for n in ("logit_done", "gexp_done", "gate_step", "weight_done"))
    wt_done, wt_copied, wb_done, wb_copied = (flow(n) for n in ("wt_done", "wt_copied", "wb_done", "wb_copied"))
    w_in = [flow(f"w_in_{i}", 48) for i in range(2)]
    pair_done, silu_done, hid_done = flow("pair_done", 16), flow("silu_done", 16), flow("hid_done", 16)
    down_done, wy_done, acc_done, start_done = flow("down_done", 4), flow("wy_done", 4), flow("acc_done", 4), flow("start_done")
    s = C["norm"](0)

    def w(eng, f, n):
        if n > 0:
            eng.wait_ge(f.sem, n)

    block = ctx.enter_context(nc.Block())
    TURNS = EXPERTS // 2

    @block.sync
    def _(sp):
        for dst, src in ((rms_w, "rms2"), (router, "router"), (pick, "pick"), (order, "order")):
            sp.dma_start(dst[:], d[src]).then_inc(loaded.sem, 16)
        with sp.Fori(0, TURNS) as turn:
            for e in range(2):
                sp.wait_ge(*down_done.at(turn, 0) if e == 0 else down_done.at(turn, 0))
                w(sp, loaded, 64)
                sp.dma_start(wg[:, e, :], expert(d["wg"], turn, e)).then_inc(w_in[e].sem, 16)
                sp.dma_start(wu[:, e, :], expert(d["wu"], turn, e)).then_inc(w_in[e].sem, 16)
                sp.dma_start(wd[:, e, :, :], expert(d["wd"], turn, e)).then_inc(w_in[e].sem, 16)

    @block.tensor
    def _(pe):
        w(pe, loaded, 64)
        for b in range(2):
            w(pe, hsq_done, b + 1)
            nc.tensor.matmul(ps[:, b, :], C["mean_ones"], hsq[:, b, :], start=True, stop=True).then_inc(ms_done.sem, 1)
        for tile in range(8):
            b, t0 = tile // 4, tile % 4 * 128
            w(pe, hn_done, b + 1)
            last = nc.tensor.matmul(ps[:, 2, 8 * tile:8 * tile + 8], hn[:, b, t0:t0 + 128], router[:], start=True, stop=True)
        last.then_inc(logit_done.sem, 1)
        w(pe, weight_done, 1)
        for tile in range(8):
            b, t0 = tile // 4, tile % 4 * 128
            last = nc.tensor.transpose(ps[0:EXPERTS, 3 + b, t0:t0 + 128], G[6][:, tile, :], C["ident"])
        last.then_inc(wt_done.sem, 1)
        w(pe, wt_copied, 2)
        for n in range(2 * EXPERTS):
            e, b = divmod(n, 2)
            w(pe, wb_copied, n - 1)
            nc.tensor.matmul(ps[:, 5 + n % 2, :], pick[:, e, :], wT[:, b, :], start=True, stop=True).then_inc(wb_done.sem, 1)
        w(pe, wb_copied, 16)

        with pe.Fori(0, TURNS) as turn:
            def down(i):
                e, b = divmod(i, 2)
                pe.wait_ge(*hid_done.at(turn, 4 * i + 4))
                if i >= 2:
                    pe.wait_ge(*wy_done.at(turn, i - 1))
                for j in range(4):
                    last = nc.tensor.matmul(ps[:, 4 + i % 2, :], wd[:, e, j, :], hid[:, 4 * (i % 2) + j, :], start=(j == 0), stop=(j == 3))
                last.then_inc(down_done.sem, 1)

            pe.wait_ge(*wy_done.at(turn, 0))
            for i in range(4):
                e, b = divmod(i, 2)
                if b == 0:
                    pe.wait_ge(*w_in[e].at(turn, 48))
                for j in range(4):
                    n = 4 * i + j
                    bank = 2 * (n % 2)
                    if n >= 2:
                        pe.wait_ge(*hid_done.at(turn, n - 1))
                    nc.tensor.matmul(ps[:, bank, :], wg[:, e, 128 * j:128 * j + 128], hn[:, b, :], start=True, stop=True)
                    nc.tensor.matmul(ps[:, bank + 1, :], wu[:, e, 128 * j:128 * j + 128], hn[:, b, :], start=True, stop=True).then_inc(pair_done.sem, 1)
                    if j == 1 and i >= 1:
                        down(i - 1)
            down(3)
        w(pe, acc_done, 4 * TURNS)
        for b in range(2):
            normalise(nc, "pe_mean", pe, s, b, total[:, b, :], None, (None, None), (ps[:, b, :], ps[:, 2 + b, :]), C, w)
        for b in range(2):
            normalise(nc, "pe_var", pe, s, b, None, None, (hsq, rn), (ps[:, b, :], ps[:, 2 + b, :]), C, w)

    @block.scalar
    def _(ac):
        A = nc.scalar.activation
        nc.scalar.preload_act_table_set("natural_log_exp_and_others")
        for b in range(2):
            A(hsq[:, b, :], h1[:, b, :], ACT.Square).then_inc(hsq_done.sem, 1)
        for b in range(2):
            w(ac, ms_done, b + 1)
            A(rn[:, b, :], ps[:, b, :], ACT.Ln, bias=C["eps"]).then_inc(ln_done.sem, 1)
            w(ac, ln_done, b + 1)
            A(rn[:, b, :], rn[:, b, :], ACT.Exp, scale=-0.5).then_inc(r_done.sem, 1)
        w(ac, gate_step, 2)
        A(G[1][:], G[0][:], ACT.Exp).then_inc(gexp_done.sem, 1)
        w(ac, wt_done, 1)
        for b in range(2):
            A(wT[:, b, :], ps[0:EXPERTS, 3 + b, :], ACT.Copy).then_inc(wt_copied.sem, 1)
        for n in range(2 * EXPERTS):
            e, b = divmod(n, 2)
            w(ac, wb_done, n + 1)
            A(w_all[:, e, b, :], ps[:, 5 + n % 2, :], ACT.Copy).then_inc(wb_copied.sem, 1)
        nc.scalar.preload_act_table_set("silu_and_others")
        with ac.Fori(0, TURNS) as turn:
            for n in range(16):
                ac.wait_ge(*pair_done.at(turn, n + 1))
                if n >= 2:
                    ac.wait_ge(*hid_done.at(turn, n - 1))
                A(sg[:, n % 2, :], ps[:, 2 * (n % 2), :], ACT.Silu).then_inc(silu_done.sem, 1)
        nc.scalar.preload_act_table_set("natural_log_exp_and_others")
        for b in range(2):
            normalise(nc, "act_square", ac, s, b, None, None, (hsq, rn), None, C, w)
        for b in range(2):
            normalise(nc, "act_rstd", ac, s, b, None, None, (hsq, rn), (ps[:, b, :], ps[:, 2 + b, :]), C, w)

    @block.vector
    def _(dv):
        v = nc.vector
        w(dv, loaded, 64)
        for b in range(2):
            w(dv, r_done, b + 1)
            v.scalar_tensor_tensor(hn[:, b, :], h1[:, b, :], rms_w[:, 0:1], rn[:, b, :], ALU.mult, ALU.mult).then_inc(hn_done.sem, 1)
        for b in range(2):
            v.tensor_tensor(total[:, b, :], x[:, b, :], h1[:, b, :], ALU.add).then_inc(start_done.sem, 1)

        at = [0]

        def go(ins):
            ins.then_inc(gate_step.sem, 1)
            at[0] += 1

        def settled():
            w(dv, gate_step, at[0])

        def bc8(n):
            return col[:, :, n:n + 1].to_broadcast([P, 8, EXPERTS])

        def best(score, hot, work, n):
            go(v.tensor_reduce(col[:, :, n], score[:], AX, ALU.max))
            settled()
            go(v.tensor_tensor(hot[:], score[:], bc8(n), ALU.is_equal))
            settled()
            go(v.tensor_tensor(work[:], hot[:], order[:], ALU.mult))
            settled()
            go(v.tensor_reduce(col[:, :, n + 1], work[:], AX, ALU.max))
            settled()
            go(v.tensor_tensor(hot[:], order[:], bc8(n + 1), ALU.is_equal))
            settled()

        w(dv, logit_done, 1)
        go(v.tensor_reduce(col[:, :, 0], ps[:, 2, 0:64].rearrange("p (t e) -> p t e", e=8), AX, ALU.max))
        settled()
        go(v.tensor_tensor(G[0][:], ps[:, 2, 0:64].rearrange("p (t e) -> p t e", e=8), bc8(0), ALU.subtract))
        w(dv, gexp_done, 1)
        go(v.tensor_reduce(col[:, :, 1], G[1][:], AX, ALU.add))
        settled()
        go(v.reciprocal(col[:, :, 0], col[:, :, 1]))
        settled()
        go(v.tensor_tensor(G[2][:], G[1][:], bc8(0), ALU.mult))
        settled()
        best(G[2], G[3], G[5], 2)
        go(v.scalar_tensor_tensor(G[4][:], G[3][:], -2.0, G[2][:], ALU.mult, ALU.add))
        settled()
        best(G[4], G[0], G[5], 4)
        go(v.tensor_tensor(G[5][:], G[0][:], G[3][:], ALU.add))
        settled()
        v.tensor_tensor(G[6][:], G[5][:], G[2][:], ALU.mult).then_inc(weight_done.sem, 1)

        w(dv, wb_copied, 16)
        with dv.Fori(0, TURNS) as turn:
            def weigh(i):
                e, b = divmod(i, 2)
                dv.wait_ge(*down_done.at(turn, i + 1))
                if i >= 2:
                    dv.wait_ge(*acc_done.at(turn, i - 1))
                else:
                    dv.wait_ge(*acc_done.at(turn, 0))
                v.tensor_tensor(wy[:, i % 2, :], ps[:, 4 + i % 2, :], w_all[:, bass.ds(turn * 2 + e, 1), b, :], ALU.mult).then_inc(wy_done.sem, 1)

            dv.wait_ge(*down_done.at(turn, 0))
            for n in range(16):
                i, j = divmod(n, 4)
                dv.wait_ge(*silu_done.at(turn, n + 1))
                if n >= 8 and j == 0:
                    dv.wait_ge(*down_done.at(turn, i - 1))
                v.tensor_tensor(hid[:, n % 8, :], sg[:, n % 2, :], ps[:, 2 * (n % 2) + 1, :], ALU.mult).then_inc(hid_done.sem, 1)
                if j == 3 and i >= 1:
                    weigh(i - 1)
            weigh(3)
        for b in range(2):
            normalise(nc, "dve_centre", dv, s, b, total[:, b, :], None, (hsq, rn), (ps[:, b, :], ps[:, 2 + b, :]), C, w)
        for b in range(2):
            normalise(nc, "dve_scale", dv, s, b, None, x1[:, b, :], (hsq, rn), None, C, w)
        dv.wait_ge(*s["scaled"].at(s["use"], 2))

    @block.gpsimd
    def _(pool):
        w(pool, start_done, 2)
        with pool.Fori(0, TURNS) as turn:
            for i in range(4):
                b = i % 2
                pool.wait_ge(*wy_done.at(turn, i + 1))
                if i >= 2:
                    pool.wait_ge(*acc_done.at(turn, i - 1))
                else:
                    pool.wait_ge(*acc_done.at(turn, 0))
                nc.gpsimd.tensor_tensor(total[:, b, :], total[:, b, :], wy[:, i % 2, :], ALU.add).then_inc(acc_done.sem, 1)


def build_cross(nc, ctx, x1, x2, d, C):
    def sb(name, shape, dt=F32):
        return ctx.enter_context(nc.sbuf_tensor("cr_" + name, shape, dt))

    def flow(name, per=0):
        return Flow(C["sems"].enter_context(nc.semaphore("cr_" + name)), per)

    ps = C["psum"]
    wq = sb("wq", [P, P])
    wk = sb("wk", [P, P])
    wv = sb("wv", [P, P])
    wo = sb("wo", [P, P])
    ctxT = sb("ctxT", [P, 2, 4, KEYS])
    rel = sb("rel", [BUCKETS, HEADS])
    onehot = sb("onehot", [BUCKETS, SPAN])
    head_of = sb("head_of", [P, HEADS])
    quarter = sb("quarter", [P, HEADS])
    line = sb("line", [HEADS, SPAN])
    bias = sb("bias", [P, 4, HEADS, KEYS])
    qT = sb("qT", [P, 2, SEQ])
    kbd = sb("kbd", [P, 2, HEADS, KEYS])
    vbd = sb("vbd", [P, 2, HEADS, 8])
    sc = sb("sc", [P, 2, HEADS, KEYS])
    pr = sb("pr", [P, 2, HEADS, KEYS])
    mx = sb("mx", [P, 2, HEADS])
    sm = sb("sm", [P, 2, HEADS])
    ri = sb("ri", [P, 2, HEADS])
    pT = sb("pT", [P, 2, 4, P])
    oT = sb("oT", [P, 2, SEQ])
    centred = sb("centred", [P, 2, SEQ])
    ln = sb("ln", [P, 2, SEQ])
    total = sb("total", [P, 2, SEQ])

    loaded, loaded2 = flow("loaded"), flow("loaded2")
    line_done, line_copied, line_out, bias_in = (flow(n) for n in ("line_done", "line_copied", "line_out", "bias_in"))
    q_done, q_copied, k_done, kbd_done, v_done, vbd_done = (flow(n) for n in ("q_done", "q_copied", "k_done", "kbd_done", "v_done", "vbd_done"))
    s_done, add_done, mx_done, sub_done, exp_done, sum_done, rec_done, norm_done = (flow(n) for n in (
        "s_done", "add_done", "mx_done", "sub_done", "exp_done", "sum_done", "rec_done", "norm_done"))
    t_done, t_copied, o_done, o_copied, wo_done, res_done = (flow(n) for n in ("t_done", "t_copied", "o_done", "o_copied", "wo_done", "res_done"))
    s = C["norm"](1)

    def w(eng, f, n):
        if n > 0:
            eng.wait_ge(f.sem, n)

    block = ctx.enter_context(nc.Block())

    @block.sync
    def _(sp):
        for dst, src in ((rel, "rel"), (onehot, "onehot")):
            sp.dma_start(dst[:], d[src]).then_inc(loaded.sem, 16)
        for dst, src in ((wq, "xwq"), (wk, "xwk"), (wv, "xwv"), (wo, "xwo"), (ctxT, "ctxT"), (head_of, "head_of"), (quarter, "quarter")):
            sp.dma_start(dst[:], d[src]).then_inc(loaded2.sem, 16)
        w(sp, line_copied, 2)
        sp.dma_start(d["line"], line[:]).then_inc(line_out.sem, 16)
        w(sp, line_out, 16)
        for tile in range(4):
            src = bass.AP(d["line"].tensor, 128 * tile, [[1, P], [SPAN, HEADS], [1, KEYS]])
            sp.dma_start(bias[:, tile], src).then_inc(bias_in.sem, 16)

    @block.tensor
    def _(pe):
        w(pe, loaded, 32)
        nc.tensor.matmul(ps[0:HEADS, 0, :], rel[:], onehot[:, 0:512], start=True, stop=True).then_inc(line_done.sem, 1)
        nc.tensor.matmul(ps[0:HEADS, 1, 0:SPAN - 512], rel[:], onehot[:, 512:SPAN], start=True, stop=True).then_inc(line_done.sem, 1)
        w(pe, loaded2, 112)
        for b in range(2):
            nc.tensor.matmul(ps[:, 2 + b, 0:KEYS], wk[:], ctxT[:, b, 0, :], start=True, stop=True).then_inc(k_done.sem, 1)
            nc.tensor.matmul(ps[:, 4 + b, 0:P], ctxT[:, b].rearrange("p r k -> p (r k)"), wv[:], start=True, stop=True).then_inc(v_done.sem, 1)
        for b in range(2):
            nc.tensor.matmul(ps[:, 6 + b, :], wq[:], x1[:, b, :], start=True, stop=True).then_inc(q_done.sem, 1)

        def scores(u):
            b, t0 = u // 4, u % 4 * 128
            if u == 0:
                w(pe, line_copied, 2)
                w(pe, kbd_done, 2)
            w(pe, q_copied, b + 1)
            w(pe, add_done, u - 1)
            nc.tensor.matmul(ps[:, u % 2, :], qT[:, b, t0:t0 + 128], kbd[:, b].rearrange("p h k -> p (h k)"), start=True, stop=True).then_inc(s_done.sem, 1)

        def turn(u):
            w(pe, norm_done, u + 1)
            w(pe, t_copied, u - 1)
            w(pe, kbd_done, 2)
            for g in range(4):
                last = nc.tensor.transpose(ps[:, 2 + u % 2, 128 * g:128 * g + 128], pr[:, u % 2, 4 * g:4 * g + 4, :].rearrange("p h k -> p (h k)"), C["ident"])
            last.then_inc(t_done.sem, 1)

        def values(u):
            b, t0 = u // 4, u % 4 * 128
            w(pe, vbd_done, 2)
            w(pe, t_copied, u + 1)
            for g in range(4):
                last = nc.tensor.matmul(ps[32 * g:32 * g + 32, 4 + b, t0:t0 + 128], vbd[:, b, 4 * g:4 * g + 4, :].rearrange("p h d -> p (h d)"),
                                        pT[:, u % 2, g, :], start=True, stop=True)
            last.then_inc(o_done.sem, 1)

        scores(0)
        for u in range(8):
            if u < 7:
                scores(u + 1)
            turn(u)
            values(u)
        for b in range(2):
            w(pe, o_copied, b + 1)
            nc.tensor.matmul(ps[:, 6 + b, :], wo[:], oT[:, b, :], start=True, stop=True).then_inc(wo_done.sem, 1)
        w(pe, add_done, 8)
        w(pe, t_copied, 8)
        for b in range(2):
            w(pe, res_done, b + 1)
            normalise(nc, "pe_mean", pe, s, b, total[:, b, :], None, (None, None), (ps[:, b, :], ps[:, 2 + b, :]), C, w)
        for b in range(2):
            normalise(nc, "pe_var", pe, s, b, None, None, (centred, ln), (ps[:, b, :], ps[:, 2 + b, :]), C, w)

    @block.scalar
    def _(ac):
        A = nc.scalar.activation
        nc.scalar.preload_act_table_set("natural_log_exp_and_others")
        w(ac, line_done, 1)
        A(line[:, 0:512], ps[0:HEADS, 0, :], ACT.Copy).then_inc(line_copied.sem, 1)
        w(ac, line_done, 2)
        A(line[:, 512:SPAN], ps[0:HEADS, 1, 0:SPAN - 512], ACT.Copy).then_inc(line_copied.sem, 1)
        for b in range(2):
            w(ac, q_done, b + 1)
            A(qT[:, b, :], ps[:, 6 + b, :], ACT.Copy).then_inc(q_copied.sem, 1)
        for u in range(9):
            if u >= 1:
                w(ac, t_done, u)
                w(ac, o_done, u - 2)
                A(pT[:, (u - 1) % 2].rearrange("p g t -> p (g t)"), ps[:, 2 + (u - 1) % 2, :], ACT.Copy).then_inc(t_copied.sem, 1)
            if u < 8:
                w(ac, sub_done, u + 1)
                A(pr[:, u % 2], pr[:, u % 2], ACT.Exp).then_inc(exp_done.sem, 1)
            if u == 5 or u == 8:
                b = u // 8
                w(ac, o_done, 4 * b + 4)
                A(oT[:, b, :], ps[:, 4 + b, :], ACT.Copy).then_inc(o_copied.sem, 1)
        for b in range(2):
            normalise(nc, "act_square", ac, s, b, None, None, (centred, ln), None, C, w)
        for b in range(2):
            normalise(nc, "act_rstd", ac, s, b, None, None, (centred, ln), (ps[:, b, :], ps[:, 2 + b, :]), C, w)

    @block.vector
    def _(dv):
        v = nc.vector
        w(dv, loaded2, 112)
        for b in range(2):
            w(dv, k_done, b + 1)
            v.tensor_tensor(kbd[:, b], ps[:, 2 + b, 0:KEYS].unsqueeze(1).to_broadcast([P, HEADS, KEYS]),
                            head_of[:].unsqueeze(2).to_broadcast([P, HEADS, KEYS]), ALU.mult).then_inc(kbd_done.sem, 1)
            w(dv, v_done, b + 1)
            v.tensor_tensor(vbd[:, b], ps[:, 4 + b, 0:P].rearrange("p (h d) -> p h d", d=8),
                            quarter[:].unsqueeze(2).to_broadcast([P, HEADS, 8]), ALU.mult).then_inc(vbd_done.sem, 1)
        w(dv, bias_in, 64)
        for u in range(8):
            i = u % 2
            w(dv, s_done, u + 1)
            w(dv, sub_done, u - 1)
            v.tensor_tensor(sc[:, i], ps[:, i, :].rearrange("p (h k) -> p h k", k=KEYS), bias[:, u % 4], ALU.add).then_inc(add_done.sem, 1)
            w(dv, add_done, u + 1)
            w(dv, sub_done, u - 1)
            v.tensor_reduce(mx[:, i, :], sc[:, i], AX, ALU.max).then_inc(mx_done.sem, 1)
            w(dv, mx_done, u + 1)
            w(dv, t_done, u - 1)
            v.tensor_tensor(pr[:, i], sc[:, i], mx[:, i, :].unsqueeze(2).to_broadcast([P, HEADS, KEYS]), ALU.subtract).then_inc(sub_done.sem, 1)
            w(dv, exp_done, u + 1)
            w(dv, rec_done, u - 1)
            v.tensor_reduce(sm[:, i, :], pr[:, i], AX, ALU.add).then_inc(sum_done.sem, 1)
            w(dv, sum_done, u + 1)
            w(dv, norm_done, u - 1)
            v.reciprocal(ri[:, i, :], sm[:, i, :]).then_inc(rec_done.sem, 1)
        for b in range(2):
            w(dv, wo_done, b + 1)
            v.tensor_tensor(total[:, b, :], ps[:, 6 + b, :], x1[:, b, :], ALU.add).then_inc(res_done.sem, 1)
        for b in range(2):
            normalise(nc, "dve_centre", dv, s, b, total[:, b, :], None, (centred, ln), (ps[:, b, :], ps[:, 2 + b, :]), C, w)
        for b in range(2):
            normalise(nc, "dve_scale", dv, s, b, None, x2[:, b, :], (centred, ln), None, C, w)
        dv.wait_ge(*s["scaled"].at(s["use"], 2))

    @block.gpsimd
    def _(pool):
        for u in range(8):
            i = u % 2
            w(pool, rec_done, u + 1)
            nc.gpsimd.tensor_tensor(pr[:, i], pr[:, i], ri[:, i, :].unsqueeze(2).to_broadcast([P, HEADS, KEYS]), ALU.mult).then_inc(norm_done.sem, 1)


def build_stack(nc, ctx, Y, d, C):
    def sb(name, shape, dt=F32):
        return ctx.enter_context(nc.sbuf_tensor(name, shape, dt))

    def flow(name, per):
        return Flow(C["sems"].enter_context(nc.semaphore(name)), per)

    ps = C["psum"]
    gemm_bank = [ps[:, 0, :], ps[:, 1, :]]
    norm_bank = [ps[:, 2, :], ps[:, 3, :]]
    score_bank = [ps[:, 4, :], ps[:, 5, :]]
    turn_bank = [ps[:, 6, :], ps[:, 7, :]]
    out_bank = norm_bank

    wqk = sb("st_wqk", [P, 16, P])
    wv = sb("st_wv", [P, 1024])
    wo = sb("st_wo", [P, 8, P])
    w1 = sb("st_w1", [P, 2 * HID])
    w2 = sb("st_w2", [P, 3, P])
    rope_scale = sb("st_rope_scale", [P, 4])
    ffn_param = sb("st_ffn_param", [P, 9])
    table = sb("st_table", [P, 4, SEQ])
    qT = sb("st_qT", [P, 2, 8, SEQ])
    kT = sb("st_kT", [P, 2, 8, WIN + SEQ])
    vn = sb("st_vn", [P, 2, 4, 1024])
    vs = sb("st_vs", [P, 2, 4, 1024])
    sq = sb("st_sq", [P, 2, SEQ])
    rn = sb("st_rn", [P, 2, SEQ])
    swapped = sb("st_swapped", [P, 2, SEQ])
    cos_part = sb("st_cos_part", [P, 2, SEQ])
    sin_part = sb("st_sin_part", [P, 2, SEQ])
    turned = sb("st_turned", [P, 2, SEQ])
    prob = sb("st_prob", [P, 2, 8, 64])
    pn = sb("st_pn", [P, 2, 9 * 64])
    pT = sb("st_pT", [P, 2, 8, 64])
    mx = sb("st_mx", [P, 2, 8])
    rs = sb("st_rs", [P, 2, 8])
    ri = sb("st_ri", [P, 2, 8])
    dx, dsq, lnv, rstd, xn, gate, act = sq, turned, rn, swapped, cos_part, sin_part, turned

    def act_of(j):
        return act[:, j, :] if j < 2 else prob[:, 0].rearrange("p h k -> p (h k)")

    wqk_in, wv_in, wo_in = flow("wqk_in", 16), flow("wv_in", 16), flow("wo_in", 16)
    w1_in, w2_in = flow("w1_in", 16), flow("w2_in", 48)
    rope_in, ffn_in = flow("rope_in", 32), flow("ffn_in", 16)
    vs_in = [flow(f"vs_in_{b}", 32) for b in range(2)]
    pads_zero = flow("pads_zero", 0)
    tables_ready = flow("tables_ready", 4)
    gemm_done = flow("gemm_done", 48)
    v_copied = flow("v_copied", 16)
    sq_done, norm_done = flow("sq_done", 32), flow("norm_done", 32)
    ln_done, r_done = flow("ln_done", 32), flow("r_done", 32)
    swap_done, cos_done, sin_done = flow("swap_done", 32), flow("cos_done", 32), flow("sin_done", 32)
    add_done, rope_done = flow("add_done", 32), flow("rope_done", 32)
    s_done, mx_done, sub_done = flow("s_done", 16), flow("mx_done", 16), flow("sub_done", 16)
    exp_done, sum_done, rec_done = flow("exp_done", 16), flow("sum_done", 16), flow("rec_done", 16)
    pn_done, t_done = flow("pn_done", 32), flow("t_done", 32)
    low_done, high_done = flow("low_done", 32), flow("high_done", 32)
    pv_done, o_copied = flow("pv_done", 16), flow("o_copied", 16)
    wo_done, res1_done = flow("wo_done", 2), flow("res1_done", 4)
    mean_done, dx_done, dsq_done, var_done = flow("mean_done", 2), flow("dx_done", 2), flow("dsq_done", 2), flow("var_done", 2)
    lnv_done, rstd_done, xh_done, xn_done = flow("lnv_done", 2), flow("rstd_done", 2), flow("xh_done", 2), flow("xn_done", 2)
    w1_done, gate_done, act_done = flow("w1_done", 6), flow("gate_done", 6), flow("act_done", 6)
    w2_step, res2_done = flow("w2_step", 6), flow("res2_done", 4)

    ident, ident16, mask16 = C["ident"], C["ident16"], C["mask16"]
    head_ones, mean_ones = C["head_ones"], C["mean_ones"]

    def gemm_no(b, kind, n):
        return b * 24 + (n if kind == "v" else 8 + n)

    def bank_left(eng, turn, z):
        if z < 2:
            return
        b, n = divmod(z - 2, 24)
        if n < 8:
            eng.wait_ge(*v_copied.at(turn, b * 8 + n + 1))
        else:
            eng.wait_ge(*swap_done.at(turn, b * 16 + n - 8 + 1))

    ROWS = [128, 128, HID - 256]

    block = ctx.enter_context(nc.Block())

    @block.sync
    def _(sp):
        with sp.Fori(0, LAYERS) as turn:
            sp.wait_ge(*gemm_done.at(turn, 0))
            sp.dma_start(wqk[:], at_layer(d["wqk"], turn)).then_inc(wqk_in.sem, 16)
            sp.dma_start(wv[:], at_layer(d["wv"], turn)).then_inc(wv_in.sem, 16)
            sp.wait_ge(*sin_done.at(turn, 0))
            sp.dma_start(table[:], d["rope"]).then_inc(rope_in.sem, 16)
            sp.dma_start(rope_scale[:], at_layer(d["rope_scale"], turn)).then_inc(rope_in.sem, 16)
            sp.wait_ge(*wo_done.at(turn, 0))
            sp.dma_start(wo[:], at_layer(d["wo"], turn)).then_inc(wo_in.sem, 16)
            sp.wait_ge(*w1_done.at(turn, 0))
            sp.dma_start(w1[:], at_layer(d["w1"], turn)).then_inc(w1_in.sem, 16)
            sp.wait_ge(*w2_step.at(turn, 0))
            for j, rows in enumerate(ROWS):
                sp.dma_start(w2[0:rows, j, :], at_layer(d["w2"], turn)[j * 128:j * 128 + rows, :]).then_inc(w2_in.sem, 16)
            sp.wait_ge(*res2_done.at(turn, 0))
            sp.wait_ge(*act_done.at(turn, 0))
            sp.dma_start(ffn_param[:], at_layer(d["ffn_param"], turn)).then_inc(ffn_in.sem, 16)
            for b in range(2):
                sp.wait_ge(*v_copied.at(turn, b * 8 + 8))
                sp.dma_start(vs[32:128, b, :, :], vn[0:96, b, :, :]).then_inc(vs_in[b].sem, 16)
                sp.dma_start(vs[0:32, b, 1:4, :], vn[96:128, b, 0:3, :]).then_inc(vs_in[b].sem, 16)
        for f in (wqk_in, wv_in, wo_in, w1_in, w2_in, rope_in, ffn_in, *vs_in):
            sp.wait_ge(f.sem, LAYERS * f.per)

    @block.tensor
    def _(pe):
        def v_gemm(turn, b, n):
            tile, half = divmod(n, 2)
            z = gemm_no(b, "v", n)
            bank_left(pe, turn, z)
            nc.tensor.matmul(gemm_bank[z % 2], Y[:, b, tile * 128:tile * 128 + 128], wv[:, half * 512:half * 512 + 512],
                             start=True, stop=True).then_inc(gemm_done.sem, 1)

        def qk_gemm(turn, b, m):
            z = gemm_no(b, "qk", m)
            bank_left(pe, turn, z)
            nc.tensor.matmul(gemm_bank[z % 2], wqk[:, m, :], Y[:, b, 0:SEQ], start=True, stop=True).then_inc(gemm_done.sem, 1)

        def head_norm(turn, g):
            pe.wait_ge(*sq_done.at(turn, g + 1))
            if g >= 2:
                pe.wait_ge(*ln_done.at(turn, g - 1))
            nc.tensor.matmul(norm_bank[g % 2], head_ones, sq[:, g % 2, :], start=True, stop=True).then_inc(norm_done.sem, 1)

        def scores(turn, u):
            b, tile, odd = u // 8, u // 2 % 4, u % 2
            pe.wait_ge(*rope_done.at(turn, b * 16 + 16))
            if u >= 2:
                pe.wait_ge(*sub_done.at(turn, u - 1))
            bank = score_bank[u % 2]
            nc.tensor.matmul(bank, ident16, mask16[:, min(tile, 1), :].unsqueeze(1).to_broadcast([P, 8, 64]),
                             start=True, stop=False, skip_group_check=True)
            for h in range(8):
                lo = 64 * odd
                for c in range(4):
                    t0 = tile * 128 + 32 * c
                    last = nc.tensor.matmul(bank[32 * c:32 * c + 32, 64 * h:64 * h + 64],
                                            qT[lo:lo + 64, b, h, t0:t0 + 32], kT[lo:lo + 64, b, h, t0:t0 + 64],
                                            start=False, stop=(h == 7), skip_group_check=True)
            last.then_inc(s_done.sem, 1)

        def turn_probs(turn, u):
            pe.wait_ge(*pn_done.at(turn, 2 * u + 2))
            for s in range(2):
                n = 2 * u + s
                if n >= 2:
                    pe.wait_ge(*low_done.at(turn, n - 1))
                    pe.wait_ge(*high_done.at(turn, n - 1))
                for h in range(4 * s, 4 * s + 4):
                    last = nc.tensor.transpose(turn_bank[s][:, (h % 4) * 128:(h % 4) * 128 + 128],
                                               pn[:, u % 2, 64 * h:64 * h + 128], ident)
                last.then_inc(t_done.sem, 1)

        def values(turn, u):
            b, tile, odd = u // 8, u // 2 % 4, u % 2
            pe.wait_ge(pads_zero.sem, 2)
            pe.wait_ge(*vs_in[b].at(turn, 32))
            pe.wait_ge(*low_done.at(turn, 2 * u + 2))
            pe.wait_ge(*high_done.at(turn, 2 * u + 2))
            if u >= 2:
                pe.wait_ge(*o_copied.at(turn, u // 2 * 2))
            for h in range(8):
                head = 2 * h + odd
                for c in range(4):
                    lo = 64 * (c // 2)
                    keys = vn if c % 2 else vs
                    slot = h if c < 2 else (h + 7) % 8
                    last = nc.tensor.matmul(
                        out_bank[c // 2][64 * odd:64 * odd + 64, 64 * h + 32 * (c % 2):64 * h + 32 * (c % 2) + 32],
                        keys[lo:lo + 64, b, tile, 64 * head:64 * head + 64],
                        pT[lo:lo + 64, u % 2, slot, 32 * (c % 2):32 * (c % 2) + 32], start=True, stop=True)
            last.then_inc(pv_done.sem, 1)

        pe.wait_ge(pads_zero.sem, 2)
        with pe.Fori(0, LAYERS) as turn:
            pe.wait_ge(*res2_done.at(turn, 0))
            pe.wait_ge(*wv_in.at(turn, 16))
            for b in range(2):
                for n in range(8):
                    v_gemm(turn, b, n)
                if b == 0:
                    pe.wait_ge(*wqk_in.at(turn, 16))
                for m in range(16):
                    qk_gemm(turn, b, m)
                    if m >= 1:
                        head_norm(turn, b * 16 + m - 1)
                head_norm(turn, b * 16 + 15)
            pe.wait_ge(*ln_done.at(turn, 32))
            scores(turn, 0)
            for u in range(16):
                if u < 15:
                    scores(turn, u + 1)
                turn_probs(turn, u)
                values(turn, u)
            pe.wait_ge(*wo_in.at(turn, 16))
            pe.wait_ge(*swap_done.at(turn, 32))
            for b in range(2):
                pe.wait_ge(*o_copied.at(turn, 8 * b + 8))
                for blk in range(8):
                    last = nc.tensor.matmul(gemm_bank[b], wo[:, blk, :], qT[:, b, blk, :], start=(blk == 0), stop=(blk == 7))
                last.then_inc(wo_done.sem, 1)
            for b in range(2):
                pe.wait_ge(*res1_done.at(turn, 2 * b + 2))
                nc.tensor.matmul(norm_bank[b], mean_ones, Y[:, b, 0:SEQ], start=True, stop=True).then_inc(mean_done.sem, 1)
            for b in range(2):
                pe.wait_ge(*dsq_done.at(turn, b + 1))
                nc.tensor.matmul(score_bank[b], mean_ones, dsq[:, b, :], start=True, stop=True).then_inc(var_done.sem, 1)
            pe.wait_ge(*w1_in.at(turn, 16))
            pe.wait_ge(*w2_in.at(turn, 48))
            pe.wait_ge(*ffn_in.at(turn, 16))

            def down(b, j):
                pe.wait_ge(*act_done.at(turn, 3 * b + j + 1))
                nc.tensor.matmul(norm_bank[b], w2[0:ROWS[j], j, :], act_of(j)[0:ROWS[j]],
                                 start=(j == 0), stop=(j == 2)).then_inc(w2_step.sem, 1)

            for b in range(2):
                pe.wait_ge(*xn_done.at(turn, b + 1))
                for j in range(3):
                    n = 3 * b + j
                    pair = [gemm_bank, turn_bank][n % 2]
                    if n >= 2:
                        pe.wait_ge(*act_done.at(turn, n - 1))
                    nc.tensor.matmul(pair[1][0:ROWS[j], :], w1[:, HID + 128 * j:HID + 128 * j + ROWS[j]], xn[:, b, :],
                                     start=True, stop=True)
                    nc.tensor.matmul(pair[0][0:ROWS[j], :], w1[:, 128 * j:128 * j + ROWS[j]], xn[:, b, :],
                                     start=True, stop=True).then_inc(w1_done.sem, 1)
                    if n >= 1:
                        down((n - 1) // 3, (n - 1) % 3)
            down(1, 2)

    @block.scalar
    def _(act_e):
        def ln_r(turn, g):
            act_e.wait_ge(*norm_done.at(turn, g + 1))
            if g >= 2:
                act_e.wait_ge(*rope_done.at(turn, g - 1))
            nc.scalar.activation(rn[:, g % 2, :], norm_bank[g % 2], ACT.Ln, bias=C["tiny"], scale=SS_SCALE).then_inc(ln_done.sem, 1)
            act_e.wait_ge(*ln_done.at(turn, g + 1))
            nc.scalar.activation(rn[:, g % 2, :], rn[:, g % 2, :], ACT.Exp, bias=C["ln_scale"], scale=-0.5).then_inc(r_done.sem, 1)

        def low(turn, u, s):
            n = 2 * u + s
            act_e.wait_ge(*t_done.at(turn, n + 1))
            if u >= 2:
                act_e.wait_ge(*pv_done.at(turn, u - 1))
            nc.scalar.activation(pT[0:64, u % 2, 4 * s:4 * s + 4, :],
                                 turn_bank[s][0:64, :].rearrange("p (h q) -> p h q", q=128)[:, :, 0:64], ACT.Copy).then_inc(low_done.sem, 1)

        def out_copy(turn, u):
            b, tile = u // 8, u // 2 % 4
            act_e.wait_ge(*pv_done.at(turn, u + 1))
            for half in range(2):
                t0 = tile * 128 + 64 * half
                nc.scalar.activation(qT[:, b, :, t0:t0 + 64], out_bank[half].rearrange("p (k q) -> p k q", q=64),
                                     ACT.Copy).then_inc(o_copied.sem, 1)

        with act_e.Fori(0, LAYERS) as turn:
            nc.scalar.preload_act_table_set("natural_log_exp_and_others")
            act_e.wait_ge(*w2_step.at(turn, 0))
            act_e.wait_ge(*act_done.at(turn, 0))
            act_e.wait_ge(*xn_done.at(turn, 0))
            for b in range(2):
                for n in range(8):
                    z = gemm_no(b, "v", n)
                    act_e.wait_ge(*gemm_done.at(turn, z + 1))
                    nc.scalar.activation(vn[:, b, n // 2, (n % 2) * 512:(n % 2) * 512 + 512], gemm_bank[z % 2], ACT.Copy).then_inc(v_copied.sem, 1)
                    if b == 1 and n == 0:
                        ln_r(turn, 15)
                for m in range(16):
                    g, z = b * 16 + m, gemm_no(b, "qk", m)
                    act_e.wait_ge(*gemm_done.at(turn, z + 1))
                    if g >= 2:
                        act_e.wait_ge(*norm_done.at(turn, g - 1))
                    nc.scalar.activation(sq[:, g % 2, :], gemm_bank[z % 2], ACT.Square).then_inc(sq_done.sem, 1)
                    if m >= 1:
                        ln_r(turn, g - 1)
            ln_r(turn, 31)
            for u in range(17):
                if u >= 1:
                    low(turn, u - 1, 0)
                if u < 16:
                    act_e.wait_ge(*sub_done.at(turn, u + 1))
                    nc.scalar.activation(prob[:, u % 2], prob[:, u % 2], ACT.Exp, scale=QK_SCALE).then_inc(exp_done.sem, 1)
                if u >= 1:
                    low(turn, u - 1, 1)
                    if u % 2 == 0:
                        out_copy(turn, u - 1)
            act_e.wait_ge(*r_done.at(turn, 32))
            for b in range(2):
                act_e.wait_ge(*dx_done.at(turn, b + 1))
                nc.scalar.activation(dsq[:, b, :], dx[:, b, :], ACT.Square).then_inc(dsq_done.sem, 1)
            for b in range(2):
                act_e.wait_ge(*var_done.at(turn, b + 1))
                nc.scalar.activation(lnv[:, b, :], score_bank[b], ACT.Ln, bias=C["eps"]).then_inc(lnv_done.sem, 1)
                act_e.wait_ge(*lnv_done.at(turn, b + 1))
                nc.scalar.activation(rstd[:, b, :], lnv[:, b, :], ACT.Exp, scale=-0.5).then_inc(rstd_done.sem, 1)
            act_e.wait_ge(*ffn_in.at(turn, 16))
            for n in range(6):
                b, j = divmod(n, 3)
                pair = [gemm_bank, turn_bank][n % 2]
                act_e.wait_ge(*w1_done.at(turn, n + 1))
                if n >= 2:
                    act_e.wait_ge(*act_done.at(turn, n - 1))
                r = ROWS[j]
                nc.scalar.activation(gate[0:r, n % 2, :], pair[1][0:r, :], ACT.Gelu, bias=ffn_param[0:r, 5 + j:6 + j]).then_inc(gate_done.sem, 1)

    @block.vector
    def _(dve):
        def rope_last(turn, g):
            b, m = divmod(g, 16)
            dve.wait_ge(*add_done.at(turn, g + 1))
            dve.wait_ge(*r_done.at(turn, g + 1))
            dst = qT[:, b, m, :] if m < 8 else kT[:, b, m - 8, WIN:]
            nc.vector.scalar_tensor_tensor(dst, rn[:, g % 2, :], 1e12, turned[:, g % 2, :], ALU.min, ALU.mult).then_inc(rope_done.sem, 1)

        def high(turn, u, s):
            n = 2 * u + s
            dve.wait_ge(*t_done.at(turn, n + 1))
            if u >= 2:
                dve.wait_ge(*pv_done.at(turn, u - 1))
            nc.vector.tensor_copy(pT[64:128, u % 2, 4 * s:4 * s + 4, :],
                                  turn_bank[s][64:128, :].rearrange("p (h q) -> p h q", q=128)[:, :, 64:128]).then_inc(high_done.sem, 1)

        nc.vector.memset(kT[:, :, :, 0:WIN], 0.0).then_inc(pads_zero.sem, 1)
        nc.vector.memset(vs[0:32, :, 0, :], 0.0).then_inc(pads_zero.sem, 1)
        with dve.Fori(0, LAYERS) as turn:
            dve.wait_ge(*rope_in.at(turn, 32))
            for n in range(4):
                nc.vector.tensor_scalar(table[:, n, :], table[:, n, :], rope_scale[:, n:n + 1], None, ALU.mult).then_inc(tables_ready.sem, 1)
            dve.wait_ge(*tables_ready.at(turn, 4))
            dve.wait_ge(*w2_step.at(turn, 0))
            dve.wait_ge(*xh_done.at(turn, 0))
            dve.wait_ge(*act_done.at(turn, 0))
            for g in range(32):
                b, m = divmod(g, 16)
                z = gemm_no(b, "qk", m)
                src = gemm_bank[z % 2]
                tab = 0 if m < 8 else 2
                dve.wait_ge(*sq_done.at(turn, g + 1))
                if g >= 2:
                    dve.wait_ge(*sin_done.at(turn, g - 1))
                    dve.wait_ge(*add_done.at(turn, g - 1))
                nc.vector.tensor_tensor(cos_part[:, g % 2, :], src, table[:, tab, :], ALU.mult).then_inc(cos_done.sem, 1)
                nc.vector.stream_shuffle(swapped[:, g % 2, :], src, HALF_SWAP).then_inc(swap_done.sem, 1)
                dve.wait_ge(*swap_done.at(turn, g + 1))
                nc.vector.tensor_tensor(sin_part[:, g % 2, :], swapped[:, g % 2, :], table[:, tab + 1, :], ALU.mult).then_inc(sin_done.sem, 1)
                if g >= 1:
                    rope_last(turn, g - 1)
            rope_last(turn, 31)
            for u in range(17):
                i = u % 2
                if u < 16:
                    bank = score_bank[i].rearrange("p (h k) -> p h k", k=64)
                    dve.wait_ge(*s_done.at(turn, u + 1))
                    if u >= 2:
                        dve.wait_ge(*sub_done.at(turn, u - 1))
                    nc.vector.tensor_reduce(mx[:, i, :], bank, AX, ALU.max).then_inc(mx_done.sem, 1)
                    dve.wait_ge(*mx_done.at(turn, u + 1))
                    if u >= 2:
                        dve.wait_ge(*pn_done.at(turn, 2 * u - 2))
                        dve.wait_ge(*sum_done.at(turn, u - 1))
                    nc.vector.tensor_tensor(prob[:, i], bank, mx[:, i, :].unsqueeze(2).to_broadcast([P, 8, 64]), ALU.subtract).then_inc(sub_done.sem, 1)
                if u >= 1:
                    high(turn, u - 1, 0)
                    high(turn, u - 1, 1)
                if u < 16:
                    dve.wait_ge(*exp_done.at(turn, u + 1))
                    if u >= 2:
                        dve.wait_ge(*rec_done.at(turn, u - 1))
                    nc.vector.tensor_reduce(rs[:, i, :], prob[:, i], AX, ALU.add).then_inc(sum_done.sem, 1)
                    dve.wait_ge(*sum_done.at(turn, u + 1))
                    nc.vector.reciprocal(ri[:, i, :], rs[:, i, :]).then_inc(rec_done.sem, 1)
            for b in range(2):
                dve.wait_ge(*wo_done.at(turn, b + 1))
                for f in range(2):
                    dst = Y[64 * f:64 * f + 64, b, f:f + SEQ]
                    nc.vector.tensor_tensor(dst, gemm_bank[b][64 * f:64 * f + 64, :], dst, ALU.add).then_inc(res1_done.sem, 1)
            for b in range(2):
                dve.wait_ge(*mean_done.at(turn, b + 1))
                nc.vector.tensor_tensor(dx[:, b, :], Y[:, b, 0:SEQ], norm_bank[b], ALU.subtract).then_inc(dx_done.sem, 1)
            dve.wait_ge(*ffn_in.at(turn, 16))
            for b in range(2):
                dve.wait_ge(*rstd_done.at(turn, b + 1))
                nc.vector.tensor_tensor(xn[:, b, :], dx[:, b, :], rstd[:, b, :], ALU.mult).then_inc(xh_done.sem, 1)
                dve.wait_ge(*xh_done.at(turn, b + 1))
                nc.vector.tensor_scalar(xn[:, b, :], xn[:, b, :], ffn_param[:, 0:1], ffn_param[:, 1:2], ALU.mult, ALU.add).then_inc(xn_done.sem, 1)

            def residual(b):
                dve.wait_ge(*w2_step.at(turn, 3 * b + 3))
                for f in range(2):
                    dst = Y[64 * f:64 * f + 64, b, f:f + SEQ]
                    nc.vector.scalar_tensor_tensor(dst, norm_bank[b][64 * f:64 * f + 64, :], ffn_param[64 * f:64 * f + 64, 8:9], dst,
                                                   ALU.add, ALU.add).then_inc(res2_done.sem, 1)

            for n in range(6):
                b, j = divmod(n, 3)
                r = ROWS[j]
                pair = [gemm_bank, turn_bank][n % 2]
                dve.wait_ge(*gate_done.at(turn, n + 1))
                dst = act_of(j)[0:r]
                if n == 2:
                    dve.wait_ge(*pn_done.at(turn, 32))
                if n >= 3:
                    dve.wait_ge(*w2_step.at(turn, n - 2))
                nc.vector.scalar_tensor_tensor(dst, pair[0][0:r, :], ffn_param[0:r, 2 + j:3 + j], gate[0:r, n % 2, :],
                                               ALU.add, ALU.mult).then_inc(act_done.sem, 1)
                if n == 4:
                    residual(0)
            residual(1)

    @block.gpsimd
    def _(pool):
        with pool.Fori(0, LAYERS) as turn:
            pool.wait_ge(*w2_step.at(turn, 0))
            for g in range(32):
                pool.wait_ge(*sin_done.at(turn, g + 1))
                if g >= 2:
                    pool.wait_ge(*rope_done.at(turn, g - 1))
                nc.gpsimd.tensor_tensor(turned[:, g % 2, :], cos_part[:, g % 2, :], sin_part[:, g % 2, :], ALU.add).then_inc(add_done.sem, 1)
            for u in range(16):
                i = u % 2
                pool.wait_ge(*rec_done.at(turn, u + 1))
                if u >= 2:
                    pool.wait_ge(*t_done.at(turn, 2 * u - 2))
                nc.gpsimd.tensor_tensor(pn[:, i, 0:512].rearrange("p (h k) -> p h k", k=64), prob[:, i],
                                        ri[:, i, :].unsqueeze(2).to_broadcast([P, 8, 64]), ALU.mult).then_inc(pn_done.sem, 1)
                nc.gpsimd.tensor_tensor(pn[:, i, 512:576], prob[:, i, 0, :], ri[:, i, 0:1].to_broadcast([P, 64]), ALU.mult).then_inc(pn_done.sem, 1)


def build_last_norm(nc, ctx, x2, Y, out, C):
    def sb(name, shape, dt=F32):
        return ctx.enter_context(nc.sbuf_tensor("la_" + name, shape, dt))

    ps = C["psum"]
    total = sb("total", [P, 2, SEQ])
    centred = sb("centred", [P, 2, SEQ])
    ln = sb("ln", [P, 2, SEQ])
    res = sb("res", [P, 2, SEQ])
    sum_done = Flow(C["sems"].enter_context(nc.semaphore("la_sum_done")), 4)
    stored = Flow(C["sems"].enter_context(nc.semaphore("la_stored")), 32)
    s = C["norm"](2)

    def w(eng, f, n):
        eng.wait_ge(f.sem, n)

    def rows(b):
        return ps[:, b, :], ps[:, 2 + b, :]

    block = ctx.enter_context(nc.Block())

    @block.sync
    def _(sp):
        for b in range(2):
            sp.wait_ge(*s["scaled"].at(s["use"], b + 1))
            sp.dma_start(out[:, b, :], res[:, b, :]).then_inc(stored.sem, 16)
        w(sp, stored, 32)

    @block.tensor
    def _(pe):
        for b in range(2):
            w(pe, sum_done, 2 * b + 2)
            normalise(nc, "pe_mean", pe, s, b, total[:, b, :], None, (None, None), rows(b), C, w)
        for b in range(2):
            normalise(nc, "pe_var", pe, s, b, None, None, (centred, ln), rows(b), C, w)

    @block.scalar
    def _(ac):
        nc.scalar.preload_act_table_set("natural_log_exp_and_others")
        for b in range(2):
            normalise(nc, "act_square", ac, s, b, None, None, (centred, ln), None, C, w)
        for b in range(2):
            normalise(nc, "act_rstd", ac, s, b, None, None, (centred, ln), rows(b), C, w)

    @block.vector
    def _(dv):
        for b in range(2):
            for f in range(2):
                half = slice(64 * f, 64 * f + 64)
                nc.vector.tensor_tensor(total[half, b, :], Y[half, b, f:f + SEQ], x2[half, b, :], ALU.add).then_inc(sum_done.sem, 1)
        w(dv, sum_done, 4)
        for b in range(2):
            normalise(nc, "dve_centre", dv, s, b, total[:, b, :], None, (centred, ln), rows(b), C, w)
        for b in range(2):
            normalise(nc, "dve_scale", dv, s, b, None, res[:, b, :], (centred, ln), None, C, w)


def program(nc, d, out, probes=None):
    d = {**d, "line": nc.dram_tensor("bias_line", (HEADS, SPAN), F32).ap()}
    with ExitStack() as ctx:
        def sb(name, shape, dt=F32):
            return ctx.enter_context(nc.sbuf_tensor(name, shape, dt))

        C = {"sems": ctx, "psum": ctx.enter_context(nc.psum_tensor("banks", [P, 8, 512], F32))}
        Y = sb("stream", [P, 2, SEQ + 1])
        x2 = sb("x2", [P, 2, SEQ])
        steps = norm_steps(nc, ctx)
        C["norm"] = lambda use: {**steps, "use": use}
        consts = dict(ident=sb("ident", [P, P]), ident16=sb("ident16", [P, P], BF16), mask16=sb("mask16", [P, 2, 64], BF16),
                      head_ones=sb("head_ones", [P, P]), mean_ones=sb("mean_ones", [P, P]))
        for name, t in consts.items():
            C[name] = t[:]
        fill = sb("fill", [P, 4])
        FILL = (("tiny", 2.0 ** -64), ("eps", 1e-5), ("ln_scale", float(0.5 * np.log(SS_SCALE))), ("one", 1.0))
        for i, (name, _) in enumerate(FILL):
            C[name] = fill[:, i:i + 1]
        C["const_in"] = Flow(C["sems"].enter_context(nc.semaphore("const_in")), 0)
        C["fill"] = Flow(C["sems"].enter_context(nc.semaphore("fill_done")), 0)
        C["const_n"], C["fill_n"] = 16 * (len(consts) + 1), len(FILL)
        probed = ctx.enter_context(nc.semaphore("probed"))

        def probe(name, t, n):
            if probes:
                with nc.Block() as block:
                    @block.sync
                    def _(sp):
                        sp.dma_start(probes[name], t[:]).then_inc(probed, 16)
                        sp.wait_ge(probed, 16 * n)

        with ExitStack() as front:
            x = front.enter_context(nc.sbuf_tensor("x", [P, 2, SEQ], F32))
            h1 = front.enter_context(nc.sbuf_tensor("h1", [P, 2, SEQ], F32))
            x1 = front.enter_context(nc.sbuf_tensor("x1", [P, 2, SEQ], F32))
            with nc.Block() as block:
                @block.sync
                def _(sp):
                    sp.dma_start(x[:], d["x"]).then_inc(C["const_in"].sem, 16)
                    for name in consts:
                        sp.dma_start(C[name], d["c_" + name]).then_inc(C["const_in"].sem, 16)

                @block.scalar
                def _(ac):
                    ac.wait_ge(C["const_in"].sem, C["const_n"])

                @block.vector
                def _(dv):
                    for i, (_, value) in enumerate(FILL):
                        nc.vector.memset(fill[:, i:i + 1], value).then_inc(C["fill"].sem, 1)
            with ExitStack() as part:
                build_mamba(nc, part, x, h1, d, C)
            probe("h1", h1, 1)
            with ExitStack() as part:
                build_moe(nc, part, x, h1, x1, d, C)
            probe("x1", x1, 2)
            with ExitStack() as part:
                build_cross(nc, part, x1, x2, d, C)
            probe("x2", x2, 3)
        placed = ctx.enter_context(nc.semaphore("placed"))
        with nc.Block() as block:
            @block.vector
            def _(dv):
                nc.vector.memset(Y[64:128, :, 0:1], 0.0).then_inc(placed, 1)
                nc.vector.tensor_copy(Y[0:64, :, 0:SEQ], x2[0:64]).then_inc(placed, 1)
                nc.vector.tensor_copy(Y[64:128, :, 1:], x2[64:128]).then_inc(placed, 1)
        with ExitStack() as part:
            build_stack(nc, part, Y, d, C)
        with ExitStack() as part:
            build_last_norm(nc, part, x2, Y, out, C)


def head_rows():
    return [*range(0, 16), *range(32, 48), *range(16, 32), *range(48, 64)]

def stack_constants():
    half = np.arange(0, DH, 2, dtype=np.float32)
    inv_freq = (1.0 / np.float32(10000.0) ** (half / np.float32(DH))).astype(np.float32)
    t = np.arange(SEQ, dtype=np.float32)
    fr = t[:, None] * inv_freq[None, :]
    fr = np.concatenate([fr, fr], -1)
    bs = (half + np.float32(0.4 * DH)) / np.float32(1.4 * DH)
    power = (t - SEQ // 2) / np.float32(WIN // 2)
    sc = (bs[None, :] ** power[:, None]).astype(np.float32)
    sc = np.concatenate([sc, sc], -1)
    sign = np.where(np.arange(DH) < DH // 2, -1.0, 1.0).astype(np.float32)
    cos, sin = np.cos(fr), np.sin(fr) * sign
    rows = head_rows() * 1
    tabs = [cos * sc, sin * sc, cos / sc, sin / sc]
    rope = np.stack([np.tile(x[:, rows].T, (2, 1)) for x in tabs], 1).astype(np.float32)
    i = np.arange(32)[:, None]; j = np.arange(64)[None, :]
    ok = (j >= i) & (j <= i + 32)
    m = np.where(ok, 0.0, -1e30)
    later = np.tile(m, (4, 1))
    first = later.copy(); first[0:32] = np.where(ok & (j >= 32), 0.0, -1e30)
    mask = np.stack([first, later], 1).astype(np.dtype("bfloat16"))
    ho = np.kron(np.eye(2), np.ones((64, 64))).astype(np.float32)
    return dict(rope=rope, c_mask16=mask, c_ident=np.eye(128, dtype=np.float32), c_ident16=np.eye(128).astype(np.dtype("bfloat16")),
                c_head_ones=ho, c_mean_ones=np.full((128, 128), 1 / 128, np.float32))

def stack_inputs(Wqkv, q_scale, k_scale, Wo, ln_g, ln_b, W1, b1, W2, b2):
    rows = np.array(head_rows())
    partner = (rows + 32) % 64
    L = Wqkv.shape[0]
    w = Wqkv.reshape(L, 128, 3, 16, 64)
    wqk = w[:, :, 0:2][..., rows].reshape(L, 128, 2 * 8, 128)
    wv = np.ascontiguousarray(w[:, :, 2].reshape(L, 128, 1024))
    rs = np.stack([np.tile(x, (1, 2)) for x in (q_scale[:, rows], q_scale[:, partner], k_scale[:, rows], k_scale[:, partner])], -1)
    wo = np.ascontiguousarray(Wo.reshape(L, 8, 128, 128).transpose(0, 2, 1, 3))
    def cols(v):
        o = np.zeros((L, 384), v.dtype); o[:, :HID] = v
        return list(o.reshape(L, 3, 128).transpose(1, 0, 2))
    prm = np.stack([ln_g, ln_b, *cols(b1[:, :HID]), *cols(b1[:, HID:]), b2], -1)
    return dict(wqk=np.ascontiguousarray(wqk), wv=wv, rope_scale=np.ascontiguousarray(rs), wo=wo, w1=W1, w2=W2, ffn_param=np.ascontiguousarray(prm))

def front_inputs(i):
    A = lambda n: i['L0_attn_' + n]
    blocks = lambda v: np.stack([v[0:128], v[128:256]], 1)
    xproj = A('x_proj_w')
    o = {}
    o['x'] = np.ascontiguousarray(i['x'].transpose(2, 0, 1))
    o['rms1'] = A('rms1_w')[:, None]; o['rms2'] = A('rms2_w')[:, None]
    o['in_w'] = A('in_proj_w').reshape(128, 4, 128)
    o['xdt_w'] = blocks(xproj[:, 0:64])
    o['xbc_w'] = np.tile(blocks(xproj[:, 64:96]), (1, 1, 3))
    o['dt_w'] = A('dt_proj_w').reshape(64, 2, 128)
    o['out_w'] = blocks(A('out_proj_w'))
    chan = np.concatenate([A('conv_w')[:, 0, :], A('conv_b')[:, None], A('dt_proj_b')[:, None], A('D_skip')[:, None]], 1)
    o['chan'] = blocks(chan)
    o['a_log'] = blocks(A('A_log'))
    o['router'] = A('router_w')
    o['wg'] = A('Wg'); o['wu'] = A('Wu')
    o['wd'] = A('Wd').reshape(8, 4, 128, 128).transpose(0, 2, 1, 3)
    o['xwq'] = i['L0_xattn_Wq']; o['xwk'] = i['L0_xattn_Wkv'][:, :128]; o['xwv'] = i['L0_xattn_Wkv'][:, 128:]
    o['xwo'] = i['L0_xattn_Wo']; o['rel'] = i['L0_xattn_rel_bias']
    o['ctxT'] = np.tile(i['ctx_1024'][:, ::-1].transpose(2, 0, 1)[:, :, None, :], (1, 1, 4, 1))
    return {k: np.ascontiguousarray(v) for k, v in o.items()}

def buckets(rel):
    nb = 16
    out = (rel > 0).astype(np.int32) * nb
    rel = np.abs(rel)
    me = nb // 2
    rf = np.maximum(rel, 1).astype(np.float32)
    large = me + (np.log(rf / np.float32(me)) / np.float32(np.log(128 / me)) * np.float32(nb - me)).astype(np.int32)
    large = np.minimum(large, nb - 1)
    return out + np.where(rel < me, rel, large)

def front_constants():
    sel = np.zeros((96, 32, 128), np.float32)
    for p in range(96): sel[p, p % 32] = 1
    pick = np.zeros((8, 8, 128), np.float32)
    for p in range(8): pick[p, p] = 1
    order = np.broadcast_to(np.arange(8, 0, -1, dtype=np.float32), (128, 8, 8))
    b = buckets(31 - np.arange(544))
    oh = (np.arange(32)[:, None] == b[None]).astype(np.float32)
    ho = np.kron(np.eye(16), np.ones((8, 1))).astype(np.float32)
    qu = np.zeros((128, 16), np.float32)
    for p in range(128):
        qu[p, [h for h in range(16) if h % 4 == p // 32]] = 1
    return dict(select=sel.astype(np.dtype("bfloat16")), pick=pick, order=np.ascontiguousarray(order), onehot=oh, head_of=ho, quarter=qu)


def laid_out(inputs):
    stack = {name[len("L0_ffn_"):]: a for name, a in inputs.items() if name.startswith("L0_ffn_")}
    return {**stack_inputs(**stack), **front_inputs(inputs)}


def shape_constants():
    return {**stack_constants(), **front_constants()}


def kernel(**inputs):
    import concourse.bacc as _bacc
    from concourse.bass_utils import run_bass_kernel_spmd as _run

    inputs = {name: np.asarray(a) for name, a in inputs.items()}
    arrays = {"in_" + name: np.ascontiguousarray(a) for name, a in {**laid_out(inputs), **shape_constants()}.items()}
    nc = _bacc.Bacc("TRN2", target_bir_lowering=False, num_devices=1)
    d = {name[3:]: nc.dram_tensor(name, a.shape, mybir.dt.from_np(a.dtype), kind="ExternalInput").ap() for name, a in arrays.items()}
    out = nc.dram_tensor("out", (P, BATCH, SEQ), F32, kind="ExternalOutput").ap()
    program(nc, d, out)
    got = _run(nc, [arrays], core_ids=[0]).results[0]["out"]
    return np.ascontiguousarray(got.transpose(1, 2, 0))
```

```python
import numpy as np
import concourse.bass as bass
from concourse import mybir
from contextlib import ExitStack

F32 = mybir.dt.float32
BF16 = mybir.dt.bfloat16
ACT = mybir.ActivationFunctionType
ALU = mybir.AluOpType
AX = mybir.AxisListType.X

P = 128
BATCH = 2
SEQ = 512
DIM = 128
LAYERS = 6
HEADS = 16
DH = 64
WIN = 32
DT_RANK = 64
STATES = 16
EXPERTS = 8
KEYS = 32
BUCKETS = 32
SPAN = SEQ + KEYS
HID = int(DIM * 4 * 2 / 3)
QK_SCALE = 8.0
SS_SCALE = 65536.0
HALF_SWAP = [(i + 16) % 32 for i in range(32)]


class Flow:

    def __init__(self, sem, per):
        self.sem = sem
        self.per = per

    def at(self, turn, n):
        return self.sem, turn * self.per + n

    def any(self, turn, n):
        return not isinstance(turn, int) or turn * self.per + n > 0


def at_layer(ap, turn):
    one = ap[bass.ds(turn, 1)]
    return one.rearrange("o p n -> (o p) n" if len(ap.shape) == 3 else "o p m n -> (o p) m n")


def expert(ap, turn, e):
    one = ap[bass.ds(turn * 2 + e, 1)]
    return one.rearrange("o p n -> (o p) n" if len(ap.shape) == 3 else "o p m n -> (o p) m n")


def norm_steps(nc, ctx):
    return {what: Flow(ctx.enter_context(nc.semaphore(f"norm_{what}")), 2)
            for what in ("mean", "centred", "square", "var", "ln", "rstd", "scaled")}


def build_mamba(nc, ctx, x, h1, weights, d, C):
    def sb(name, shape, dt=F32):
        return ctx.enter_context(nc.sbuf_tensor("ma_" + name, shape, dt))

    def flow(name, per=0):
        return Flow(C["sems"].enter_context(nc.semaphore("ma_" + name)), per)

    ps = C["psum"]
    in_w = sb("in_w", [P, 4, P])
    xdt_w = sb("xdt_w", [P, 2, DT_RANK])
    xbc_w = sb("xbc_w", [P, 2, 96])
    dt_w = sb("dt_w", [DT_RANK, 2, P])
    out_w = sb("out_w", [P, 2, P])
    chan = sb("chan", [P, 2, 7])
    a_log = sb("a_log", [P, 2, STATES])
    rms_w = sb("rms_w", [P, 1])
    select = sb("select", [96, 2 * STATES, P], BF16)
    xsq = sb("xsq", [P, 2, SEQ])
    rn = sb("rn", [P, 2, SEQ])
    hn = sb("hn", [P, 2, SEQ])
    xi = sb("xi", [P, 2, 2, 3 + SEQ])
    sz = sb("sz", [P, 2, 2, SEQ])
    conv = sb("conv", [P, 2, 2, 2, SEQ])
    xc = sb("xc", [P, 2, 2, SEQ])
    dt = sb("dt", [DT_RANK, 2, SEQ])
    part = sb("part", [96, 3, 2, SEQ], BF16)
    rest = sb("rest", [96, 3, 2, SEQ])
    bc3 = sb("bc3", [96, 2, SEQ], BF16)
    pre = sb("pre", [P, 2, 2, SEQ])
    mag = sb("mag", [P, 2, 2, SEQ])
    delta = sb("delta", [P, 2, 2, SEQ])
    u = sb("u", [P, 2, 2, SEQ])
    a_neg = sb("a_neg", [P, 2, STATES])
    decay = conv.rearrange("p i k b t -> p (i k) b t")
    bc = sb("bc", [P, 4, 2, SEQ])
    dbx = sb("dbx", [P, 4, SEQ])
    state = sb("state", [P, 2, SEQ])
    hc = sb("hc", [P, 4, SEQ])

    loaded, loaded2 = flow("loaded"), flow("loaded2")
    pads = flow("pads")
    xsq_done, ms_done, ln_done, r_done, hn_done = flow("xsq_done"), flow("ms_done"), flow("ln_done"), flow("r_done"), flow("hn_done")
    in_done, in_copied = flow("in_done"), flow("in_copied")
    conv_done, xc_done = flow("conv_done"), flow("xc_done")
    proj_done, dt_copied, split_done = flow("proj_done"), flow("dt_copied"), flow("split_done")
    dtp_done, pre_done, mag_done, sp_exp, sp_ln, delta_done, u_done = (flow(n) for n in (
        "dtp_done", "pre_done", "mag_done", "sp_exp", "sp_ln", "delta_done", "u_done"))
    aexp_done, aneg_done = flow("aexp_done"), flow("aneg_done")
    bc_done, bc_copied, decay_done, dbx_done, scan_done, hc_done, sum_done = (flow(n) for n in (
        "bc_done", "bc_copied", "decay_done", "dbx_done", "scan_done", "hc_done", "sum_done"))
    skip_done, gated_done, out_done, h1_done = flow("skip_done"), flow("gated_done"), flow("out_done"), flow("h1_done")

    block = ctx.enter_context(nc.Block())
    STEPS = [(k, b) for k in range(2) for b in range(2)]

    @block.sync
    def _(sp):
        sp.dma_start(rms_w[:], d["rms1"]).then_inc(loaded.sem, 16)
        sp.dma_start(in_w[:], d["in_w"]).then_inc(loaded.sem, 16)
        for dst, src in ((chan, "chan"), (a_log, "a_log"), (xdt_w, "xdt_w"), (xbc_w, "xbc_w"), (dt_w, "dt_w"), (out_w, "out_w"), (select, "select")):
            sp.dma_start(dst[:], d[src]).then_inc(loaded2.sem, 16)
        for e in range(2):
            weights.load(sp, d, 0, e)

    @block.tensor
    def _(pe):
        pe.wait_ge(C["const_in"].sem, C["const_n"])
        for b in range(2):
            pe.wait_ge(xsq_done.sem, b + 1)
            nc.tensor.matmul(ps[:, b, :], C["mean_ones"], xsq[:, b, :], start=True, stop=True).then_inc(ms_done.sem, 1)
        pe.wait_ge(loaded.sem, 32)
        for b in range(2):
            pe.wait_ge(hn_done.sem, b + 1)
            for m in range(4):
                nc.tensor.matmul(ps[:, (2 + 4 * b + m) % 8, :], in_w[:, m, :], hn[:, b, :], start=True, stop=True).then_inc(in_done.sem, 1)
        pe.wait_ge(loaded2.sem, 112)
        pe.wait_ge(in_copied.sem, 8)
        for b in range(2):
            pe.wait_ge(xc_done.sem, 2 + b + 1)
            for k in range(2):
                nc.tensor.matmul(ps[0:DT_RANK, b, :], xdt_w[:, k, :], xc[:, k, b, :], start=(k == 0), stop=(k == 1))
            for k in range(2):
                last = nc.tensor.matmul(ps[0:96, 2 + b, :], xbc_w[:, k, :], xc[:, k, b, :], start=(k == 0), stop=(k == 1))
            last.then_inc(proj_done.sem, 1)
        for n, (k, b) in enumerate(STEPS):
            pe.wait_ge(dt_copied.sem, b + 1)
            nc.tensor.matmul(ps[:, 4 + n, :], dt_w[:, k, :], dt[:, b, :], start=True, stop=True).then_inc(dtp_done.sem, 1)

        def broadcast(i):
            n, b = divmod(i, 2)
            if i - 1 > 0:
                pe.wait_ge(bc_copied.sem, i - 1)
            for s in range(2):
                last = nc.tensor.matmul(ps[:, 4 + 2 * (i % 2) + s, :], select[:, STATES * s + n, :], bc3[:, b, :], start=True, stop=True)
            last.then_inc(bc_done.sem, 1)

        pe.wait_ge(split_done.sem, 2)
        pe.wait_ge(mag_done.sem, 4)
        broadcast(0)
        broadcast(1)
        pe.wait_ge(dt_copied.sem, 2)
        broadcast(2)
        for i in range(2 * STATES):
            n, b = divmod(i, 2)
            if i + 3 < 2 * STATES:
                broadcast(i + 3)
            for k in range(2):
                j = 2 * i + k
                pe.wait_ge(hc_done.sem, j + 1)
                nc.tensor.matmul(ps[:, 2 * k + b, :], C["ident"], hc[:, j % 4, :], start=(n == 0), stop=(n == STATES - 1)).then_inc(sum_done.sem, 1)
        for b in range(2):
            pe.wait_ge(gated_done.sem, 2 * b + 2)
            for k in range(2):
                last = nc.tensor.matmul(ps[:, 4 + b, :], out_w[:, k, :], xc[:, k, b, :], start=(k == 0), stop=(k == 1))
            last.then_inc(out_done.sem, 1)

    @block.scalar
    def _(ac):
        A = nc.scalar.activation
        nc.scalar.preload_act_table_set("natural_log_exp_and_others")
        ac.wait_ge(C["const_in"].sem, C["const_n"])
        ac.wait_ge(C["fill"].sem, C["fill_n"])
        for b in range(2):
            A(xsq[:, b, :], x[:, b, :], ACT.Square).then_inc(xsq_done.sem, 1)
        for b in range(2):
            ac.wait_ge(ms_done.sem, b + 1)
            A(rn[:, b, :], ps[:, b, :], ACT.Ln, bias=C["eps"]).then_inc(ln_done.sem, 1)
            ac.wait_ge(ln_done.sem, b + 1)
            A(rn[:, b, :], rn[:, b, :], ACT.Exp, scale=-0.5).then_inc(r_done.sem, 1)
        for b in range(2):
            for m in range(2):
                ac.wait_ge(in_done.sem, 4 * b + m + 1)
                A(xi[:, m, b, 3:], ps[:, (2 + 4 * b + m) % 8, :], ACT.Copy).then_inc(in_copied.sem, 1)
        for b in range(2):
            for m in range(2, 4):
                ac.wait_ge(in_done.sem, 4 * b + m + 1)
                A(sz[:, m - 2, b, :], ps[:, (2 + 4 * b + m) % 8, :], ACT.Silu).then_inc(in_copied.sem, 1)
        for b in range(2):
            for k in range(2):
                ac.wait_ge(conv_done.sem, 8 * b + 4 * k + 4)
                A(xc[:, k, b, :], conv[:, 1, k, b, :], ACT.Silu, bias=chan[:, k, 4:5]).then_inc(xc_done.sem, 1)
        nc.scalar.preload_act_table_set("natural_log_exp_and_others")
        A(a_neg[:], a_log[:], ACT.Exp).then_inc(aexp_done.sem, 1)
        for b in range(2):
            ac.wait_ge(proj_done.sem, b + 1)
            A(dt[:, b, :], ps[0:DT_RANK, b, :], ACT.Copy).then_inc(dt_copied.sem, 1)
        for n, (k, b) in enumerate(STEPS):
            ac.wait_ge(mag_done.sem, n + 1)
            A(mag[:, k, b, :], mag[:, k, b, :], ACT.Exp).then_inc(sp_exp.sem, 1)
        for n, (k, b) in enumerate(STEPS):
            ac.wait_ge(sp_exp.sem, n + 1)
            A(mag[:, k, b, :], mag[:, k, b, :], ACT.Ln, bias=C["one"]).then_inc(sp_ln.sem, 1)

        def copy_bc(i):
            ac.wait_ge(bc_done.sem, i + 1)
            if 2 * (i - 3) > 0:
                ac.wait_ge(hc_done.sem, 2 * (i - 3))
            A(bc[:, i % 4], ps[:, 4 + 2 * (i % 2):6 + 2 * (i % 2), :], ACT.Copy).then_inc(bc_copied.sem, 1)

        copy_bc(0)
        copy_bc(1)
        ac.wait_ge(aneg_done.sem, 1)
        ac.wait_ge(delta_done.sem, 4)
        ac.wait_ge(xc_done.sem, 4)
        for n in range(STATES):
            for k in range(2):
                if 4 * (n - 1) > 0:
                    ac.wait_ge(scan_done.sem, 4 * (n - 1))
                A(decay[:, 2 * (n % 2) + k], delta[:, k], ACT.Exp, scale=a_neg[:, k, n:n + 1]).then_inc(decay_done.sem, 1)
                if 2 * n + k + 2 < 2 * STATES:
                    copy_bc(2 * n + k + 2)

    @block.vector
    def _(dv):
        v = nc.vector
        v.memset(xi[:, :, :, 0:3], 0.0).then_inc(pads.sem, 1)
        dv.wait_ge(C["const_in"].sem, C["const_n"])
        dv.wait_ge(loaded.sem, 32)
        for b in range(2):
            dv.wait_ge(r_done.sem, b + 1)
            v.scalar_tensor_tensor(hn[:, b, :], x[:, b, :], rms_w[:, 0:1], rn[:, b, :], ALU.mult, ALU.mult).then_inc(hn_done.sem, 1)
        dv.wait_ge(loaded2.sem, 112)
        dv.wait_ge(pads.sem, 1)
        for b in range(2):
            for k in range(2):
                dv.wait_ge(in_copied.sem, 2 * b + k + 1)
                v.tensor_scalar(conv[:, 0, k, b, :], xi[:, k, b, 0:SEQ], chan[:, k, 0:1], None, ALU.mult).then_inc(conv_done.sem, 1)
                for i in range(1, 4):
                    dv.wait_ge(conv_done.sem, 8 * b + 4 * k + i)
                    v.scalar_tensor_tensor(conv[:, i % 2, k, b, :], xi[:, k, b, i:i + SEQ], chan[:, k, i:i + 1],
                                           conv[:, (i + 1) % 2, k, b, :], ALU.mult, ALU.add).then_inc(conv_done.sem, 1)
        dv.wait_ge(aexp_done.sem, 1)
        v.tensor_scalar(a_neg[:], a_neg[:], -1.0, None, ALU.mult).then_inc(aneg_done.sem, 1)
        step = flow("split_step")
        at = 0
        for b in range(2):
            dv.wait_ge(proj_done.sem, b + 1)
            v.tensor_copy(rest[:, 0, b, :], ps[0:96, 2 + b, :]).then_inc(step.sem, 1)
            for i in range(3):
                at += 1
                dv.wait_ge(step.sem, at)
                v.tensor_copy(part[:, i, b, :], rest[:, i, b, :]).then_inc(step.sem, 1)
                at += 1
                dv.wait_ge(step.sem, at)
                if i < 2:
                    v.tensor_tensor(rest[:, i + 1, b, :], rest[:, i, b, :], part[:, i, b, :], ALU.subtract).then_inc(step.sem, 1)
            for i in range(3):
                last = v.tensor_copy(bc3[32 * i:32 * i + 32, b, :], part[32 * i:32 * i + 32, i, b, :])
            last.then_inc(split_done.sem, 1)
        for n, (k, b) in enumerate(STEPS):
            dv.wait_ge(dtp_done.sem, n + 1)
            v.tensor_scalar(pre[:, k, b, :], ps[:, 4 + n, :], chan[:, k, 5:6], None, ALU.add).then_inc(pre_done.sem, 1)
            dv.wait_ge(pre_done.sem, n + 1)
            v.scalar_tensor_tensor(mag[:, k, b, :], pre[:, k, b, :], -1.0, pre[:, k, b, :], ALU.mult, ALU.min).then_inc(mag_done.sem, 1)
        for n, (k, b) in enumerate(STEPS):
            dv.wait_ge(sp_ln.sem, n + 1)
            v.scalar_tensor_tensor(delta[:, k, b, :], pre[:, k, b, :], 0.0, mag[:, k, b, :], ALU.max, ALU.add).then_inc(delta_done.sem, 1)
            dv.wait_ge(delta_done.sem, n + 1)
            dv.wait_ge(xc_done.sem, 4)
            v.tensor_tensor(u[:, k, b, :], delta[:, k, b, :], xc[:, k, b, :], ALU.mult).then_inc(u_done.sem, 1)

        def times_c(j):
            dv.wait_ge(scan_done.sem, j + 1)
            if j - 3 > 0:
                dv.wait_ge(sum_done.sem, j - 3)
            v.tensor_tensor(hc[:, j % 4, :], state[:, j % 2, :], bc[:, j // 2 % 4, 1, :], ALU.mult).then_inc(hc_done.sem, 1)

        for j in range(4 * STATES):
            n, b, k = j // 4, j // 2 % 2, j % 2
            dv.wait_ge(dbx_done.sem, j + 1)
            dv.wait_ge(decay_done.sem, 2 * n + k + 1)
            if j - 1 > 0:
                dv.wait_ge(hc_done.sem, j - 1)
            v.tensor_tensor_scan(state[:, j % 2, :], decay[:, 2 * (n % 2) + k, b, :], dbx[:, j % 4, :], 0.0, ALU.mult, ALU.add).then_inc(scan_done.sem, 1)
            if j >= 1:
                times_c(j - 1)
        times_c(4 * STATES - 1)
        for n, (b, k) in enumerate(STEPS):
            dv.wait_ge(sum_done.sem, 4 * STATES)
            v.scalar_tensor_tensor(u[:, k, b, :], xc[:, k, b, :], chan[:, k, 6:7], ps[:, 2 * k + b, :], ALU.mult, ALU.add).then_inc(skip_done.sem, 1)
            dv.wait_ge(skip_done.sem, n + 1)
            dv.wait_ge(in_copied.sem, 8)
            v.tensor_tensor(xc[:, k, b, :], u[:, k, b, :], sz[:, k, b, :], ALU.mult).then_inc(gated_done.sem, 1)
        for b in range(2):
            dv.wait_ge(out_done.sem, b + 1)
            v.tensor_tensor(h1[:, b, :], ps[:, 4 + b, :], x[:, b, :], ALU.add).then_inc(h1_done.sem, 1)
        dv.wait_ge(h1_done.sem, 2)

    @block.gpsimd
    def _(pool):
        pool.wait_ge(u_done.sem, 4)
        for j in range(4 * STATES):
            i, b, k = j // 2, j // 2 % 2, j % 2
            pool.wait_ge(bc_copied.sem, i + 1)
            if j - 3 > 0:
                pool.wait_ge(scan_done.sem, j - 3)
            nc.gpsimd.tensor_tensor(dbx[:, j % 4, :], u[:, k, b, :], bc[:, i % 4, 0, :], ALU.mult).then_inc(dbx_done.sem, 1)


def normalise(nc, who, eng, s, b, src, dst, work, rows, C):
    centred, ln = work
    if who == "pe_mean":
        nc.tensor.matmul(rows[0], C["mean_ones"], src, start=True, stop=True).then_inc(s["mean"].sem, 1)
    elif who == "dve_centre":
        eng.wait_ge(*s["mean"].at(s["use"], b + 1))
        nc.vector.tensor_tensor(centred[:, b, :], src, rows[0], ALU.subtract).then_inc(s["centred"].sem, 1)
    elif who == "act_square":
        eng.wait_ge(*s["centred"].at(s["use"], b + 1))
        nc.scalar.activation(ln[:, b, :], centred[:, b, :], ACT.Square).then_inc(s["square"].sem, 1)
    elif who == "pe_var":
        eng.wait_ge(*s["square"].at(s["use"], b + 1))
        nc.tensor.matmul(rows[1], C["mean_ones"], ln[:, b, :], start=True, stop=True).then_inc(s["var"].sem, 1)
    elif who == "act_rstd":
        eng.wait_ge(*s["var"].at(s["use"], b + 1))
        nc.scalar.activation(ln[:, b, :], rows[1], ACT.Ln, bias=C["eps"]).then_inc(s["ln"].sem, 1)
        eng.wait_ge(*s["ln"].at(s["use"], b + 1))
        nc.scalar.activation(ln[:, b, :], ln[:, b, :], ACT.Exp, scale=-0.5).then_inc(s["rstd"].sem, 1)
    elif who == "dve_scale":
        eng.wait_ge(*s["rstd"].at(s["use"], b + 1))
        nc.vector.tensor_tensor(dst, centred[:, b, :], ln[:, b, :], ALU.mult).then_inc(s["scaled"].sem, 1)


class ExpertWeights:

    def __init__(self, nc, ctx, C):
        def sb(name, shape):
            return ctx.enter_context(nc.sbuf_tensor("mo_" + name, shape, F32))

        self.gate, self.up = sb("wg", [P, 2, 4 * P]), sb("wu", [P, 2, 4 * P])
        self.down = sb("wd", [P, 2, 4, P])
        self.loaded = [Flow(C["sems"].enter_context(nc.semaphore(f"mo_weights_{i}")), 48) for i in range(2)]

    def load(self, sp, d, turn, e):
        sp.dma_start(self.gate[:, e, :], expert(d["wg"], turn, e)).then_inc(self.loaded[e].sem, 16)
        sp.dma_start(self.up[:, e, :], expert(d["wu"], turn, e)).then_inc(self.loaded[e].sem, 16)
        sp.dma_start(self.down[:, e, :, :], expert(d["wd"], turn, e)).then_inc(self.loaded[e].sem, 16)


def build_moe(nc, ctx, x, h1, x1, weights, d, C):
    def sb(name, shape, dt=F32):
        return ctx.enter_context(nc.sbuf_tensor("mo_" + name, shape, dt))

    def flow(name, per=0):
        return Flow(C["sems"].enter_context(nc.semaphore("mo_" + name)), per)

    ps = C["psum"]
    rms_w = sb("rms_w", [P, 1])
    router = sb("router", [P, EXPERTS])
    order = sb("order", [P, 8, EXPERTS])
    hsq = sb("hsq", [P, 2, SEQ])
    rn = sb("rn", [P, 2, SEQ])
    hn = sb("hn", [P, 2, SEQ])
    G = [sb(f"gate{i}", [P, 8, EXPERTS]) for i in range(7)]
    col = sb("col", [P, 8, 6])
    wT = sb("wT", [EXPERTS, 2, SEQ])
    w_all = sb("w_all", [P, EXPERTS, 2, SEQ])
    sg = sb("sg", [P, 2, SEQ])
    hid = sb("hid", [P, 8, SEQ])
    wy = sb("wy", [P, 2, SEQ])
    total = sb("total", [P, 2, SEQ])

    loaded = flow("loaded")
    hsq_done, ms_done, ln_done, r_done, hn_done = (flow(n) for n in ("hsq_done", "ms_done", "ln_done", "r_done", "hn_done"))
    logit_done, gexp_done, gate_step, weight_done = (flow(n) for n in ("logit_done", "gexp_done", "gate_step", "weight_done"))
    wt_done, wt_copied, wt_out = (flow(n) for n in ("wt_done", "wt_copied", "wt_out"))
    spread = [flow(f"spread_{i}") for i in range(2)]
    pair_done, silu_done, hid_done = flow("pair_done", 16), flow("silu_done", 16), flow("hid_done", 16)
    down_done, wy_done, acc_done, start_done = flow("down_done", 4), flow("wy_done", 4), flow("acc_done", 4), flow("start_done")
    s = C["norm"](0)

    TURNS = EXPERTS // 2

    def all_turns(eng, body):
        body(0)
        with eng.Fori(1, TURNS) as turn:
            body(turn)

    def passes(turn):
        return range(0 if isinstance(turn, int) else -1, 3)

    block = ctx.enter_context(nc.Block())

    @block.sync
    def _(sp):
        for dst, src in ((rms_w, "rms2"), (router, "router"), (order, "order")):
            sp.dma_start(dst[:], d[src]).then_inc(loaded.sem, 16)
        sp.wait_ge(wt_copied.sem, 2)
        sp.dma_start(d["gates"], wT[:]).then_inc(wt_out.sem, 16)
        sp.wait_ge(wt_out.sem, 16)
        for i, (lo, hi) in enumerate(((0, 2), (2, EXPERTS))):
            src = bass.AP(d["gates"].tensor, lo * 2 * SEQ, [[0, P], [1, (hi - lo) * 2 * SEQ]])
            sp.dma_start(w_all[:, lo:hi].rearrange("p e b t -> p (e b t)"), src).then_inc(spread[i].sem, 16)
        with sp.Fori(1, TURNS) as turn:
            for e in range(2):
                sp.wait_ge(*down_done.at(turn, 2 * e - 2))
                weights.load(sp, d, turn, e)

    @block.tensor
    def _(pe):
        pe.wait_ge(loaded.sem, 48)
        for b in range(2):
            pe.wait_ge(hsq_done.sem, b + 1)
            nc.tensor.matmul(ps[:, b, :], C["mean_ones"], hsq[:, b, :], start=True, stop=True).then_inc(ms_done.sem, 1)
        for tile in range(8):
            b, t0 = tile // 4, tile % 4 * 128
            pe.wait_ge(hn_done.sem, b + 1)
            last = nc.tensor.matmul(ps[:, 6, 8 * tile:8 * tile + 8], hn[:, b, t0:t0 + 128], router[:], start=True, stop=True)
        last.then_inc(logit_done.sem, 1)

        def down(turn, i):
            e, b = i // 2 % 2, i % 2
            pe.wait_ge(*hid_done.at(turn, 4 * i + 4))
            if wy_done.any(turn, i - 1):
                pe.wait_ge(*wy_done.at(turn, i - 1))
            for j in range(4):
                last = nc.tensor.matmul(ps[:, 4 + b, :], weights.down[:, e, j, :], hid[:, 4 * b + j, :], start=(j == 0), stop=(j == 3))
            last.then_inc(down_done.sem, 1)

        def body(turn):
            for i in range(4):
                e, b = divmod(i, 2)
                if b == 0:
                    pe.wait_ge(*weights.loaded[e].at(turn, 48))
                for j in range(4):
                    n = 4 * i + j
                    bank = 2 * (n % 2)
                    if hid_done.any(turn, n - 1):
                        pe.wait_ge(*hid_done.at(turn, n - 1))
                    nc.tensor.matmul(ps[:, bank, :], weights.gate[:, e, P * j:P * j + P], hn[:, b, :], start=True, stop=True)
                    nc.tensor.matmul(ps[:, bank + 1, :], weights.up[:, e, P * j:P * j + P], hn[:, b, :], start=True, stop=True).then_inc(pair_done.sem, 1)
                    if j == 1 and i - 1 in passes(turn):
                        down(turn, i - 1)
                    if isinstance(turn, int) and n == 2:
                        pe.wait_ge(weight_done.sem, 1)
                        for tile in range(8):
                            last = nc.tensor.transpose(ps[0:EXPERTS, 6 + tile // 4, tile % 4 * P:tile % 4 * P + P], G[6][:, tile, :], C["ident"])
                        last.then_inc(wt_done.sem, 1)

        all_turns(pe, body)
        down(TURNS - 1, 3)
        pe.wait_ge(acc_done.sem, 4 * TURNS)
        for b in range(2):
            normalise(nc, "pe_mean", pe, s, b, total[:, b, :], None, (None, None), (ps[:, b, :], ps[:, 2 + b, :]), C)
        for b in range(2):
            normalise(nc, "pe_var", pe, s, b, None, None, (hsq, rn), (ps[:, b, :], ps[:, 2 + b, :]), C)

    @block.scalar
    def _(ac):
        A = nc.scalar.activation
        nc.scalar.preload_act_table_set("natural_log_exp_and_others")
        for b in range(2):
            A(hsq[:, b, :], h1[:, b, :], ACT.Square).then_inc(hsq_done.sem, 1)
        for b in range(2):
            ac.wait_ge(ms_done.sem, b + 1)
            A(rn[:, b, :], ps[:, b, :], ACT.Ln, bias=C["eps"]).then_inc(ln_done.sem, 1)
            ac.wait_ge(ln_done.sem, b + 1)
            A(rn[:, b, :], rn[:, b, :], ACT.Exp, scale=-0.5).then_inc(r_done.sem, 1)
        ac.wait_ge(gate_step.sem, 2)
        A(G[1][:], G[0][:], ACT.Exp).then_inc(gexp_done.sem, 1)
        nc.scalar.preload_act_table_set("silu_and_others")

        def body(turn):
            for n in range(16):
                ac.wait_ge(*pair_done.at(turn, n + 1))
                if hid_done.any(turn, n - 1):
                    ac.wait_ge(*hid_done.at(turn, n - 1))
                A(sg[:, n % 2, :], ps[:, 2 * (n % 2), :], ACT.Silu).then_inc(silu_done.sem, 1)
                if isinstance(turn, int) and n == 2:
                    ac.wait_ge(wt_done.sem, 1)
                    for b in range(2):
                        A(wT[:, b, :], ps[0:EXPERTS, 6 + b, :], ACT.Copy).then_inc(wt_copied.sem, 1)

        all_turns(ac, body)
        nc.scalar.preload_act_table_set("natural_log_exp_and_others")
        for b in range(2):
            normalise(nc, "act_square", ac, s, b, None, None, (hsq, rn), None, C)
        for b in range(2):
            normalise(nc, "act_rstd", ac, s, b, None, None, (hsq, rn), (ps[:, b, :], ps[:, 2 + b, :]), C)

    @block.vector
    def _(dv):
        v = nc.vector
        dv.wait_ge(loaded.sem, 48)
        for b in range(2):
            dv.wait_ge(r_done.sem, b + 1)
            v.scalar_tensor_tensor(hn[:, b, :], h1[:, b, :], rms_w[:, 0:1], rn[:, b, :], ALU.mult, ALU.mult).then_inc(hn_done.sem, 1)
        for b in range(2):
            v.tensor_tensor(total[:, b, :], x[:, b, :], h1[:, b, :], ALU.add).then_inc(start_done.sem, 1)

        at = [0]

        def go(ins):
            ins.then_inc(gate_step.sem, 1)
            at[0] += 1

        def settled():
            dv.wait_ge(gate_step.sem, at[0])

        def bc8(n):
            return col[:, :, n:n + 1].to_broadcast([P, 8, EXPERTS])

        def best(score, hot, work, n):
            go(v.tensor_reduce(col[:, :, n], score[:], AX, ALU.max))
            settled()
            go(v.tensor_tensor(hot[:], score[:], bc8(n), ALU.is_equal))
            settled()
            go(v.tensor_tensor(work[:], hot[:], order[:], ALU.mult))
            settled()
            go(v.tensor_reduce(col[:, :, n + 1], work[:], AX, ALU.max))
            settled()
            go(v.tensor_tensor(hot[:], order[:], bc8(n + 1), ALU.is_equal))
            settled()

        dv.wait_ge(logit_done.sem, 1)
        go(v.tensor_reduce(col[:, :, 0], ps[:, 6, 0:64].rearrange("p (t e) -> p t e", e=8), AX, ALU.max))
        settled()
        go(v.tensor_tensor(G[0][:], ps[:, 6, 0:64].rearrange("p (t e) -> p t e", e=8), bc8(0), ALU.subtract))
        dv.wait_ge(gexp_done.sem, 1)
        go(v.tensor_reduce(col[:, :, 1], G[1][:], AX, ALU.add))
        settled()
        go(v.reciprocal(col[:, :, 0], col[:, :, 1]))
        settled()
        go(v.tensor_tensor(G[2][:], G[1][:], bc8(0), ALU.mult))
        settled()
        best(G[2], G[3], G[5], 2)
        go(v.scalar_tensor_tensor(G[4][:], G[3][:], -2.0, G[2][:], ALU.mult, ALU.add))
        settled()
        best(G[4], G[0], G[5], 4)
        go(v.tensor_tensor(G[5][:], G[0][:], G[3][:], ALU.add))
        settled()
        v.tensor_tensor(G[6][:], G[5][:], G[2][:], ALU.mult).then_inc(weight_done.sem, 1)

        def weigh(turn, i):
            dv.wait_ge(*down_done.at(turn, i + 1))
            if acc_done.any(turn, i - 1):
                dv.wait_ge(*acc_done.at(turn, i - 1))
            v.tensor_tensor(wy[:, i % 2, :], ps[:, 4 + i % 2, :], w_all[:, bass.ds(turn * 2 + i // 2, 1), i % 2, :], ALU.mult).then_inc(wy_done.sem, 1)

        def body(turn):
            for n in range(16):
                i, j = divmod(n, 4)
                dv.wait_ge(*silu_done.at(turn, n + 1))
                if j == 0:
                    if down_done.any(turn, i - 1):
                        dv.wait_ge(*down_done.at(turn, i - 1))
                v.tensor_tensor(hid[:, n % 8, :], sg[:, n % 2, :], ps[:, 2 * (n % 2) + 1, :], ALU.mult).then_inc(hid_done.sem, 1)
                if j == 3 and i - 1 in passes(turn):
                    if isinstance(turn, int) and i == 1:
                        dv.wait_ge(spread[0].sem, 16)
                    if not isinstance(turn, int) and i == 0:
                        dv.wait_ge(spread[1].sem, 16)
                    weigh(turn, i - 1)

        all_turns(dv, body)
        weigh(TURNS - 1, 3)
        for b in range(2):
            normalise(nc, "dve_centre", dv, s, b, total[:, b, :], None, (hsq, rn), (ps[:, b, :], ps[:, 2 + b, :]), C)
        for b in range(2):
            normalise(nc, "dve_scale", dv, s, b, None, x1[:, b, :], (hsq, rn), None, C)
        dv.wait_ge(*s["scaled"].at(s["use"], 2))

    @block.gpsimd
    def _(pool):
        def accumulate(turn, i):
            b = i % 2
            pool.wait_ge(*wy_done.at(turn, i + 1))
            if acc_done.any(turn, i - 1):
                pool.wait_ge(*acc_done.at(turn, i - 1))
            nc.gpsimd.tensor_tensor(total[:, b, :], total[:, b, :], wy[:, b, :], ALU.add).then_inc(acc_done.sem, 1)

        def body(turn):
            for i in passes(turn):
                accumulate(turn, i)

        pool.wait_ge(start_done.sem, 2)
        all_turns(pool, body)
        accumulate(TURNS - 1, 3)


def build_cross(nc, ctx, x1, x2, d, C):
    def sb(name, shape, dt=F32):
        return ctx.enter_context(nc.sbuf_tensor("cr_" + name, shape, dt))

    def flow(name, per=0):
        return Flow(C["sems"].enter_context(nc.semaphore("cr_" + name)), per)

    ps = C["psum"]
    wq = sb("wq", [P, P])
    wk = sb("wk", [P, P])
    wv = sb("wv", [P, P])
    wo = sb("wo", [P, P])
    ctxT = sb("ctxT", [P, 2, 4, KEYS])
    rel = sb("rel", [BUCKETS, HEADS])
    onehot = sb("onehot", [BUCKETS, SPAN])
    head_of = sb("head_of", [P, HEADS])
    quarter = sb("quarter", [P, HEADS])
    line = sb("line", [HEADS, SPAN])
    bias = sb("bias", [P, 4, HEADS, KEYS])
    qT = sb("qT", [P, 2, SEQ])
    kbd = sb("kbd", [P, 2, HEADS, KEYS])
    vbd = sb("vbd", [P, 2, HEADS, 8])
    sc = sb("sc", [P, 2, HEADS, KEYS])
    pr = sb("pr", [P, 2, HEADS, KEYS])
    mx = sb("mx", [P, 2, HEADS])
    sm = sb("sm", [P, 2, HEADS])
    ri = sb("ri", [P, 2, HEADS])
    pT = sb("pT", [P, 2, 4, P])
    oT = sb("oT", [P, 2, SEQ])
    centred = sb("centred", [P, 2, SEQ])
    ln = sb("ln", [P, 2, SEQ])
    total = sb("total", [P, 2, SEQ])

    loaded, loaded2 = flow("loaded"), flow("loaded2")
    line_done, line_copied, line_out, bias_in = (flow(n) for n in ("line_done", "line_copied", "line_out", "bias_in"))
    q_done, q_copied, k_done, kbd_done, v_done, vbd_done = (flow(n) for n in ("q_done", "q_copied", "k_done", "kbd_done", "v_done", "vbd_done"))
    s_done, add_done, mx_done, sub_done, exp_done, sum_done, rec_done, norm_done = (flow(n) for n in (
        "s_done", "add_done", "mx_done", "sub_done", "exp_done", "sum_done", "rec_done", "norm_done"))
    t_done, t_copied, o_done, o_copied, wo_done, res_done = (flow(n) for n in ("t_done", "t_copied", "o_done", "o_copied", "wo_done", "res_done"))
    s = C["norm"](1)

    block = ctx.enter_context(nc.Block())

    @block.sync
    def _(sp):
        for dst, src in ((rel, "rel"), (onehot, "onehot")):
            sp.dma_start(dst[:], d[src]).then_inc(loaded.sem, 16)
        for dst, src in ((wq, "xwq"), (wk, "xwk"), (wv, "xwv"), (wo, "xwo"), (ctxT, "ctxT"), (head_of, "head_of"), (quarter, "quarter")):
            sp.dma_start(dst[:], d[src]).then_inc(loaded2.sem, 16)
        sp.wait_ge(line_copied.sem, 2)
        sp.dma_start(d["line"], line[:]).then_inc(line_out.sem, 16)
        sp.wait_ge(line_out.sem, 16)
        for tile in range(4):
            src = bass.AP(d["line"].tensor, 128 * tile, [[1, P], [SPAN, HEADS], [1, KEYS]])
            sp.dma_start(bias[:, tile], src).then_inc(bias_in.sem, 16)

    @block.tensor
    def _(pe):
        pe.wait_ge(loaded.sem, 32)
        nc.tensor.matmul(ps[0:HEADS, 0, :], rel[:], onehot[:, 0:512], start=True, stop=True).then_inc(line_done.sem, 1)
        nc.tensor.matmul(ps[0:HEADS, 1, 0:SPAN - 512], rel[:], onehot[:, 512:SPAN], start=True, stop=True).then_inc(line_done.sem, 1)
        pe.wait_ge(loaded2.sem, 112)
        for b in range(2):
            nc.tensor.matmul(ps[:, 2 + b, 0:KEYS], wk[:], ctxT[:, b, 0, :], start=True, stop=True).then_inc(k_done.sem, 1)
            nc.tensor.matmul(ps[:, 4 + b, 0:P], ctxT[:, b].rearrange("p r k -> p (r k)"), wv[:], start=True, stop=True).then_inc(v_done.sem, 1)
        for b in range(2):
            nc.tensor.matmul(ps[:, 6 + b, :], wq[:], x1[:, b, :], start=True, stop=True).then_inc(q_done.sem, 1)

        def scores(u):
            b, t0 = u // 4, u % 4 * 128
            if u == 0:
                pe.wait_ge(line_copied.sem, 2)
                pe.wait_ge(kbd_done.sem, 2)
            pe.wait_ge(q_copied.sem, b + 1)
            if u - 1 > 0:
                pe.wait_ge(add_done.sem, u - 1)
            nc.tensor.matmul(ps[:, u % 2, :], qT[:, b, t0:t0 + 128], kbd[:, b].rearrange("p h k -> p (h k)"), start=True, stop=True).then_inc(s_done.sem, 1)

        def turn(u):
            pe.wait_ge(norm_done.sem, u + 1)
            if u - 1 > 0:
                pe.wait_ge(t_copied.sem, u - 1)
            pe.wait_ge(kbd_done.sem, 2)
            for g in range(4):
                last = nc.tensor.transpose(ps[:, 2 + u % 2, 128 * g:128 * g + 128], pr[:, u % 2, 4 * g:4 * g + 4, :].rearrange("p h k -> p (h k)"), C["ident"])
            last.then_inc(t_done.sem, 1)

        def values(u):
            b, t0 = u // 4, u % 4 * 128
            pe.wait_ge(vbd_done.sem, 2)
            pe.wait_ge(t_copied.sem, u + 1)
            for g in range(4):
                last = nc.tensor.matmul(ps[32 * g:32 * g + 32, 4 + b, t0:t0 + 128], vbd[:, b, 4 * g:4 * g + 4, :].rearrange("p h d -> p (h d)"),
                                        pT[:, u % 2, g, :], start=True, stop=True)
            last.then_inc(o_done.sem, 1)

        scores(0)
        for u in range(8):
            if u < 7:
                scores(u + 1)
            turn(u)
            values(u)
        for b in range(2):
            pe.wait_ge(o_copied.sem, b + 1)
            nc.tensor.matmul(ps[:, 6 + b, :], wo[:], oT[:, b, :], start=True, stop=True).then_inc(wo_done.sem, 1)
        pe.wait_ge(add_done.sem, 8)
        pe.wait_ge(t_copied.sem, 8)
        for b in range(2):
            pe.wait_ge(res_done.sem, b + 1)
            normalise(nc, "pe_mean", pe, s, b, total[:, b, :], None, (None, None), (ps[:, b, :], ps[:, 2 + b, :]), C)
        for b in range(2):
            normalise(nc, "pe_var", pe, s, b, None, None, (centred, ln), (ps[:, b, :], ps[:, 2 + b, :]), C)

    @block.scalar
    def _(ac):
        A = nc.scalar.activation
        nc.scalar.preload_act_table_set("natural_log_exp_and_others")
        ac.wait_ge(line_done.sem, 1)
        A(line[:, 0:512], ps[0:HEADS, 0, :], ACT.Copy).then_inc(line_copied.sem, 1)
        ac.wait_ge(line_done.sem, 2)
        A(line[:, 512:SPAN], ps[0:HEADS, 1, 0:SPAN - 512], ACT.Copy).then_inc(line_copied.sem, 1)
        for b in range(2):
            ac.wait_ge(q_done.sem, b + 1)
            A(qT[:, b, :], ps[:, 6 + b, :], ACT.Copy).then_inc(q_copied.sem, 1)
        for u in range(9):
            if u >= 1:
                ac.wait_ge(t_done.sem, u)
                if u - 2 > 0:
                    ac.wait_ge(o_done.sem, u - 2)
                A(pT[:, (u - 1) % 2].rearrange("p g t -> p (g t)"), ps[:, 2 + (u - 1) % 2, :], ACT.Copy).then_inc(t_copied.sem, 1)
            if u < 8:
                ac.wait_ge(sub_done.sem, u + 1)
                A(pr[:, u % 2], pr[:, u % 2], ACT.Exp).then_inc(exp_done.sem, 1)
            if u == 5 or u == 8:
                b = u // 8
                ac.wait_ge(o_done.sem, 4 * b + 4)
                A(oT[:, b, :], ps[:, 4 + b, :], ACT.Copy).then_inc(o_copied.sem, 1)
        for b in range(2):
            normalise(nc, "act_square", ac, s, b, None, None, (centred, ln), None, C)
        for b in range(2):
            normalise(nc, "act_rstd", ac, s, b, None, None, (centred, ln), (ps[:, b, :], ps[:, 2 + b, :]), C)

    @block.vector
    def _(dv):
        v = nc.vector
        dv.wait_ge(loaded2.sem, 112)
        for b in range(2):
            dv.wait_ge(k_done.sem, b + 1)
            v.tensor_tensor(kbd[:, b], ps[:, 2 + b, 0:KEYS].unsqueeze(1).to_broadcast([P, HEADS, KEYS]),
                            head_of[:].unsqueeze(2).to_broadcast([P, HEADS, KEYS]), ALU.mult).then_inc(kbd_done.sem, 1)
            dv.wait_ge(v_done.sem, b + 1)
            v.tensor_tensor(vbd[:, b], ps[:, 4 + b, 0:P].rearrange("p (h d) -> p h d", d=8),
                            quarter[:].unsqueeze(2).to_broadcast([P, HEADS, 8]), ALU.mult).then_inc(vbd_done.sem, 1)
        dv.wait_ge(bias_in.sem, 64)
        for u in range(8):
            i = u % 2
            dv.wait_ge(s_done.sem, u + 1)
            if u - 1 > 0:
                dv.wait_ge(sub_done.sem, u - 1)
            v.tensor_tensor(sc[:, i], ps[:, i, :].rearrange("p (h k) -> p h k", k=KEYS), bias[:, u % 4], ALU.add).then_inc(add_done.sem, 1)
            dv.wait_ge(add_done.sem, u + 1)
            if u - 1 > 0:
                dv.wait_ge(sub_done.sem, u - 1)
            v.tensor_reduce(mx[:, i, :], sc[:, i], AX, ALU.max).then_inc(mx_done.sem, 1)
            dv.wait_ge(mx_done.sem, u + 1)
            if u - 1 > 0:
                dv.wait_ge(t_done.sem, u - 1)
            v.tensor_tensor(pr[:, i], sc[:, i], mx[:, i, :].unsqueeze(2).to_broadcast([P, HEADS, KEYS]), ALU.subtract).then_inc(sub_done.sem, 1)
            dv.wait_ge(exp_done.sem, u + 1)
            if u - 1 > 0:
                dv.wait_ge(rec_done.sem, u - 1)
            v.tensor_reduce(sm[:, i, :], pr[:, i], AX, ALU.add).then_inc(sum_done.sem, 1)
            dv.wait_ge(sum_done.sem, u + 1)
            if u - 1 > 0:
                dv.wait_ge(norm_done.sem, u - 1)
            v.reciprocal(ri[:, i, :], sm[:, i, :]).then_inc(rec_done.sem, 1)
        for b in range(2):
            dv.wait_ge(wo_done.sem, b + 1)
            v.tensor_tensor(total[:, b, :], ps[:, 6 + b, :], x1[:, b, :], ALU.add).then_inc(res_done.sem, 1)
        for b in range(2):
            normalise(nc, "dve_centre", dv, s, b, total[:, b, :], None, (centred, ln), (ps[:, b, :], ps[:, 2 + b, :]), C)
        for b in range(2):
            normalise(nc, "dve_scale", dv, s, b, None, x2[:, b, :], (centred, ln), None, C)
        dv.wait_ge(*s["scaled"].at(s["use"], 2))

    @block.gpsimd
    def _(pool):
        for u in range(8):
            i = u % 2
            pool.wait_ge(rec_done.sem, u + 1)
            nc.gpsimd.tensor_tensor(pr[:, i], pr[:, i], ri[:, i, :].unsqueeze(2).to_broadcast([P, HEADS, KEYS]), ALU.mult).then_inc(norm_done.sem, 1)


def build_stack(nc, ctx, Y, d, C):
    def sb(name, shape, dt=F32):
        return ctx.enter_context(nc.sbuf_tensor("st_" + name, shape, dt))

    def flow(name, per):
        return Flow(C["sems"].enter_context(nc.semaphore("st_" + name)), per)

    ps = C["psum"]
    QK_BANK = [ps[:, 0, :], ps[:, 1, :]]
    V_BANK, NORM_BANK, SCORE_BANK, TURN_BANK = (ps[:, 2 + i, :] for i in range(4))
    OUT_BANK = [ps[:, 6, :], ps[:, 7, :]]
    UNITS, PAIRS = 16, 8

    w_in_proj = sb("w_in_proj", [P, PAIRS, 3 * P])
    wo = sb("wo", [P, PAIRS, P])
    w1 = sb("w1", [P, 2 * HID])
    w2 = sb("w2", [P, 3, P])
    rope_scale = sb("rope_scale", [P, 2, 4])
    ffn_param = sb("ffn_param", [P, 9])
    table = sb("table", [P, 4, SEQ])
    q_blocks = sb("q_blocks", [P, 2, 8, 2, 2, WIN])
    kT = sb("kT", [P, 2, WIN + SEQ])
    vn = sb("vn", [P, 2, 4, P])
    vs = sb("vs", [P, 2, 4, P])
    sq = sb("sq", [P, 2, SEQ])
    rn = sb("rn", [P, 2, SEQ])
    swapped = sb("swapped", [P, 2, SEQ])
    cos_part = sb("cos_part", [P, 2, SEQ])
    sin_part = sb("sin_part", [P, 2, SEQ])
    turned = sb("turned", [P, 2, SEQ])
    prob = sb("prob", [P, 2, 8, 64])
    pn = sb("pn", [P, 2, 8, 64])
    p_blocks = sb("p_blocks", [P, 2, 4, 2, 2, 2, WIN])
    oT = sb("oT", [P, 2, SEQ])
    mx = sb("mx", [P, 2, 8])
    rs = sb("rs", [P, 2, 8])
    ri = sb("ri", [P, 2, 8])
    dx = sb("dx", [P, SEQ])
    dsq = sb("dsq", [P, SEQ])
    rstd = sb("rstd", [P, SEQ])
    xn = sb("xn", [P, SEQ])
    gate = sb("gate", [P, SEQ])
    act = sb("act", [P, 2, SEQ])

    proj_in = [flow(f"proj_in_{i}", 16) for i in range(2)]
    wo_in = [flow(f"wo_in_{i}", 16) for i in range(2)]
    scale_in = [flow(f"scale_in_{i}", 16) for i in range(2)]
    ffn_in, table_in = flow("ffn_in", 80), flow("table_in", 0)
    vs_in = [flow(f"vs_in_{i}", UNITS // 2 * 32) for i in range(2)]
    pads_zero = flow("pads_zero", 0)
    qk_done, sq_done, norm_done, ln_done, r_done = (flow(n, 2 * UNITS) for n in ("qk_done", "sq_done", "norm_done", "ln_done", "r_done"))
    cos_done, swap_done, sin_done, add_done = (flow(n, 2 * UNITS) for n in ("cos_done", "swap_done", "sin_done", "add_done"))
    rope_done = flow("rope_done", 3 * UNITS)
    v_done, v_copied = flow("v_done", UNITS), flow("v_copied", UNITS)
    score_done, mx_done, sub_done, exp_done, sum_done, rec_done, pn_done, t_done, o_copied, pv_done = (flow(n, UNITS) for n in (
        "score_done", "mx_done", "sub_done", "exp_done", "sum_done", "rec_done", "pn_done", "t_done", "o_copied", "pv_done"))
    pt_copied = flow("pt_copied", 2 * UNITS)
    wo_step = flow("wo_step", UNITS)
    res1_done, res2_done = flow("res1_done", 4), flow("res2_done", 4)
    mean_done, dx_done, dsq_done, var_done, lnv_done, rstd_done, xh_done, xn_done = (flow(n, 2) for n in (
        "mean_done", "dx_done", "dsq_done", "var_done", "lnv_done", "rstd_done", "xh_done", "xn_done"))
    w1_done, gate_done, act_done, w2_step = (flow(n, 6) for n in ("w1_done", "gate_done", "act_done", "w2_step"))

    ROWS = [P, P, HID - 2 * P]

    class Steps:

        def __init__(self, turn, first, last):
            self.turn, self.first, self.last = turn, first, last
            self.range = range(-2 if first else 0, UNITS + 6 if last else UNITS)

        def unit(self, n):
            return (n >= 0 or not self.first) and (n < UNITS or not self.last)

        def stage(self, t):
            job, stage = t // 8 - 1, t % 8
            there = stage < 6 and (job >= 0 or not self.first) and (job < 1 or self.last)
            return (job, stage) if there and t >= 0 else (None, None)

    def all_turns(eng, body):
        body(Steps(0, True, False))
        with eng.Fori(1, LAYERS - 1) as turn:
            body(Steps(turn, False, False))
        body(Steps(LAYERS - 1, False, True))

    block = ctx.enter_context(nc.Block())

    @block.sync
    def _(sp):
        def load_proj(layer, half):
            sp.dma_start(w_in_proj[:, 4 * half:4 * half + 4, :], at_layer(d["w_proj"], layer)[:, 4 * half:4 * half + 4, :]).then_inc(proj_in[half].sem, 16)

        def load_wo(layer, half):
            sp.dma_start(wo[:, 4 * half:4 * half + 4, :], at_layer(d["wo"], layer)[:, 4 * half:4 * half + 4, :]).then_inc(wo_in[half].sem, 16)

        def load_scale(layer, b):
            sp.dma_start(rope_scale[:, b, :], at_layer(d["rope_scale"], layer)).then_inc(scale_in[b].sem, 16)

        def load_ffn(layer):
            sp.dma_start(w1[:], at_layer(d["w1"], layer)).then_inc(ffn_in.sem, 16)
            for j, rows in enumerate(ROWS):
                sp.dma_start(w2[0:rows, j, :], at_layer(d["w2"], layer)[j * P:j * P + rows, :]).then_inc(ffn_in.sem, 16)
            sp.dma_start(ffn_param[:], at_layer(d["ffn_param"], layer)).then_inc(ffn_in.sem, 16)

        load_proj(0, 0)
        sp.dma_start(table[:], d["rope"]).then_inc(table_in.sem, 16)
        for half in range(2):
            load_scale(0, half)
        load_proj(0, 1)
        for half in range(2):
            load_wo(0, half)

        def body(s):
            turn = s.turn
            for t in s.range:
                if t == 0 and not s.first:
                    sp.wait_ge(*wo_step.at(turn, 0))
                    load_wo(turn, 1)
                if t == 6:
                    if res2_done.any(turn, 0):
                        sp.wait_ge(*res2_done.at(turn, 0))
                    load_ffn(turn)
                if not s.last:
                    if t == 8:
                        sp.wait_ge(*sin_done.at(turn, 16))
                        load_scale(turn + 1, 0)
                    if t == 11:
                        sp.wait_ge(*v_done.at(turn, 12))
                        load_proj(turn + 1, 0)
                    if t == 13:
                        sp.wait_ge(*wo_step.at(turn, 12))
                        load_wo(turn + 1, 0)
                    if t == 15:
                        sp.wait_ge(*v_done.at(turn, 16))
                        load_proj(turn + 1, 1)
                        sp.wait_ge(*sin_done.at(turn, 32))
                        load_scale(turn + 1, 1)
                n = t + 1
                if t >= -1 and s.unit(n):
                    r = n % 2
                    sp.wait_ge(*v_copied.at(turn, n + 1))
                    sp.dma_start(vs[32:128, r, :, :], vn[0:96, r, :, :]).then_inc(vs_in[r].sem, 16)
                    sp.dma_start(vs[0:32, r, 1:4, :], vn[96:128, r, 0:3, :]).then_inc(vs_in[r].sem, 16)

        all_turns(sp, body)

    @block.tensor
    def _(pe):
        mm = nc.tensor.matmul

        def project(s, n, which):
            b, pair = n // 8 % 2, n % 8
            if which == 0:
                pe.wait_ge(*proj_in[pair // 4].at(s.turn, 16 * (n // 16) + 16))
                if n % 8 == 0:
                    if res2_done.any(s.turn, 4 * (n // 16) - 4 + 2 * b + 2):
                        pe.wait_ge(*res2_done.at(s.turn, 4 * (n // 16) - 4 + 2 * b + 2))
            if swap_done.any(s.turn, 2 * (n - 1) + which + 1):
                pe.wait_ge(*swap_done.at(s.turn, 2 * (n - 1) + which + 1))
            mm(QK_BANK[which], w_in_proj[:, pair, P * which:P * which + P], Y[:, b, 0:SEQ], start=True, stop=True).then_inc(qk_done.sem, 1)

        def head_norm(s, n, which):
            pe.wait_ge(*sq_done.at(s.turn, 2 * n + which + 1))
            if ln_done.any(s.turn, 2 * n + which):
                pe.wait_ge(*ln_done.at(s.turn, 2 * n + which))
            mm(NORM_BANK, C["head_ones"], sq[:, which, :], start=True, stop=True).then_inc(norm_done.sem, 1)

        def project_v(s, n, here, before):
            b, pair = n // 8 % 2, n % 8
            if v_copied.any(s.turn, n):
                pe.wait_ge(*v_copied.at(s.turn, n))
            if before[1] == 1:
                pe.wait_ge(*lnv_done.at(s.turn, before[0] + 1))
            if here[1] in (2, 3, 4):
                pe.wait_ge(*act_done.at(s.turn, 3 * here[0] + here[1] - 1))
            for tile in range(4):
                last = mm(V_BANK[:, P * tile:P * tile + P], Y[:, b, P * tile:P * tile + P], w_in_proj[:, pair, 2 * P:3 * P], start=True, stop=True)
            last.then_inc(v_done.sem, 1)

        def scores(s, n):
            r = n % 2
            pe.wait_ge(*rope_done.at(s.turn, 3 * n + 3))
            if sub_done.any(s.turn, n):
                pe.wait_ge(*sub_done.at(s.turn, n))
            mm(SCORE_BANK, C["ident16"], C["mask16"], start=True, stop=False, skip_group_check=True)
            for i in range(8):
                for odd in range(2):
                    t0 = 64 * i + WIN * odd
                    last = mm(SCORE_BANK[64 * odd:64 * odd + 64, 64 * i:64 * i + 64],
                              q_blocks[:, r, i, odd].rearrange("p h q -> p (h q)"), kT[:, r, t0:t0 + 64],
                              start=False, stop=(i == 7), skip_group_check=True)
            last.then_inc(score_done.sem, 1)

        def turn_probs(s, n, here):
            r = n % 2
            pe.wait_ge(*vs_in[r].at(s.turn, 32 * (n // 2) + 32))
            pe.wait_ge(*pn_done.at(s.turn, n + 1))
            if o_copied.any(s.turn, n):
                pe.wait_ge(*o_copied.at(s.turn, n))
            job, stage = here
            if stage == 1:
                pe.wait_ge(*dx_done.at(s.turn, job + 1))
            if stage in (2, 3, 4):
                pe.wait_ge(*gate_done.at(s.turn, 3 * job + stage - 1))
            for j in range(4):
                last = nc.tensor.transpose(TURN_BANK[:, P * j:P * j + P], pn[:, r, 2 * j:2 * j + 2, :].rearrange("p i k -> p (i k)"), C["ident"])
            last.then_inc(t_done.sem, 1)

        def values(s, n):
            r = n % 2
            pe.wait_ge(*pt_copied.at(s.turn, 2 * n + 2))
            for j in range(4):
                for odd in range(2):
                    for head in range(2):
                        rows = slice(64 * head, 64 * head + 64)
                        last = mm(TURN_BANK[rows, P * j:P * j + P].rearrange("p (h o q) -> p h o q", h=2, q=WIN)[:, :, odd, :],
                                  (vn if odd else vs)[:, r, j, rows], p_blocks[:, r, j, odd, head].rearrange("p h q -> p (h q)"),
                                  start=True, stop=True)
            last.then_inc(pv_done.sem, 1)

        def out_proj(s, n):
            b, pair = n // 8 % 2, n % 8
            if n >= 0:
                pe.wait_ge(*wo_in[pair // 4].at(s.turn, 16))
            pe.wait_ge(*o_copied.at(s.turn, n + 1))
            mm(OUT_BANK[b], wo[:, pair, :], oT[:, n % 2, :], start=(pair == 0), stop=(pair == 7)).then_inc(wo_step.sem, 1)

        def up(s, t, job, j):
            if j == 0:
                pe.wait_ge(*ffn_in.at(s.turn, 80 * (job + 1) if job < 1 else 80))
                pe.wait_ge(*xn_done.at(s.turn, job + 1))
                pe.wait_ge(*lnv_done.at(s.turn, job + 1))
            pe.wait_ge(*v_copied.at(s.turn, min(t + 1, UNITS) if s.last else t + 1))
            pe.wait_ge(*o_copied.at(s.turn, min(t, UNITS) if s.last else t))
            if act_done.any(s.turn, 3 * job + j):
                pe.wait_ge(*act_done.at(s.turn, 3 * job + j))
            mm(TURN_BANK[0:ROWS[j], :], w1[:, HID + P * j:HID + P * j + ROWS[j]], xn[:], start=True, stop=True)
            mm(V_BANK[0:ROWS[j], :], w1[:, P * j:P * j + ROWS[j]], xn[:], start=True, stop=True).then_inc(w1_done.sem, 1)

        def down(s, job, j):
            pe.wait_ge(*act_done.at(s.turn, 3 * job + j + 1))
            mm(OUT_BANK[job % 2], w2[0:ROWS[j], j, :], act[0:ROWS[j], j % 2, :], start=(j == 0), stop=(j == 2)).then_inc(w2_step.sem, 1)

        def body(s):
            for t in s.range:
                here, before = s.stage(t), s.stage(t - 1)
                job, stage = here
                if s.unit(t + 2):
                    project(s, t + 2, 0)
                    project(s, t + 2, 1)
                    head_norm(s, t + 2, 0)
                if stage == 1:
                    pe.wait_ge(*res1_done.at(s.turn, 2 * job + 2))
                    pe.wait_ge(*o_copied.at(s.turn, min(t, UNITS) if s.last else t))
                    mm(TURN_BANK, C["mean_ones"], Y[:, job % 2, 0:SEQ], start=True, stop=True).then_inc(mean_done.sem, 1)
                if stage in (3, 4, 5):
                    down(s, job, stage - 3)
                if stage in (2, 3, 4):
                    up(s, t, job, stage - 2)
                if t >= -1 and s.unit(t + 1):
                    scores(s, t + 1)
                if s.unit(t + 2):
                    head_norm(s, t + 2, 1)
                if s.unit(t) and t >= 0:
                    turn_probs(s, t, here)
                if t >= -1 and s.unit(t + 1):
                    project_v(s, t + 1, here, before)
                if s.unit(t - 1) and t - 1 >= -1:
                    out_proj(s, t - 1)
                if s.unit(t) and t >= 0:
                    values(s, t)
                if stage == 1:
                    pe.wait_ge(*dsq_done.at(s.turn, job + 1))
                    pe.wait_ge(*v_copied.at(s.turn, t + 2 if s.unit(t + 1) else UNITS))
                    mm(V_BANK, C["mean_ones"], dsq[:], start=True, stop=True).then_inc(var_done.sem, 1)

        pe.wait_ge(pads_zero.sem, 4)
        all_turns(pe, body)

    @block.scalar
    def _(ac):
        A = nc.scalar.activation

        def logarithm(s, n, which):
            i = 2 * n + which
            ac.wait_ge(*norm_done.at(s.turn, i + 1))
            if rope_done.any(s.turn, 3 * (n - 1) + 2 + which):
                ac.wait_ge(*rope_done.at(s.turn, 3 * (n - 1) + 2 + which))
            A(rn[:, which, :], NORM_BANK, ACT.Ln, bias=C["tiny"], scale=SS_SCALE).then_inc(ln_done.sem, 1)

        def root(s, n, which):
            ac.wait_ge(*ln_done.at(s.turn, 2 * n + which + 1))
            A(rn[:, which, :], rn[:, which, :], ACT.Exp, bias=C["ln_scale"], scale=-0.5).then_inc(r_done.sem, 1)

        def body(s):
            for t in s.range:
                job, stage = s.stage(t)
                if s.unit(t - 1) and t >= 0:
                    ac.wait_ge(*pv_done.at(s.turn, t))
                    if wo_step.any(s.turn, t - 2):
                        ac.wait_ge(*wo_step.at(s.turn, t - 2))
                    A(oT[:, (t - 1) % 2, :], TURN_BANK, ACT.Copy).then_inc(o_copied.sem, 1)
                if s.unit(t + 2):
                    for which in range(2):
                        ac.wait_ge(*qk_done.at(s.turn, 2 * (t + 2) + which + 1))
                        if norm_done.any(s.turn, 2 * (t + 1) + which + 1):
                            ac.wait_ge(*norm_done.at(s.turn, 2 * (t + 1) + which + 1))
                        A(sq[:, which, :], QK_BANK[which], ACT.Square).then_inc(sq_done.sem, 1)
                if s.unit(t + 2):
                    logarithm(s, t + 2, 0)
                    root(s, t + 2, 0)
                if stage in (2, 3, 4):
                    j = stage - 2
                    if j == 0:
                        ac.wait_ge(*ffn_in.at(s.turn, 80 * (job + 1) if job < 1 else 80))
                    ac.wait_ge(*w1_done.at(s.turn, 3 * job + j + 1))
                    if act_done.any(s.turn, 3 * job + j):
                        ac.wait_ge(*act_done.at(s.turn, 3 * job + j))
                    A(gate[0:ROWS[j], :], TURN_BANK[0:ROWS[j], :], ACT.Gelu, bias=ffn_param[0:ROWS[j], 5 + j:6 + j]).then_inc(gate_done.sem, 1)
                    nc.scalar.preload_act_table_set("natural_log_exp_and_others")
                if stage == 1:
                    ac.wait_ge(*dx_done.at(s.turn, job + 1))
                    if var_done.any(s.turn, job):
                        ac.wait_ge(*var_done.at(s.turn, job))
                    A(dsq[:], dx[:], ACT.Square).then_inc(dsq_done.sem, 1)
                if s.unit(t + 2):
                    logarithm(s, t + 2, 1)
                if s.unit(t) and t >= 0:
                    ac.wait_ge(*t_done.at(s.turn, t + 1))
                    if pv_done.any(s.turn, t - 1):
                        ac.wait_ge(*pv_done.at(s.turn, t - 1))
                    for half in range(2):
                        rows = slice(64 * half, 64 * half + 64)
                        A(p_blocks[rows, t % 2, :, :, :, half, :].rearrange("p j o h q -> p (j o h) q"),
                          TURN_BANK[rows, :].rearrange("p (n q) -> p n q", q=WIN), ACT.Copy).then_inc(pt_copied.sem, 1)
                if s.unit(t + 2):
                    root(s, t + 2, 1)
                if t >= -1 and s.unit(t + 1):
                    ac.wait_ge(*v_done.at(s.turn, t + 2))
                    if pv_done.any(s.turn, t):
                        ac.wait_ge(*pv_done.at(s.turn, t))
                    if vs_in[(t + 1) % 2].any(s.turn, 32 * ((t + 1) // 2)):
                        ac.wait_ge(*vs_in[(t + 1) % 2].at(s.turn, 32 * ((t + 1) // 2)))
                    A(vn[:, (t + 1) % 2], V_BANK.rearrange("p (j f) -> p j f", f=P), ACT.Copy).then_inc(v_copied.sem, 1)
                if t >= -1 and s.unit(t + 1):
                    ac.wait_ge(*sub_done.at(s.turn, t + 2))
                    A(prob[:, (t + 1) % 2], prob[:, (t + 1) % 2], ACT.Exp, scale=QK_SCALE).then_inc(exp_done.sem, 1)
                if stage == 1:
                    ac.wait_ge(*var_done.at(s.turn, job + 1))
                    if xh_done.any(s.turn, job):
                        ac.wait_ge(*xh_done.at(s.turn, job))
                    A(rstd[:], V_BANK, ACT.Ln, bias=C["eps"]).then_inc(lnv_done.sem, 1)
                    ac.wait_ge(*lnv_done.at(s.turn, job + 1))
                    A(rstd[:], rstd[:], ACT.Exp, scale=-0.5).then_inc(rstd_done.sem, 1)

        nc.scalar.preload_act_table_set("natural_log_exp_and_others")
        ac.wait_ge(pads_zero.sem, 4)
        all_turns(ac, body)

    @block.vector
    def _(dv):
        v = nc.vector

        def rotate(s, n, which):
            i, tab, b = 2 * n + which, 2 * which, n // 8 % 2
            if which == 0 and n % 8 == 0:
                dv.wait_ge(*scale_in[b].at(s.turn, 16 * (n // 16) + 16))
            dv.wait_ge(*sq_done.at(s.turn, i + 1))
            if add_done.any(s.turn, i - 1):
                dv.wait_ge(*add_done.at(s.turn, i - 1))
            if sin_done.any(s.turn, i - 1):
                dv.wait_ge(*sin_done.at(s.turn, i - 1))
            v.scalar_tensor_tensor(cos_part[:, which, :], QK_BANK[which], rope_scale[:, b, tab:tab + 1], table[:, tab, :],
                                   ALU.mult, ALU.mult).then_inc(cos_done.sem, 1)
            v.stream_shuffle(swapped[:, which, :], QK_BANK[which], HALF_SWAP).then_inc(swap_done.sem, 1)

        def rotate_sin(s, n, which):
            i, tab, b = 2 * n + which, 2 * which, n // 8 % 2
            dv.wait_ge(*swap_done.at(s.turn, i + 1))
            v.scalar_tensor_tensor(sin_part[:, which, :], swapped[:, which, :], rope_scale[:, b, tab + 1:tab + 2], table[:, tab + 1, :],
                                   ALU.mult, ALU.mult).then_inc(sin_done.sem, 1)

        def rope_last(s, n, which):
            r = n % 2
            dv.wait_ge(*add_done.at(s.turn, 2 * n + which + 1))
            dv.wait_ge(*r_done.at(s.turn, 2 * n + which + 1))
            if score_done.any(s.turn, n - 1):
                dv.wait_ge(*score_done.at(s.turn, n - 1))
            if which == 0:
                for head in range(2):
                    rows = slice(64 * head, 64 * head + 64)
                    v.scalar_tensor_tensor(q_blocks[rows, r, :, :, head, :].rearrange("p i o q -> p (i o) q"),
                                           rn[rows, 0, :].rearrange("p (w q) -> p w q", q=WIN), 1e12,
                                           turned[rows, 0, :].rearrange("p (w q) -> p w q", q=WIN), ALU.min, ALU.mult).then_inc(rope_done.sem, 1)
            else:
                v.scalar_tensor_tensor(kT[:, r, WIN:], rn[:, 1, :], 1e12, turned[:, 1, :], ALU.min, ALU.mult).then_inc(rope_done.sem, 1)

        def residual1(s, job):
            b = job % 2
            dv.wait_ge(*wo_step.at(s.turn, 8 * job + 8))
            for f in range(2):
                dst = Y[64 * f:64 * f + 64, b, f:f + SEQ]
                v.tensor_tensor(dst, OUT_BANK[b][64 * f:64 * f + 64, :], dst, ALU.add).then_inc(res1_done.sem, 1)

        def residual2(s, job):
            b = job % 2
            dv.wait_ge(*w2_step.at(s.turn, 3 * job + 3))
            for f in range(2):
                dst = Y[64 * f:64 * f + 64, b, f:f + SEQ]
                v.scalar_tensor_tensor(dst, OUT_BANK[b][64 * f:64 * f + 64, :], ffn_param[64 * f:64 * f + 64, 8:9], dst,
                                       ALU.add, ALU.add).then_inc(res2_done.sem, 1)

        def body(s):
            for t in s.range:
                job, stage = s.stage(t)
                if stage == 2:
                    dv.wait_ge(*ffn_in.at(s.turn, 80 * (job + 1) if job < 1 else 80))
                    dv.wait_ge(*rstd_done.at(s.turn, job + 1))
                    if w1_done.any(s.turn, 3 * job):
                        dv.wait_ge(*w1_done.at(s.turn, 3 * job))
                    v.tensor_tensor(xn[:], dx[:], rstd[:], ALU.mult).then_inc(xh_done.sem, 1)
                    dv.wait_ge(*xh_done.at(s.turn, job + 1))
                    v.tensor_scalar(xn[:], xn[:], ffn_param[:, 0:1], ffn_param[:, 1:2], ALU.mult, ALU.add).then_inc(xn_done.sem, 1)
                n = t + 2
                if s.unit(n):
                    rotate(s, n, 0)
                    rotate(s, n, 1)
                if stage == 1:
                    dv.wait_ge(*mean_done.at(s.turn, job + 1))
                    if xh_done.any(s.turn, job):
                        dv.wait_ge(*xh_done.at(s.turn, job))
                    if dsq_done.any(s.turn, job):
                        dv.wait_ge(*dsq_done.at(s.turn, job))
                    v.tensor_tensor(dx[:], Y[:, job % 2, 0:SEQ], TURN_BANK, ALU.subtract).then_inc(dx_done.sem, 1)
                if s.unit(n):
                    rotate_sin(s, n, 0)
                    rotate_sin(s, n, 1)
                if stage == 5:
                    residual2(s, job)
                if stage in (2, 3, 4):
                    j = stage - 2
                    rows = ROWS[j]
                    dv.wait_ge(*gate_done.at(s.turn, 3 * job + j + 1))
                    if w2_step.any(s.turn, 3 * job + j - 1):
                        dv.wait_ge(*w2_step.at(s.turn, 3 * job + j - 1))
                    v.scalar_tensor_tensor(act[0:rows, j % 2, :], V_BANK[0:rows, :], ffn_param[0:rows, 2 + j:3 + j], gate[0:rows, :],
                                           ALU.add, ALU.mult).then_inc(act_done.sem, 1)
                n = t + 1
                if t >= -1 and s.unit(n):
                    r = n % 2
                    bank = SCORE_BANK.rearrange("p (i k) -> p i k", k=64)
                    dv.wait_ge(*score_done.at(s.turn, n + 1))
                    if sub_done.any(s.turn, n - 1):
                        dv.wait_ge(*sub_done.at(s.turn, n - 1))
                    v.tensor_reduce(mx[:, r, :], bank, AX, ALU.max).then_inc(mx_done.sem, 1)
                    dv.wait_ge(*mx_done.at(s.turn, n + 1))
                    if pn_done.any(s.turn, n - 1):
                        dv.wait_ge(*pn_done.at(s.turn, n - 1))
                    if sum_done.any(s.turn, n - 1):
                        dv.wait_ge(*sum_done.at(s.turn, n - 1))
                    v.tensor_tensor(prob[:, r], bank, mx[:, r, :].unsqueeze(2).to_broadcast([P, 8, 64]), ALU.subtract).then_inc(sub_done.sem, 1)
                if s.unit(t + 2):
                    rope_last(s, t + 2, 0)
                    rope_last(s, t + 2, 1)
                if t >= -1 and s.unit(n):
                    dv.wait_ge(*exp_done.at(s.turn, n + 1))
                    if rec_done.any(s.turn, n - 1):
                        dv.wait_ge(*rec_done.at(s.turn, n - 1))
                    v.tensor_reduce(rs[:, r, :], prob[:, r], AX, ALU.add).then_inc(sum_done.sem, 1)
                    dv.wait_ge(*sum_done.at(s.turn, n + 1))
                    if pn_done.any(s.turn, n - 1):
                        dv.wait_ge(*pn_done.at(s.turn, n - 1))
                    v.reciprocal(ri[:, r, :], rs[:, r, :]).then_inc(rec_done.sem, 1)
                if stage == 0:
                    residual1(s, job)

        v.memset(kT[:, :, 0:WIN], 0.0).then_inc(pads_zero.sem, 1)
        v.memset(vs[0:32, :, 0, :], 0.0).then_inc(pads_zero.sem, 1)
        v.memset(q_blocks[:], 0.0).then_inc(pads_zero.sem, 1)
        v.memset(p_blocks[:], 0.0).then_inc(pads_zero.sem, 1)
        dv.wait_ge(pads_zero.sem, 4)
        dv.wait_ge(table_in.sem, 16)
        all_turns(dv, body)

    @block.gpsimd
    def _(pool):
        def body(s):
            for t in s.range:
                if s.unit(t) and t >= 0:
                    r = t % 2
                    pool.wait_ge(*rec_done.at(s.turn, t + 1))
                    if t_done.any(s.turn, t - 1):
                        pool.wait_ge(*t_done.at(s.turn, t - 1))
                    nc.gpsimd.tensor_tensor(pn[:, r], prob[:, r], ri[:, r, :].unsqueeze(2).to_broadcast([P, 8, 64]), ALU.mult).then_inc(pn_done.sem, 1)
                if s.unit(t + 2):
                    for which in range(2):
                        n = t + 2
                        pool.wait_ge(*sin_done.at(s.turn, 2 * n + which + 1))
                        if rope_done.any(s.turn, 3 * (n - 1) + 2 + which):
                            pool.wait_ge(*rope_done.at(s.turn, 3 * (n - 1) + 2 + which))
                        nc.gpsimd.tensor_tensor(turned[:, which, :], cos_part[:, which, :], sin_part[:, which, :], ALU.add).then_inc(add_done.sem, 1)

        all_turns(pool, body)


def build_last_norm(nc, ctx, x2, Y, out, C):
    def sb(name, shape, dt=F32):
        return ctx.enter_context(nc.sbuf_tensor("la_" + name, shape, dt))

    ps = C["psum"]
    total = sb("total", [P, 2, SEQ])
    centred = sb("centred", [P, 2, SEQ])
    ln = sb("ln", [P, 2, SEQ])
    res = sb("res", [P, 2, SEQ])
    sum_done = Flow(C["sems"].enter_context(nc.semaphore("la_sum_done")), 4)
    stored = Flow(C["sems"].enter_context(nc.semaphore("la_stored")), 32)
    s = C["norm"](2)

    def rows(b):
        return ps[:, b, :], ps[:, 2 + b, :]

    block = ctx.enter_context(nc.Block())

    @block.sync
    def _(sp):
        for b in range(2):
            sp.wait_ge(*s["scaled"].at(s["use"], b + 1))
            sp.dma_start(out[:, b, :], res[:, b, :]).then_inc(stored.sem, 16)
        sp.wait_ge(stored.sem, 32)

    @block.tensor
    def _(pe):
        for b in range(2):
            pe.wait_ge(sum_done.sem, 2 * b + 2)
            normalise(nc, "pe_mean", pe, s, b, total[:, b, :], None, (None, None), rows(b), C)
        for b in range(2):
            normalise(nc, "pe_var", pe, s, b, None, None, (centred, ln), rows(b), C)

    @block.scalar
    def _(ac):
        nc.scalar.preload_act_table_set("natural_log_exp_and_others")
        for b in range(2):
            normalise(nc, "act_square", ac, s, b, None, None, (centred, ln), None, C)
        for b in range(2):
            normalise(nc, "act_rstd", ac, s, b, None, None, (centred, ln), rows(b), C)

    @block.vector
    def _(dv):
        for b in range(2):
            for f in range(2):
                half = slice(64 * f, 64 * f + 64)
                nc.vector.tensor_tensor(total[half, b, :], Y[half, b, f:f + SEQ], x2[half, b, :], ALU.add).then_inc(sum_done.sem, 1)
        dv.wait_ge(sum_done.sem, 4)
        for b in range(2):
            normalise(nc, "dve_centre", dv, s, b, total[:, b, :], None, (centred, ln), rows(b), C)
        for b in range(2):
            normalise(nc, "dve_scale", dv, s, b, None, res[:, b, :], (centred, ln), None, C)


def program(nc, d, out, probes=None):
    d = {**d, "line": nc.dram_tensor("bias_line", (HEADS, SPAN), F32).ap(),
         "gates": nc.dram_tensor("gate_rows", (EXPERTS, BATCH, SEQ), F32).ap()}
    with ExitStack() as ctx:
        def sb(name, shape, dt=F32):
            return ctx.enter_context(nc.sbuf_tensor(name, shape, dt))

        C = {"sems": ctx, "psum": ctx.enter_context(nc.psum_tensor("banks", [P, 8, 512], F32))}
        Y = sb("stream", [P, 2, SEQ + 1])
        x2 = sb("x2", [P, 2, SEQ])
        steps = norm_steps(nc, ctx)
        C["norm"] = lambda use: {**steps, "use": use}
        consts = dict(ident=sb("ident", [P, P]), ident16=sb("ident16", [P, P], BF16), mask16=sb("mask16", [P, SEQ], BF16),
                      head_ones=sb("head_ones", [P, P]), mean_ones=sb("mean_ones", [P, P]))
        for name, t in consts.items():
            C[name] = t[:]
        fill = sb("fill", [P, 4])
        FILL = (("tiny", 2.0 ** -64), ("eps", 1e-5), ("ln_scale", float(0.5 * np.log(SS_SCALE))), ("one", 1.0))
        for i, (name, _) in enumerate(FILL):
            C[name] = fill[:, i:i + 1]
        C["const_in"] = Flow(C["sems"].enter_context(nc.semaphore("const_in")), 0)
        C["fill"] = Flow(C["sems"].enter_context(nc.semaphore("fill_done")), 0)
        C["const_n"], C["fill_n"] = 16 * (len(consts) + 1), len(FILL)
        probed = ctx.enter_context(nc.semaphore("probed"))

        def probe(name, t, n):
            if probes:
                with nc.Block() as block:
                    @block.sync
                    def _(sp):
                        sp.dma_start(probes[name], t[:]).then_inc(probed, 16)
                        sp.wait_ge(probed, 16 * n)

        with ExitStack() as front:
            x = front.enter_context(nc.sbuf_tensor("x", [P, 2, SEQ], F32))
            h1 = front.enter_context(nc.sbuf_tensor("h1", [P, 2, SEQ], F32))
            x1 = front.enter_context(nc.sbuf_tensor("x1", [P, 2, SEQ], F32))
            weights = ExpertWeights(nc, front, C)
            with nc.Block() as block:
                @block.sync
                def _(sp):
                    sp.dma_start(x[:], d["x"]).then_inc(C["const_in"].sem, 16)
                    for name in consts:
                        sp.dma_start(C[name], d["c_" + name]).then_inc(C["const_in"].sem, 16)

                @block.scalar
                def _(ac):
                    ac.wait_ge(C["const_in"].sem, C["const_n"])

                @block.vector
                def _(dv):
                    for i, (_, value) in enumerate(FILL):
                        nc.vector.memset(fill[:, i:i + 1], value).then_inc(C["fill"].sem, 1)
            with ExitStack() as part:
                build_mamba(nc, part, x, h1, weights, d, C)
            probe("h1", h1, 1)
            with ExitStack() as part:
                build_moe(nc, part, x, h1, x1, weights, d, C)
            probe("x1", x1, 2)
            with ExitStack() as part:
                build_cross(nc, part, x1, x2, d, C)
            probe("x2", x2, 3)
        placed = ctx.enter_context(nc.semaphore("placed"))
        with nc.Block() as block:
            @block.vector
            def _(dv):
                nc.vector.memset(Y[64:128, :, 0:1], 0.0).then_inc(placed, 1)
                nc.vector.tensor_copy(Y[0:64, :, 0:SEQ], x2[0:64]).then_inc(placed, 1)
                nc.vector.tensor_copy(Y[64:128, :, 1:], x2[64:128]).then_inc(placed, 1)
        with ExitStack() as part:
            build_stack(nc, part, Y, d, C)
        with ExitStack() as part:
            build_last_norm(nc, part, x2, Y, out, C)


def head_rows():
    return [*range(0, 16), *range(32, 48), *range(16, 32), *range(48, 64)]

def stack_constants():
    half = np.arange(0, DH, 2, dtype=np.float32)
    inv_freq = (1.0 / np.float32(10000.0) ** (half / np.float32(DH))).astype(np.float32)
    t = np.arange(SEQ, dtype=np.float32)
    fr = t[:, None] * inv_freq[None, :]
    fr = np.concatenate([fr, fr], -1)
    bs = (half + np.float32(0.4 * DH)) / np.float32(1.4 * DH)
    power = (t - SEQ // 2) / np.float32(WIN // 2)
    sc = (bs[None, :] ** power[:, None]).astype(np.float32)
    sc = np.concatenate([sc, sc], -1)
    sign = np.where(np.arange(DH) < DH // 2, -1.0, 1.0).astype(np.float32)
    cos, sin = np.cos(fr), np.sin(fr) * sign
    rows = head_rows() * 1
    tabs = [cos * sc, sin * sc, cos / sc, sin / sc]
    rope = np.stack([np.tile(x[:, rows].T, (2, 1)) for x in tabs], 1).astype(np.float32)
    i = np.arange(32)[:, None]; j = np.arange(64)[None, :]
    ok = (j >= i) & (j <= i + 32)
    mask = np.tile(np.where(ok, 0.0, -1e30), (4, 8))
    mask[0:64, 0:32] = -1e30
    mask = mask.astype(np.dtype("bfloat16"))
    ho = np.kron(np.eye(2), np.ones((64, 64))).astype(np.float32)
    return dict(rope=rope, c_mask16=mask, c_ident=np.eye(128, dtype=np.float32), c_ident16=np.eye(128).astype(np.dtype("bfloat16")),
                c_head_ones=ho, c_mean_ones=np.full((128, 128), 1 / 128, np.float32))

def stack_inputs(Wqkv, q_scale, k_scale, Wo, ln_g, ln_b, W1, b1, W2, b2):
    rows = np.array(head_rows())
    partner = (rows + 32) % 64
    L = Wqkv.shape[0]
    w = Wqkv.reshape(L, 128, 3, 16, 64)
    pairs = lambda t: t.reshape(L, 128, 8, 128)
    w_proj = np.concatenate([pairs(w[:, :, 0][..., rows]), pairs(w[:, :, 1][..., rows]), pairs(w[:, :, 2])], -1)
    rs = np.stack([np.tile(x, (1, 2)) for x in (q_scale[:, rows], q_scale[:, partner], k_scale[:, rows], k_scale[:, partner])], -1)
    wo = np.ascontiguousarray(Wo.reshape(L, 8, 128, 128).transpose(0, 2, 1, 3))
    def cols(v):
        o = np.zeros((L, 384), v.dtype); o[:, :HID] = v
        return list(o.reshape(L, 3, 128).transpose(1, 0, 2))
    prm = np.stack([ln_g, ln_b, *cols(b1[:, :HID]), *cols(b1[:, HID:]), b2], -1)
    return dict(w_proj=w_proj, rope_scale=np.ascontiguousarray(rs), wo=wo, w1=W1, w2=W2, ffn_param=np.ascontiguousarray(prm))

def front_inputs(i):
    A = lambda n: i['L0_attn_' + n]
    blocks = lambda v: np.stack([v[0:128], v[128:256]], 1)
    xproj = A('x_proj_w')
    o = {}
    o['x'] = np.ascontiguousarray(i['x'].transpose(2, 0, 1))
    o['rms1'] = A('rms1_w')[:, None]; o['rms2'] = A('rms2_w')[:, None]
    o['in_w'] = A('in_proj_w').reshape(128, 4, 128)
    o['xdt_w'] = blocks(xproj[:, 0:64])
    o['xbc_w'] = np.tile(blocks(xproj[:, 64:96]), (1, 1, 3))
    o['dt_w'] = A('dt_proj_w').reshape(64, 2, 128)
    o['out_w'] = blocks(A('out_proj_w'))
    chan = np.concatenate([A('conv_w')[:, 0, :], A('conv_b')[:, None], A('dt_proj_b')[:, None], A('D_skip')[:, None]], 1)
    o['chan'] = blocks(chan)
    o['a_log'] = blocks(A('A_log'))
    o['router'] = A('router_w')
    o['wg'] = A('Wg'); o['wu'] = A('Wu')
    o['wd'] = A('Wd').reshape(8, 4, 128, 128).transpose(0, 2, 1, 3)
    o['xwq'] = i['L0_xattn_Wq']; o['xwk'] = i['L0_xattn_Wkv'][:, :128]; o['xwv'] = i['L0_xattn_Wkv'][:, 128:]
    o['xwo'] = i['L0_xattn_Wo']; o['rel'] = i['L0_xattn_rel_bias']
    o['ctxT'] = np.tile(i['ctx_1024'][:, ::-1].transpose(2, 0, 1)[:, :, None, :], (1, 1, 4, 1))
    return {k: np.ascontiguousarray(v) for k, v in o.items()}

def buckets(rel):
    nb = 16
    out = (rel > 0).astype(np.int32) * nb
    rel = np.abs(rel)
    me = nb // 2
    rf = np.maximum(rel, 1).astype(np.float32)
    large = me + (np.log(rf / np.float32(me)) / np.float32(np.log(128 / me)) * np.float32(nb - me)).astype(np.int32)
    large = np.minimum(large, nb - 1)
    return out + np.where(rel < me, rel, large)

def front_constants():
    sel = np.zeros((96, 32, 128), np.float32)
    for p in range(96): sel[p, p % 32] = 1
    order = np.broadcast_to(np.arange(8, 0, -1, dtype=np.float32), (128, 8, 8))
    b = buckets(31 - np.arange(544))
    oh = (np.arange(32)[:, None] == b[None]).astype(np.float32)
    ho = np.kron(np.eye(16), np.ones((8, 1))).astype(np.float32)
    qu = np.zeros((128, 16), np.float32)
    for p in range(128):
        qu[p, [h for h in range(16) if h % 4 == p // 32]] = 1
    return dict(select=sel.astype(np.dtype("bfloat16")), order=np.ascontiguousarray(order), onehot=oh, head_of=ho, quarter=qu)


def laid_out(inputs):
    stack = {name[len("L0_ffn_"):]: a for name, a in inputs.items() if name.startswith("L0_ffn_")}
    return {**stack_inputs(**stack), **front_inputs(inputs)}


def shape_constants():
    return {**stack_constants(), **front_constants()}


def kernel(**inputs):
    import concourse.bacc as _bacc
    from concourse.bass_utils import run_bass_kernel_spmd as _run

    inputs = {name: np.asarray(a) for name, a in inputs.items()}
    arrays = {"in_" + name: np.ascontiguousarray(a) for name, a in {**laid_out(inputs), **shape_constants()}.items()}
    nc = _bacc.Bacc("TRN2", target_bir_lowering=False, num_devices=1)
    d = {name[3:]: nc.dram_tensor(name, a.shape, mybir.dt.from_np(a.dtype), kind="ExternalInput").ap() for name, a in arrays.items()}
    out = nc.dram_tensor("out", (P, BATCH, SEQ), F32, kind="ExternalOutput").ap()
    program(nc, d, out)
    got = _run(nc, [arrays], core_ids=[0]).results[0]["out"]
    return np.ascontiguousarray(got.transpose(1, 2, 0))
```

```python
import numpy as np
import concourse.bass as bass
from concourse import mybir
from contextlib import ExitStack

F32 = mybir.dt.float32
F32R = mybir.dt.float32r
BF16 = mybir.dt.bfloat16
ACT = mybir.ActivationFunctionType
ALU = mybir.AluOpType
AX = mybir.AxisListType.X

P = 128
BATCH = 2
SEQ = 512
DIM = 128
LAYERS = 6
HEADS = 16
DH = 64
WIN = 32
DT_RANK = 64
STATES = 16
EXPERTS = 8
KEYS = 32
BUCKETS = 32
SPAN = SEQ + KEYS
HID = int(DIM * 4 * 2 / 3)
QK_SCALE = 8.0
SS_SCALE = 65536.0
HALF_SWAP = [(i + 16) % 32 for i in range(32)]


class Flow:

    def __init__(self, sem, per):
        self.sem = sem
        self.per = per

    def at(self, turn, n):
        return self.sem, turn * self.per + n

    def any(self, turn, n):
        return not isinstance(turn, int) or turn * self.per + n > 0


def at_layer(ap, turn):
    one = ap[bass.ds(turn, 1)]
    return one.rearrange("o p n -> (o p) n" if len(ap.shape) == 3 else "o p m n -> (o p) m n")


def expert(ap, turn, e):
    one = ap[bass.ds(turn * 2 + e, 1)]
    return one.rearrange("o p n -> (o p) n" if len(ap.shape) == 3 else "o p m n -> (o p) m n")


def norm_steps(nc, ctx):
    return {what: Flow(ctx.enter_context(nc.semaphore(f"norm_{what}")), 2)
            for what in ("mean", "centred", "square", "var", "ln", "rstd", "scaled")}


def rms_steps(nc, ctx):
    return [Flow(ctx.enter_context(nc.semaphore(f"rms_{what}")), 2) for what in ("square", "mean", "ln", "rstd", "scaled")]


def build_mamba(nc, ctx, x, h1, weights, d, C):
    def sb(name, shape, dt=F32):
        return ctx.enter_context(nc.sbuf_tensor("ma_" + name, shape, dt))

    def flow(name, per=0):
        return Flow(C["sems"].enter_context(nc.semaphore("ma_" + name)), per)

    ps = C["psum"]
    in_w = sb("in_w", [P, 4, P])
    xdt_w = sb("xdt_w", [P, 2, DT_RANK])
    xbc_w = sb("xbc_w", [P, 2, 96])
    dt_w = sb("dt_w", [DT_RANK, 2, P])
    out_w = sb("out_w", [P, 2, P])
    chan = sb("chan", [P, 2, 7])
    a_log = sb("a_log", [P, 2, STATES])
    rms_w = sb("rms_w", [P, 1])
    select = sb("select", [96, 2 * STATES, P], BF16)
    xsq = sb("xsq", [P, 2, SEQ])
    rn = sb("rn", [P, 2, SEQ])
    hn = sb("hn", [P, 2, SEQ])
    xi = sb("xi", [P, 2, 2, 3 + SEQ])
    sz = sb("sz", [P, 2, 2, SEQ])
    conv = sb("conv", [P, 2, 2, 2, SEQ])
    xc = sb("xc", [P, 2, 2, SEQ])
    dt = sb("dt", [DT_RANK, 2, SEQ])
    part = sb("part", [96, 3, 2, SEQ], BF16)
    rest = sb("rest", [96, 3, 2, SEQ])
    bc3 = sb("bc3", [96, 2, SEQ], BF16)
    pre = sb("pre", [P, 2, 2, SEQ])
    mag = sb("mag", [P, 2, 2, SEQ])
    delta = sb("delta", [P, 2, 2, SEQ])
    u = sb("u", [P, 2, 2, SEQ])
    a_neg = sb("a_neg", [P, 2, STATES])
    decay = conv.rearrange("p i k b t -> p (i k) b t")
    bc = sb("bc", [P, 4, 2, SEQ])
    dbx = sb("dbx", [P, 4, SEQ])
    state = sb("state", [P, 3, SEQ])
    hc = sb("hc", [P, 4, SEQ])

    loaded, loaded2 = flow("loaded"), flow("loaded2")
    pads = flow("pads")
    xsq_done, ms_done, ln_done, r_done, hn_done = C["rms"]
    in_done, in_copied = flow("in_done"), flow("in_copied")
    conv_done, xc_done = flow("conv_done"), flow("xc_done")
    proj_done, dt_copied, split_done = flow("proj_done"), flow("dt_copied"), flow("split_done")
    dtp_done, pre_done, mag_done, sp_exp, sp_ln, delta_done, u_done = (flow(n) for n in (
        "dtp_done", "pre_done", "mag_done", "sp_exp", "sp_ln", "delta_done", "u_done"))
    aexp_done, aneg_done = flow("aexp_done"), flow("aneg_done")
    bc_done, bc_copied, decay_done, dbx_done, scan_done, hc_done, sum_done = (flow(n) for n in (
        "bc_done", "bc_copied", "decay_done", "dbx_done", "scan_done", "hc_done", "sum_done"))
    skip_done, gated_done, out_done, h1_done = flow("skip_done"), flow("gated_done"), flow("out_done"), flow("h1_done")

    block = ctx.enter_context(nc.Block())
    STEPS = [(k, b) for k in range(2) for b in range(2)]

    @block.sync
    def _(sp):
        sp.dma_start(rms_w[:], d["rms1"]).then_inc(loaded.sem, 16)
        sp.dma_start(in_w[:], d["in_w"]).then_inc(loaded.sem, 16)
        for dst, src in ((chan, "chan"), (a_log, "a_log"), (xdt_w, "xdt_w"), (xbc_w, "xbc_w"), (dt_w, "dt_w"), (out_w, "out_w"), (select, "select")):
            sp.dma_start(dst[:], d[src]).then_inc(loaded2.sem, 16)
        for e in range(2):
            weights.load(sp, d, 0, e)

    @block.tensor
    def _(pe):
        pe.wait_ge(C["const_in"].sem, C["const_n"])
        for b in range(2):
            pe.wait_ge(*xsq_done.at(0, b + 1))
            nc.tensor.matmul(ps[:, b, :], C["mean_ones"], xsq[:, b, :], start=True, stop=True).then_inc(ms_done.sem, 1)
        pe.wait_ge(loaded.sem, 32)
        for b in range(2):
            pe.wait_ge(*hn_done.at(0, b + 1))
            for m in range(4):
                nc.tensor.matmul(ps[:, (2 + 4 * b + m) % 8, :], in_w[:, m, :], hn[:, b, :], start=True, stop=True).then_inc(in_done.sem, 1)
        pe.wait_ge(loaded2.sem, 112)
        pe.wait_ge(in_copied.sem, 8)
        for b in range(2):
            pe.wait_ge(xc_done.sem, 2 + b + 1)
            for k in range(2):
                nc.tensor.matmul(ps[0:DT_RANK, b, :], xdt_w[:, k, :], xc[:, k, b, :], start=(k == 0), stop=(k == 1))
            for k in range(2):
                last = nc.tensor.matmul(ps[0:96, 2 + b, :], xbc_w[:, k, :], xc[:, k, b, :], start=(k == 0), stop=(k == 1))
            last.then_inc(proj_done.sem, 1)
        for n, (k, b) in enumerate(STEPS):
            pe.wait_ge(dt_copied.sem, b + 1)
            nc.tensor.matmul(ps[:, 4 + n, :], dt_w[:, k, :], dt[:, b, :], start=True, stop=True).then_inc(dtp_done.sem, 1)

        def broadcast(i):
            n, b = divmod(i, 2)
            if i - 1 > 0:
                pe.wait_ge(bc_copied.sem, i - 1)
            for s in range(2):
                last = nc.tensor.matmul(ps[:, 4 + 2 * (i % 2) + s, :], select[:, STATES * s + n, :], bc3[:, b, :], start=True, stop=True)
            last.then_inc(bc_done.sem, 1)

        pe.wait_ge(split_done.sem, 2)
        pe.wait_ge(mag_done.sem, 4)
        broadcast(0)
        broadcast(1)
        pe.wait_ge(dt_copied.sem, 2)
        broadcast(2)
        for i in range(2 * STATES):
            n, b = divmod(i, 2)
            if i + 3 < 2 * STATES:
                broadcast(i + 3)
            for k in range(2):
                j = 2 * i + k
                pe.wait_ge(hc_done.sem, j + 1)
                nc.tensor.matmul(ps[:, 2 * k + b, :], C["ident"], hc[:, j % 4, :], start=(n == 0), stop=(n == STATES - 1)).then_inc(sum_done.sem, 1)
        for b in range(2):
            pe.wait_ge(gated_done.sem, 2 * b + 2)
            for k in range(2):
                last = nc.tensor.matmul(ps[:, 4 + b, :], out_w[:, k, :], xc[:, k, b, :], start=(k == 0), stop=(k == 1))
            last.then_inc(out_done.sem, 1)

    @block.scalar
    def _(ac):
        A = nc.scalar.activation
        nc.scalar.preload_act_table_set("natural_log_exp_and_others")
        ac.wait_ge(C["const_in"].sem, C["const_n"])
        ac.wait_ge(C["fill"].sem, C["fill_n"])
        for b in range(2):
            A(xsq[:, b, :], x[:, b, :], ACT.Square).then_inc(xsq_done.sem, 1)
        for b in range(2):
            ac.wait_ge(*ms_done.at(0, b + 1))
            A(rn[:, b, :], ps[:, b, :], ACT.Ln, bias=C["eps"]).then_inc(ln_done.sem, 1)
            ac.wait_ge(*ln_done.at(0, b + 1))
            A(rn[:, b, :], rn[:, b, :], ACT.Exp, scale=-0.5).then_inc(r_done.sem, 1)
        for b in range(2):
            for m in range(2):
                ac.wait_ge(in_done.sem, 4 * b + m + 1)
                A(xi[:, m, b, 3:], ps[:, (2 + 4 * b + m) % 8, :], ACT.Copy).then_inc(in_copied.sem, 1)
        for b in range(2):
            for m in range(2, 4):
                ac.wait_ge(in_done.sem, 4 * b + m + 1)
                A(sz[:, m - 2, b, :], ps[:, (2 + 4 * b + m) % 8, :], ACT.Silu).then_inc(in_copied.sem, 1)
        for b in range(2):
            for k in range(2):
                ac.wait_ge(conv_done.sem, 8 * b + 4 * k + 4)
                A(xc[:, k, b, :], conv[:, 1, k, b, :], ACT.Silu, bias=chan[:, k, 4:5]).then_inc(xc_done.sem, 1)
        nc.scalar.preload_act_table_set("natural_log_exp_and_others")
        A(a_neg[:], a_log[:], ACT.Exp).then_inc(aexp_done.sem, 1)
        for b in range(2):
            ac.wait_ge(proj_done.sem, b + 1)
            A(dt[:, b, :], ps[0:DT_RANK, b, :], ACT.Copy).then_inc(dt_copied.sem, 1)
        for n, (k, b) in enumerate(STEPS):
            ac.wait_ge(mag_done.sem, n + 1)
            A(mag[:, k, b, :], mag[:, k, b, :], ACT.Exp).then_inc(sp_exp.sem, 1)
        for n, (k, b) in enumerate(STEPS):
            ac.wait_ge(sp_exp.sem, n + 1)
            A(mag[:, k, b, :], mag[:, k, b, :], ACT.Ln, bias=C["one"]).then_inc(sp_ln.sem, 1)

        def copy_bc(i):
            ac.wait_ge(bc_done.sem, i + 1)
            if 2 * (i - 3) > 0:
                ac.wait_ge(hc_done.sem, 2 * (i - 3))
            A(bc[:, i % 4], ps[:, 4 + 2 * (i % 2):6 + 2 * (i % 2), :], ACT.Copy).then_inc(bc_copied.sem, 1)

        copy_bc(0)
        copy_bc(1)
        ac.wait_ge(aneg_done.sem, 1)
        ac.wait_ge(delta_done.sem, 4)
        ac.wait_ge(xc_done.sem, 4)
        for n in range(STATES):
            for k in range(2):
                if 4 * (n - 1) > 0:
                    ac.wait_ge(scan_done.sem, 4 * (n - 1))
                A(decay[:, 2 * (n % 2) + k], delta[:, k], ACT.Exp, scale=a_neg[:, k, n:n + 1]).then_inc(decay_done.sem, 1)
            for k in range(2):
                if 2 * n + k + 2 < 2 * STATES:
                    copy_bc(2 * n + k + 2)

    @block.vector
    def _(dv):
        v = nc.vector
        v.memset(xi[:, :, :, 0:3], 0.0).then_inc(pads.sem, 1)
        dv.wait_ge(C["const_in"].sem, C["const_n"])
        dv.wait_ge(loaded.sem, 32)
        for b in range(2):
            dv.wait_ge(*r_done.at(0, b + 1))
            v.scalar_tensor_tensor(hn[:, b, :], x[:, b, :], rms_w[:, 0:1], rn[:, b, :], ALU.mult, ALU.mult).then_inc(hn_done.sem, 1)
        dv.wait_ge(loaded2.sem, 112)
        dv.wait_ge(pads.sem, 1)
        for b in range(2):
            for k in range(2):
                dv.wait_ge(in_copied.sem, 2 * b + k + 1)
                v.tensor_scalar(conv[:, 0, k, b, :], xi[:, k, b, 0:SEQ], chan[:, k, 0:1], None, ALU.mult).then_inc(conv_done.sem, 1)
                for i in range(1, 4):
                    dv.wait_ge(conv_done.sem, 8 * b + 4 * k + i)
                    v.scalar_tensor_tensor(conv[:, i % 2, k, b, :], xi[:, k, b, i:i + SEQ], chan[:, k, i:i + 1],
                                           conv[:, (i + 1) % 2, k, b, :], ALU.mult, ALU.add).then_inc(conv_done.sem, 1)
        dv.wait_ge(aexp_done.sem, 1)
        v.tensor_scalar(a_neg[:], a_neg[:], -1.0, None, ALU.mult).then_inc(aneg_done.sem, 1)
        step = flow("split_step")
        at = 0
        for b in range(2):
            dv.wait_ge(proj_done.sem, b + 1)
            v.tensor_copy(rest[:, 0, b, :], ps[0:96, 2 + b, :]).then_inc(step.sem, 1)
            for i in range(3):
                at += 1
                dv.wait_ge(step.sem, at)
                v.tensor_copy(part[:, i, b, :], rest[:, i, b, :]).then_inc(step.sem, 1)
                at += 1
                dv.wait_ge(step.sem, at)
                if i < 2:
                    v.tensor_tensor(rest[:, i + 1, b, :], rest[:, i, b, :], part[:, i, b, :], ALU.subtract).then_inc(step.sem, 1)
            for i in range(3):
                last = v.tensor_copy(bc3[32 * i:32 * i + 32, b, :], part[32 * i:32 * i + 32, i, b, :])
            last.then_inc(split_done.sem, 1)
        for n, (k, b) in enumerate(STEPS):
            dv.wait_ge(dtp_done.sem, n + 1)
            v.tensor_scalar(pre[:, k, b, :], ps[:, 4 + n, :], chan[:, k, 5:6], None, ALU.add).then_inc(pre_done.sem, 1)
            dv.wait_ge(pre_done.sem, n + 1)
            v.scalar_tensor_tensor(mag[:, k, b, :], pre[:, k, b, :], -1.0, pre[:, k, b, :], ALU.mult, ALU.min).then_inc(mag_done.sem, 1)
        for n, (k, b) in enumerate(STEPS):
            dv.wait_ge(sp_ln.sem, n + 1)
            v.scalar_tensor_tensor(delta[:, k, b, :], pre[:, k, b, :], 0.0, mag[:, k, b, :], ALU.max, ALU.add).then_inc(delta_done.sem, 1)
            dv.wait_ge(delta_done.sem, n + 1)
            dv.wait_ge(xc_done.sem, 4)
            v.tensor_tensor(u[:, k, b, :], delta[:, k, b, :], xc[:, k, b, :], ALU.mult).then_inc(u_done.sem, 1)

        def times_c(j):
            dv.wait_ge(scan_done.sem, j + 1)
            if j - 3 > 0:
                dv.wait_ge(sum_done.sem, j - 3)
            v.tensor_tensor(hc[:, j % 4, :], state[:, j % 3, :], bc[:, j // 2 % 4, 1, :], ALU.mult).then_inc(hc_done.sem, 1)

        for j in range(4 * STATES):
            n, b, k = j // 4, j // 2 % 2, j % 2
            dv.wait_ge(dbx_done.sem, j + 1)
            dv.wait_ge(decay_done.sem, 2 * n + k + 1)
            if j - 2 > 0:
                dv.wait_ge(hc_done.sem, j - 2)
            v.tensor_tensor_scan(state[:, j % 3, :], decay[:, 2 * (n % 2) + k, b, :], dbx[:, j % 4, :], 0.0, ALU.mult, ALU.add).then_inc(scan_done.sem, 1)
            if j >= 1:
                times_c(j - 1)
        times_c(4 * STATES - 1)
        for n, (b, k) in enumerate(STEPS):
            dv.wait_ge(sum_done.sem, 4 * STATES)
            v.scalar_tensor_tensor(u[:, k, b, :], xc[:, k, b, :], chan[:, k, 6:7], ps[:, 2 * k + b, :], ALU.mult, ALU.add).then_inc(skip_done.sem, 1)
            dv.wait_ge(skip_done.sem, n + 1)
            dv.wait_ge(in_copied.sem, 8)
            v.tensor_tensor(xc[:, k, b, :], u[:, k, b, :], sz[:, k, b, :], ALU.mult).then_inc(gated_done.sem, 1)
        for b in range(2):
            dv.wait_ge(out_done.sem, b + 1)
            v.tensor_tensor(h1[:, b, :], ps[:, 4 + b, :], x[:, b, :], ALU.add).then_inc(h1_done.sem, 1)
        dv.wait_ge(h1_done.sem, 2)

    @block.gpsimd
    def _(pool):
        pool.wait_ge(u_done.sem, 4)
        for j in range(4 * STATES):
            i, b, k = j // 2, j // 2 % 2, j % 2
            pool.wait_ge(bc_copied.sem, i + 1)
            if j - 3 > 0:
                pool.wait_ge(scan_done.sem, j - 3)
            nc.gpsimd.tensor_tensor(dbx[:, j % 4, :], u[:, k, b, :], bc[:, i % 4, 0, :], ALU.mult).then_inc(dbx_done.sem, 1)


def normalise(nc, who, eng, s, b, src, dst, work, rows, C):
    centred, ln = work
    if who == "pe_mean":
        nc.tensor.matmul(rows[0], C["mean_ones"], src, start=True, stop=True).then_inc(s["mean"].sem, 1)
    elif who == "dve_centre":
        eng.wait_ge(*s["mean"].at(s["use"], b + 1))
        nc.vector.tensor_tensor(centred[:, b, :], src, rows[0], ALU.subtract).then_inc(s["centred"].sem, 1)
    elif who == "act_square":
        eng.wait_ge(*s["centred"].at(s["use"], b + 1))
        nc.scalar.activation(ln[:, b, :], centred[:, b, :], ACT.Square).then_inc(s["square"].sem, 1)
    elif who == "pe_var":
        eng.wait_ge(*s["square"].at(s["use"], b + 1))
        nc.tensor.matmul(rows[1], C["mean_ones"], ln[:, b, :], start=True, stop=True).then_inc(s["var"].sem, 1)
    elif who == "act_rstd":
        eng.wait_ge(*s["var"].at(s["use"], b + 1))
        nc.scalar.activation(ln[:, b, :], rows[1], ACT.Ln, bias=C["eps"]).then_inc(s["ln"].sem, 1)
        eng.wait_ge(*s["ln"].at(s["use"], b + 1))
        nc.scalar.activation(ln[:, b, :], ln[:, b, :], ACT.Exp, scale=-0.5).then_inc(s["rstd"].sem, 1)
    elif who == "dve_scale":
        eng.wait_ge(*s["rstd"].at(s["use"], b + 1))
        nc.vector.tensor_tensor(dst, centred[:, b, :], ln[:, b, :], ALU.mult).then_inc(s["scaled"].sem, 1)


GATE, UP, DOWN = range(3)


class ExpertWeights:

    def __init__(self, nc, ctx, C):
        def sb(name, shape):
            return ctx.enter_context(nc.sbuf_tensor("mo_" + name, shape, F32))

        self.all = sb("w", [P, 2, 3, 4 * P])
        self.loaded = [Flow(C["sems"].enter_context(nc.semaphore(f"mo_weights_{i}")), 48) for i in range(2)]

    def load(self, sp, d, turn, e):
        sp.dma_start(self.all[:, e, GATE, :], expert(d["wg"], turn, e)).then_inc(self.loaded[e].sem, 16)
        sp.dma_start(self.all[:, e, UP, :], expert(d["wu"], turn, e)).then_inc(self.loaded[e].sem, 16)
        sp.dma_start(self.all[:, e, DOWN, :].rearrange("p (j d) -> p j d", j=4), expert(d["wd"], turn, e)).then_inc(self.loaded[e].sem, 16)


def build_moe(nc, ctx, x, h1, x1, weights, cross, d, C):
    def sb(name, shape, dt=F32):
        return ctx.enter_context(nc.sbuf_tensor("mo_" + name, shape, dt))

    def flow(name, per=0):
        return Flow(C["sems"].enter_context(nc.semaphore("mo_" + name)), per)

    ps = C["psum"]
    rms_w = sb("rms_w", [P, 1])
    router = sb("router", [P, EXPERTS])
    order = sb("order", [P, 8, EXPERTS])
    hsq = sb("hsq", [P, 2, SEQ])
    rn = sb("rn", [P, 2, SEQ])
    hn = sb("hn", [P, 2, SEQ])
    G = [sb(f"gate{i}", [P, 8, EXPERTS]) for i in range(7)]
    col = sb("col", [P, 8, 6])
    wT = sb("wT", [EXPERTS, 2, SEQ])
    w_all = sb("w_all", [P, EXPERTS, 2, SEQ])
    sg = sb("sg", [P, 2, SEQ])
    hidden = sb("hidden", [P, 4, SEQ])
    hn_high, hn_low = sb("hn_high", [P, 2, SEQ], F32R), sb("hn_low", [P, 2, SEQ], F32R)
    hid_high, hid_low = sb("hid_high", [P, 8, SEQ], F32R), sb("hid_low", [P, 8, SEQ], F32R)
    w_high, w_low = sb("w_high", [P, 2, 3, 4 * P], F32R), sb("w_low", [P, 2, 3, 4 * P], F32R)
    wy = sb("wy", [P, 2, SEQ])
    total = sb("total", [P, 2, SEQ])

    loaded = flow("loaded")
    hsq_done, ms_done, ln_done, r_done, hn_done = C["rms"]
    logit_done, gate_step, weight_done = (flow(n) for n in ("logit_done", "gate_step", "weight_done"))
    wt_done, wt_copied, wt_out = (flow(n) for n in ("wt_done", "wt_copied", "wt_out"))
    spread = [flow(f"spread_{i}") for i in range(2)]
    hn_high_done, hn_low_done = flow("hn_high_done"), flow("hn_low_done")
    w_high_done, w_low_done = flow("w_high_done", 6), flow("w_low_done", 6)
    gate_done, up_done, silu_done = flow("gate_done", 16), flow("up_done", 16), flow("silu_done", 16)
    hid_done, hid_high_done, hid_low_done = flow("hid_done", 16), flow("hid_high_done", 16), flow("hid_low_done", 16)
    down_done, wy_done, acc_done = flow("down_done", 4), flow("wy_done", 4), flow("acc_done", 4)
    s = C["norm"](0)

    TURNS = EXPERTS // 2

    def all_turns(eng, body):
        body(0)
        with eng.Fori(1, TURNS - 1) as turn:
            body(turn)
        body(TURNS - 1)

    def is_turn(turn, which):
        return isinstance(turn, int) and turn == which

    def passes(turn):
        return range(0 if is_turn(turn, 0) else -1, 3)

    def split_at(turn):
        steps = {4 + k: (1, k) for k in range(3)}
        if not is_turn(turn, TURNS - 1):
            steps.update({11 + k: (2, k) for k in range(3)})
        return steps

    block = ctx.enter_context(nc.Block())

    @block.sync
    def _(sp):
        for dst, src in ((rms_w, "rms2"), (router, "router"), (order, "order")):
            sp.dma_start(dst[:], d[src]).then_inc(loaded.sem, 16)
        cross.load(sp, d)
        cross.spread_bias(sp, d)
        sp.wait_ge(wt_copied.sem, 2)
        sp.dma_start(d["gates"], wT[:]).then_inc(wt_out.sem, 16)
        sp.wait_ge(wt_out.sem, 16)
        for i, (lo, hi) in enumerate(((0, 2), (2, EXPERTS))):
            src = bass.AP(d["gates"].tensor, lo * 2 * SEQ, [[0, P], [1, (hi - lo) * 2 * SEQ]])
            sp.dma_start(w_all[:, lo:hi].rearrange("p e b t -> p (e b t)"), src).then_inc(spread[i].sem, 16)
        with sp.Fori(1, TURNS) as turn:
            for e in range(2):
                sp.wait_ge(*w_low_done.at(turn, 3 * e - 3))
                weights.load(sp, d, turn, e)

    @block.tensor
    def _(pe):
        pe.wait_ge(loaded.sem, 48)
        for b in range(2):
            pe.wait_ge(*hsq_done.at(1, b + 1))
            nc.tensor.matmul(ps[:, b, :], C["mean_ones"], hsq[:, b, :], start=True, stop=True).then_inc(ms_done.sem, 1)
        for tile in range(8):
            b, t0 = tile // 4, tile % 4 * 128
            pe.wait_ge(*hn_done.at(1, b + 1))
            last = nc.tensor.matmul(ps[:, 6, 8 * tile:8 * tile + 8], hn[:, b, t0:t0 + 128], router[:], start=True, stop=True)
        last.then_inc(logit_done.sem, 1)
        pe.wait_ge(cross.line_in.sem, 32)
        nc.tensor.matmul(ps[0:HEADS, 7, :], cross.rel[:], cross.onehot[:, 0:512], start=True, stop=True).then_inc(cross.line_done.sem, 1)
        nc.tensor.matmul(ps[0:HEADS, 5, 0:SPAN - 512], cross.rel[:], cross.onehot[:, 512:SPAN], start=True, stop=True).then_inc(cross.line_done.sem, 1)

        def product(out, weight, e, j, high, low, start, stop):
            w_hi, w_lo = (w[:, e, weight, P * j:P * j + P] for w in (w_high, w_low))
            nc.tensor.matmul(out, w_hi, high, start=start, stop=False)
            nc.tensor.matmul(out, w_hi, low, start=False, stop=False)
            return nc.tensor.matmul(out, w_lo, high, start=False, stop=stop)

        def down(turn, i):
            e, b = i // 2 % 2, i % 2
            pe.wait_ge(*hid_low_done.at(turn, 4 * i + 4))
            if wy_done.any(turn, i - 1):
                pe.wait_ge(*wy_done.at(turn, i - 1))
            for j in range(4):
                last = product(ps[:, 4 + b, :], DOWN, e, j, hid_high[:, 4 * b + j, :], hid_low[:, 4 * b + j, :], j == 0, j == 3)
            last.then_inc(down_done.sem, 1)

        def body(turn):
            for i in range(4):
                e, b = divmod(i, 2)
                if b == 0:
                    pe.wait_ge(*w_low_done.at(turn, 3 * e + 3))
                if is_turn(turn, 0) and e == 0:
                    pe.wait_ge(hn_low_done.sem, b + 1)
                for j in range(4):
                    n = 4 * i + j
                    bank = 2 * (n % 2)
                    if silu_done.any(turn, n - 1):
                        pe.wait_ge(*silu_done.at(turn, n - 1))
                    product(ps[:, bank, :], GATE, e, j, hn_high[:, b, :], hn_low[:, b, :], True, True).then_inc(gate_done.sem, 1)
                    if hid_done.any(turn, n - 1):
                        pe.wait_ge(*hid_done.at(turn, n - 1))
                    product(ps[:, bank + 1, :], UP, e, j, hn_high[:, b, :], hn_low[:, b, :], True, True).then_inc(up_done.sem, 1)
                    if j == 2 and i - 1 in passes(turn):
                        down(turn, i - 1)
                    if is_turn(turn, 0) and n == 2:
                        pe.wait_ge(weight_done.sem, 1)
                        pe.wait_ge(cross.line_copied.sem, 2)
                        for tile in range(8):
                            last = nc.tensor.transpose(ps[0:EXPERTS, 6 + tile // 4, tile % 4 * P:tile % 4 * P + P], G[6][:, tile, :], C["ident"])
                        last.then_inc(wt_done.sem, 1)

        all_turns(pe, body)
        down(TURNS - 1, 3)
        for b in range(2):
            pe.wait_ge(acc_done.sem, 4 * TURNS + 1 + b)
            normalise(nc, "pe_mean", pe, s, b, total[:, b, :], None, (None, None), (ps[:, b, :], ps[:, 2 + b, :]), C)
        for b in range(2):
            normalise(nc, "pe_var", pe, s, b, None, None, (hsq, rn), (ps[:, b, :], ps[:, 2 + b, :]), C)

    @block.scalar
    def _(ac):
        A = nc.scalar.activation
        nc.scalar.preload_act_table_set("natural_log_exp_and_others")
        for b in range(2):
            A(hsq[:, b, :], h1[:, b, :], ACT.Square).then_inc(hsq_done.sem, 1)
        for b in range(2):
            ac.wait_ge(*ms_done.at(1, b + 1))
            A(rn[:, b, :], ps[:, b, :], ACT.Ln, bias=C["eps"]).then_inc(ln_done.sem, 1)
            ac.wait_ge(*ln_done.at(1, b + 1))
            A(rn[:, b, :], rn[:, b, :], ACT.Exp, scale=-0.5).then_inc(r_done.sem, 1)
        def weight_high(turn, e, k):
            ac.wait_ge(*weights.loaded[e % 2].at(turn, 48 * (1 + e // 2)))
            if down_done.any(turn, 2 * e - 2):
                ac.wait_ge(*down_done.at(turn, 2 * e - 2))
            A(w_high[:, e % 2, k, :], weights.all[:, e % 2, k, :], ACT.Copy).then_inc(w_high_done.sem, 1)

        for k in range(3):
            weight_high(0, 0, k)
        for b in range(2):
            ac.wait_ge(*hn_done.at(1, b + 1))
            A(hn_high[:, b, :], hn[:, b, :], ACT.Copy).then_inc(hn_high_done.sem, 1)
        ac.wait_ge(gate_step.sem, 2)
        A(G[1][:], G[0][:], ACT.Exp).then_inc(gate_step.sem, 1)
        ac.wait_ge(cross.line_done.sem, 2)
        A(cross.line[:, 0:512], ps[0:HEADS, 7, :], ACT.Copy).then_inc(cross.line_copied.sem, 1)
        A(cross.line[:, 512:SPAN], ps[0:HEADS, 5, 0:SPAN - 512], ACT.Copy).then_inc(cross.line_copied.sem, 1)
        nc.scalar.preload_act_table_set("silu_and_others")

        def hidden_high(turn, n):
            ac.wait_ge(*hid_done.at(turn, n + 1))
            if down_done.any(turn, n // 4 - 1):
                ac.wait_ge(*down_done.at(turn, n // 4 - 1))
            A(hid_high[:, n % 8, :], hidden[:, n % 4, :], ACT.Copy).then_inc(hid_high_done.sem, 1)

        def body(turn):
            for n in range(16):
                ac.wait_ge(*gate_done.at(turn, n + 1))
                if hid_done.any(turn, n - 1):
                    ac.wait_ge(*hid_done.at(turn, n - 1))
                A(sg[:, n % 2, :], ps[:, 2 * (n % 2), :], ACT.Silu).then_inc(silu_done.sem, 1)
                if hid_done.any(turn, n):
                    hidden_high(turn, n - 1)
                if n in split_at(turn):
                    weight_high(turn, *split_at(turn)[n])
                if is_turn(turn, 0) and n == 2:
                    ac.wait_ge(wt_done.sem, 1)
                    for b in range(2):
                        A(wT[:, b, :], ps[0:EXPERTS, 6 + b, :], ACT.Copy).then_inc(wt_copied.sem, 1)

        all_turns(ac, body)
        hidden_high(TURNS - 1, 15)
        nc.scalar.preload_act_table_set("natural_log_exp_and_others")
        for b in range(2):
            normalise(nc, "act_square", ac, s, b, None, None, (hsq, rn), None, C)
        for b in range(2):
            normalise(nc, "act_rstd", ac, s, b, None, None, (hsq, rn), (ps[:, b, :], ps[:, 2 + b, :]), C)

    @block.vector
    def _(dv):
        v = nc.vector
        dv.wait_ge(loaded.sem, 48)
        for b in range(2):
            dv.wait_ge(*r_done.at(1, b + 1))
            v.scalar_tensor_tensor(hn[:, b, :], h1[:, b, :], rms_w[:, 0:1], rn[:, b, :], ALU.mult, ALU.mult).then_inc(hn_done.sem, 1)
        for b in range(2):
            dv.wait_ge(hn_high_done.sem, b + 1)
            v.tensor_tensor(hn_low[:, b, :], hn[:, b, :], hn_high[:, b, :], ALU.subtract).then_inc(hn_low_done.sem, 1)

        at = [0]

        def go(ins):
            ins.then_inc(gate_step.sem, 1)
            at[0] += 1

        def settled():
            dv.wait_ge(gate_step.sem, at[0])

        def bc8(n):
            return col[:, :, n:n + 1].to_broadcast([P, 8, EXPERTS])

        def best(score, hot, work, n):
            go(v.tensor_reduce(col[:, :, n], score[:], AX, ALU.max))
            settled()
            go(v.tensor_tensor(hot[:], score[:], bc8(n), ALU.is_equal))
            settled()
            go(v.tensor_tensor(work[:], hot[:], order[:], ALU.mult))
            settled()
            go(v.tensor_reduce(col[:, :, n + 1], work[:], AX, ALU.max))
            settled()
            go(v.tensor_tensor(hot[:], order[:], bc8(n + 1), ALU.is_equal))
            settled()

        dv.wait_ge(logit_done.sem, 1)
        go(v.tensor_reduce(col[:, :, 0], ps[:, 6, 0:64].rearrange("p (t e) -> p t e", e=8), AX, ALU.max))
        settled()
        go(v.tensor_tensor(G[0][:], ps[:, 6, 0:64].rearrange("p (t e) -> p t e", e=8), bc8(0), ALU.subtract))
        at[0] += 1
        settled()
        go(v.tensor_reduce(col[:, :, 1], G[1][:], AX, ALU.add))
        settled()
        go(v.reciprocal(col[:, :, 0], col[:, :, 1]))
        settled()
        go(v.tensor_tensor(G[2][:], G[1][:], bc8(0), ALU.mult))
        settled()
        best(G[2], G[3], G[5], 2)
        go(v.scalar_tensor_tensor(G[4][:], G[3][:], -2.0, G[2][:], ALU.mult, ALU.add))
        settled()
        best(G[4], G[0], G[5], 4)
        go(v.tensor_tensor(G[5][:], G[0][:], G[3][:], ALU.add))
        settled()
        v.tensor_tensor(G[6][:], G[5][:], G[2][:], ALU.mult).then_inc(weight_done.sem, 1)

        def weigh(turn, i):
            dv.wait_ge(*down_done.at(turn, i + 1))
            dv.wait_ge(*acc_done.at(turn, i + 1))
            v.tensor_tensor(wy[:, i % 2, :], ps[:, 4 + i % 2, :], w_all[:, bass.ds(turn * 2 + i // 2, 1), i % 2, :], ALU.mult).then_inc(wy_done.sem, 1)

        def hidden_low(turn, n):
            dv.wait_ge(*hid_high_done.at(turn, n + 1))
            v.tensor_tensor(hid_low[:, n % 8, :], hidden[:, n % 4, :], hid_high[:, n % 8, :], ALU.subtract).then_inc(hid_low_done.sem, 1)

        def body(turn):
            for n in range(16):
                i, j = divmod(n, 4)
                dv.wait_ge(*silu_done.at(turn, n + 1))
                dv.wait_ge(*up_done.at(turn, n + 1))
                if hid_low_done.any(turn, n - 3):
                    dv.wait_ge(*hid_low_done.at(turn, n - 3))
                v.tensor_tensor(hidden[:, n % 4, :], sg[:, n % 2, :], ps[:, 2 * (n % 2) + 1, :], ALU.mult).then_inc(hid_done.sem, 1)
                if hid_done.any(turn, n):
                    hidden_low(turn, n - 1)
                if j == 3 and i - 1 in passes(turn):
                    if is_turn(turn, 0) and i == 1:
                        dv.wait_ge(spread[0].sem, 16)
                    if not is_turn(turn, 0) and i == 0:
                        dv.wait_ge(spread[1].sem, 16)
                    weigh(turn, i - 1)

        all_turns(dv, body)
        hidden_low(TURNS - 1, 15)
        weigh(TURNS - 1, 3)
        for b in range(2):
            normalise(nc, "dve_centre", dv, s, b, total[:, b, :], None, (hsq, rn), (ps[:, b, :], ps[:, 2 + b, :]), C)
        for b in range(2):
            normalise(nc, "dve_scale", dv, s, b, None, x1[:, b, :], (hsq, rn), None, C)
        dv.wait_ge(*s["scaled"].at(s["use"], 2))

    @block.gpsimd
    def _(pool):
        def accumulate(turn, i):
            b = i % 2
            pool.wait_ge(*wy_done.at(turn, i + 1))
            pool.wait_ge(*acc_done.at(turn, i + 1))
            nc.gpsimd.tensor_tensor(total[:, b, :], total[:, b, :], wy[:, b, :], ALU.add).then_inc(acc_done.sem, 1)

        def weight_low(turn, e, k):
            pool.wait_ge(*w_high_done.at(turn, 3 * e + k + 1))
            nc.gpsimd.tensor_tensor(w_low[:, e % 2, k, :], weights.all[:, e % 2, k, :], w_high[:, e % 2, k, :], ALU.subtract).then_inc(w_low_done.sem, 1)

        def body(turn):
            for n in range(16):
                i, j = divmod(n, 4)
                if n in split_at(turn):
                    weight_low(turn, *split_at(turn)[n])
                if j == 3 and i - 1 in passes(turn):
                    accumulate(turn, i - 1)

        for k in range(3):
            weight_low(0, 0, k)
        for b in range(2):
            nc.gpsimd.tensor_tensor(total[:, b, :], x[:, b, :], h1[:, b, :], ALU.add).then_inc(acc_done.sem, 1)
        all_turns(pool, body)
        accumulate(TURNS - 1, 3)


class CrossPlaces:

    LOADS = (("wq", "xwq", [P, P]), ("wk", "xwk", [P, P]), ("wv", "xwv", [P, P]), ("wo", "xwo", [P, P]), ("ctxT", "ctxT", [P, 2, 4, KEYS]),
             ("head_of", "head_of", [P, HEADS]), ("quarter", "quarter", [P, HEADS]))

    def __init__(self, nc, ctx, C):
        def sb(name, shape):
            return ctx.enter_context(nc.sbuf_tensor("cr_" + name, shape, F32))

        def flow(name):
            return Flow(C["sems"].enter_context(nc.semaphore("cr_" + name)), 0)

        self.place = {name: sb(name, shape) for name, _, shape in self.LOADS}
        self.place["bias"] = sb("bias", [P, 4, HEADS, KEYS])
        self.rel, self.onehot, self.line = sb("rel", [BUCKETS, HEADS]), sb("onehot", [BUCKETS, SPAN]), sb("line", [HEADS, SPAN])
        self.loaded, self.line_in, self.line_done, self.line_copied, self.line_out, self.bias_in = (flow(n) for n in (
            "loaded", "line_in", "line_done", "line_copied", "line_out", "bias_in"))

    def load(self, sp, d):
        sp.dma_start(self.rel[:], d["rel"]).then_inc(self.line_in.sem, 16)
        sp.dma_start(self.onehot[:], d["onehot"]).then_inc(self.line_in.sem, 16)
        for name, src, _ in self.LOADS:
            sp.dma_start(self.place[name][:], d[src]).then_inc(self.loaded.sem, 16)

    def spread_bias(self, sp, d):
        sp.wait_ge(self.line_copied.sem, 2)
        sp.dma_start(d["line"], self.line[:]).then_inc(self.line_out.sem, 16)
        sp.wait_ge(self.line_out.sem, 16)
        for tile in range(4):
            src = bass.AP(d["line"].tensor, 128 * tile, [[1, P], [SPAN, HEADS], [1, KEYS]])
            sp.dma_start(self.place["bias"][:, tile], src).then_inc(self.bias_in.sem, 16)


def build_cross(nc, ctx, x1, x2, Y, places, stack, d, C):
    def sb(name, shape, dt=F32):
        return ctx.enter_context(nc.sbuf_tensor("cr_" + name, shape, dt))

    def flow(name, per=0):
        return Flow(C["sems"].enter_context(nc.semaphore("cr_" + name)), per)

    ps = C["psum"]
    wq, wk, wv, wo, ctxT, head_of, quarter, bias = (places.place[n] for n in ("wq", "wk", "wv", "wo", "ctxT", "head_of", "quarter", "bias"))
    qT = sb("qT", [P, 2, SEQ])
    kbd = sb("kbd", [P, 2, HEADS, KEYS])
    vbd = sb("vbd", [P, 2, HEADS, 8])
    sc = sb("sc", [P, 2, HEADS, KEYS])
    pr = sb("pr", [P, 3, HEADS, KEYS])
    mx = sb("mx", [P, 2, HEADS])
    sm = sb("sm", [P, 2, HEADS])
    ri = sb("ri", [P, 2, HEADS])
    pT = sb("pT", [P, 2, 4, P])
    oT = sb("oT", [P, 2, SEQ])
    centred = sb("centred", [P, 2, SEQ])
    ln = sb("ln", [P, 2, SEQ])
    total = sb("total", [P, 2, SEQ])

    placed = flow("placed")
    loaded2, bias_in = places.loaded, places.bias_in
    q_done, q_copied, k_done, kbd_done, v_done, vbd_done = (flow(n) for n in ("q_done", "q_copied", "k_done", "kbd_done", "v_done", "vbd_done"))
    s_done, add_done, mx_done, sub_done, exp_done, sum_done, rec_done, norm_done = (flow(n) for n in (
        "s_done", "add_done", "mx_done", "sub_done", "exp_done", "sum_done", "rec_done", "norm_done"))
    t_done, t_copied, o_done, o_copied, wo_done, res_done = (flow(n) for n in ("t_done", "t_copied", "o_done", "o_copied", "wo_done", "res_done"))
    s = C["norm"](1)

    block = ctx.enter_context(nc.Block())

    @block.sync
    def _(sp):
        stack.load_first(sp, d)

    @block.tensor
    def _(pe):
        pe.wait_ge(loaded2.sem, 112)
        for b in range(2):
            nc.tensor.matmul(ps[:, 2 + b, 0:KEYS], wk[:], ctxT[:, b, 0, :], start=True, stop=True).then_inc(k_done.sem, 1)
            nc.tensor.matmul(ps[:, 4 + b, 0:P], ctxT[:, b].rearrange("p r k -> p (r k)"), wv[:], start=True, stop=True).then_inc(v_done.sem, 1)
        for b in range(2):
            nc.tensor.matmul(ps[:, 6 + b, :], wq[:], x1[:, b, :], start=True, stop=True).then_inc(q_done.sem, 1)

        def scores(u):
            b, t0 = u // 4, u % 4 * 128
            if u == 0:
                pe.wait_ge(kbd_done.sem, 2)
            pe.wait_ge(q_copied.sem, b + 1)
            if u - 1 > 0:
                pe.wait_ge(add_done.sem, u - 1)
            nc.tensor.matmul(ps[:, u % 2, :], qT[:, b, t0:t0 + 128], kbd[:, b].rearrange("p h k -> p (h k)"), start=True, stop=True).then_inc(s_done.sem, 1)

        def turn(u):
            pe.wait_ge(norm_done.sem, u + 1)
            if u - 1 > 0:
                pe.wait_ge(t_copied.sem, u - 1)
            pe.wait_ge(kbd_done.sem, 2)
            for g in range(4):
                last = nc.tensor.transpose(ps[:, 2 + u % 2, 128 * g:128 * g + 128], pr[:, u % 3, 4 * g:4 * g + 4, :].rearrange("p h k -> p (h k)"), C["ident"])
            last.then_inc(t_done.sem, 1)

        def values(u):
            b, t0 = u // 4, u % 4 * 128
            pe.wait_ge(vbd_done.sem, 2)
            pe.wait_ge(t_copied.sem, u + 1)
            for g in range(4):
                last = nc.tensor.matmul(ps[32 * g:32 * g + 32, 4 + b, t0:t0 + 128], vbd[:, b, 4 * g:4 * g + 4, :].rearrange("p h d -> p (h d)"),
                                        pT[:, u % 2, g, :], start=True, stop=True)
            last.then_inc(o_done.sem, 1)

        scores(0)
        scores(1)
        for u in range(8):
            if u < 6:
                scores(u + 2)
            turn(u)
            if u >= 1:
                values(u - 1)
        values(7)
        for b in range(2):
            pe.wait_ge(o_copied.sem, b + 1)
            nc.tensor.matmul(ps[:, 6 + b, :], wo[:], oT[:, b, :], start=True, stop=True).then_inc(wo_done.sem, 1)
        pe.wait_ge(add_done.sem, 8)
        pe.wait_ge(t_copied.sem, 8)
        for b in range(2):
            pe.wait_ge(res_done.sem, b + 1)
            normalise(nc, "pe_mean", pe, s, b, total[:, b, :], None, (None, None), (ps[:, b, :], ps[:, 2 + b, :]), C)
        for b in range(2):
            normalise(nc, "pe_var", pe, s, b, None, None, (centred, ln), (ps[:, b, :], ps[:, 2 + b, :]), C)

    @block.scalar
    def _(ac):
        A = nc.scalar.activation
        nc.scalar.preload_act_table_set("natural_log_exp_and_others")
        for b in range(2):
            ac.wait_ge(q_done.sem, b + 1)
            A(qT[:, b, :], ps[:, 6 + b, :], ACT.Copy).then_inc(q_copied.sem, 1)
        for u in range(9):
            if u < 8:
                ac.wait_ge(sub_done.sem, u + 1)
                A(pr[:, u % 3], pr[:, u % 3], ACT.Exp).then_inc(exp_done.sem, 1)
            if u >= 1:
                ac.wait_ge(t_done.sem, u)
                if u - 2 > 0:
                    ac.wait_ge(o_done.sem, u - 2)
                A(pT[:, (u - 1) % 2].rearrange("p g t -> p (g t)"), ps[:, 2 + (u - 1) % 2, :], ACT.Copy).then_inc(t_copied.sem, 1)
            if u == 5 or u == 8:
                b = u // 8
                ac.wait_ge(o_done.sem, 4 * b + 4)
                A(oT[:, b, :], ps[:, 4 + b, :], ACT.Copy).then_inc(o_copied.sem, 1)
        for b in range(2):
            normalise(nc, "act_square", ac, s, b, None, None, (centred, ln), None, C)
        for b in range(2):
            normalise(nc, "act_rstd", ac, s, b, None, None, (centred, ln), (ps[:, b, :], ps[:, 2 + b, :]), C)

    @block.vector
    def _(dv):
        v = nc.vector
        dv.wait_ge(loaded2.sem, 112)
        for b in range(2):
            dv.wait_ge(k_done.sem, b + 1)
            v.tensor_tensor(kbd[:, b], ps[:, 2 + b, 0:KEYS].unsqueeze(1).to_broadcast([P, HEADS, KEYS]),
                            head_of[:].unsqueeze(2).to_broadcast([P, HEADS, KEYS]), ALU.mult).then_inc(kbd_done.sem, 1)
            dv.wait_ge(v_done.sem, b + 1)
            v.tensor_tensor(vbd[:, b], ps[:, 4 + b, 0:P].rearrange("p (h d) -> p h d", d=8),
                            quarter[:].unsqueeze(2).to_broadcast([P, HEADS, 8]), ALU.mult).then_inc(vbd_done.sem, 1)

        def total_of(u):
            i = u % 2
            dv.wait_ge(exp_done.sem, u + 1)
            if u - 1 > 0:
                dv.wait_ge(rec_done.sem, u - 1)
            v.tensor_reduce(sm[:, i, :], pr[:, u % 3], AX, ALU.add).then_inc(sum_done.sem, 1)
            dv.wait_ge(sum_done.sem, u + 1)
            if u - 1 > 0:
                dv.wait_ge(norm_done.sem, u - 1)
            v.reciprocal(ri[:, i, :], sm[:, i, :]).then_inc(rec_done.sem, 1)

        dv.wait_ge(bias_in.sem, 64)
        for u in range(8):
            i = u % 2
            dv.wait_ge(s_done.sem, u + 1)
            if u - 1 > 0:
                dv.wait_ge(sub_done.sem, u - 1)
            v.tensor_tensor(sc[:, i], ps[:, i, :].rearrange("p (h k) -> p h k", k=KEYS), bias[:, u % 4], ALU.add).then_inc(add_done.sem, 1)
            dv.wait_ge(add_done.sem, u + 1)
            if u - 1 > 0:
                dv.wait_ge(sub_done.sem, u - 1)
            v.tensor_reduce(mx[:, i, :], sc[:, i], AX, ALU.max).then_inc(mx_done.sem, 1)
            dv.wait_ge(mx_done.sem, u + 1)
            if u - 2 > 0:
                dv.wait_ge(t_done.sem, u - 2)
            v.tensor_tensor(pr[:, u % 3], sc[:, i], mx[:, i, :].unsqueeze(2).to_broadcast([P, HEADS, KEYS]), ALU.subtract).then_inc(sub_done.sem, 1)
            if u >= 1:
                total_of(u - 1)
        total_of(7)
        for b in range(2):
            dv.wait_ge(wo_done.sem, b + 1)
            v.tensor_tensor(total[:, b, :], ps[:, 6 + b, :], x1[:, b, :], ALU.add).then_inc(res_done.sem, 1)
        for b in range(2):
            normalise(nc, "dve_centre", dv, s, b, total[:, b, :], None, (centred, ln), (ps[:, b, :], ps[:, 2 + b, :]), C)
        for b in range(2):
            normalise(nc, "dve_scale", dv, s, b, None, x2[:, b, :], (centred, ln), None, C)
        dv.wait_ge(*s["scaled"].at(s["use"], 2))
        v.memset(Y[64:128, :, 0:1], 0.0).then_inc(placed.sem, 1)
        v.tensor_copy(Y[0:64, :, 0:SEQ], x2[0:64]).then_inc(placed.sem, 1)
        v.tensor_copy(Y[64:128, :, 1:], x2[64:128]).then_inc(placed.sem, 1)

    @block.gpsimd
    def _(pool):
        stack.clear(nc.gpsimd)
        for u in range(8):
            i = u % 2
            pool.wait_ge(rec_done.sem, u + 1)
            nc.gpsimd.tensor_tensor(pr[:, u % 3], pr[:, u % 3], ri[:, i, :].unsqueeze(2).to_broadcast([P, HEADS, KEYS]), ALU.mult).then_inc(norm_done.sem, 1)


class StackPlaces:

    def __init__(self, nc, ctx, C):
        def sb(name, shape):
            return ctx.enter_context(nc.sbuf_tensor("st_" + name, shape, F32))

        def flow(name, per):
            return Flow(C["sems"].enter_context(nc.semaphore("st_" + name)), per)

        self.w_raw, self.wv, self.wo = sb("w_raw", [P, 8, 2 * P]), sb("wv", [P, 8, P]), sb("wo", [P, 8, P])
        self.rope_scale, self.table = sb("rope_scale", [P, 2, 4]), sb("table", [P, 4, SEQ])
        self.q_blocks = sb("q_blocks", [P, 2, 8, 2, 2, WIN])
        self.p_blocks = sb("p_blocks", [P, 2, 4, 2, 2, 2, WIN])
        self.kT, self.vs = sb("kT", [P, 2, WIN + SEQ]), sb("vs", [P, 2, 4, P])
        self.proj_in = [flow(f"proj_in_{i}", 16) for i in range(2)]
        self.wv_in = [flow(f"wv_in_{i}", 16) for i in range(2)]
        self.wo_in = [flow(f"wo_in_{i}", 16) for i in range(2)]
        self.scale_in = [flow(f"scale_in_{i}", 16) for i in range(2)]
        self.table_in, self.pads_zero = flow("table_in", 0), flow("pads_zero", 0)

    def load_qk(self, sp, d, layer, half):
        pairs = slice(4 * half, 4 * half + 4)
        sp.dma_start(self.w_raw[:, pairs, :], at_layer(d["w_qk"], layer)[:, pairs, :]).then_inc(self.proj_in[half].sem, 16)

    def load_v(self, sp, d, layer, half):
        pairs = slice(4 * half, 4 * half + 4)
        sp.dma_start(self.wv[:, pairs, :], at_layer(d["w_v"], layer)[:, pairs, :]).then_inc(self.wv_in[half].sem, 16)

    def load_wo(self, sp, d, layer, half):
        pairs = slice(4 * half, 4 * half + 4)
        sp.dma_start(self.wo[:, pairs, :], at_layer(d["wo"], layer)[:, pairs, :]).then_inc(self.wo_in[half].sem, 16)

    def load_scale(self, sp, d, layer, b):
        sp.dma_start(self.rope_scale[:, b, :], at_layer(d["rope_scale"], layer)).then_inc(self.scale_in[b].sem, 16)

    def load_first(self, sp, d):
        sp.dma_start(self.table[:], d["rope"]).then_inc(self.table_in.sem, 16)
        for half in range(2):
            self.load_qk(sp, d, 0, half)
            self.load_v(sp, d, 0, half)
            self.load_wo(sp, d, 0, half)
            self.load_scale(sp, d, 0, half)

    def clear(self, engine):
        for part in (self.kT[:, :, 0:WIN], self.vs[0:32, :, 0, :], self.q_blocks[:], self.p_blocks[:]):
            engine.memset(part, 0.0).then_inc(self.pads_zero.sem, 1)


def build_stack(nc, ctx, Y, places, d, C):
    def sb(name, shape, dt=F32):
        return ctx.enter_context(nc.sbuf_tensor("st_" + name, shape, dt))

    def flow(name, per):
        return Flow(C["sems"].enter_context(nc.semaphore("st_" + name)), per)

    ps = C["psum"]
    QK_BANK = [ps[:, 0, :], ps[:, 1, :]]
    V_BANK, NORM_BANK, SCORE_BANK, TURN_BANK = (ps[:, 2 + i, :] for i in range(4))
    OUT_BANK = [ps[:, 6, :], ps[:, 7, :]]
    UNITS, PAIRS = 16, 8

    w_high, w_low = sb("w_high", [P, PAIRS, 2 * P], F32R), sb("w_low", [P, PAIRS, 2 * P], F32R)
    y_high, y_low = sb("y_high", [P, 2, SEQ], F32R), sb("y_low", [P, 2, SEQ], F32R)
    sq_high, sq_low = sb("sq_high", [P, SEQ], F32R), sb("sq_low", [P, SEQ], F32R)
    head_ones = sb("head_ones", [P, P], F32R)
    w1 = sb("w1", [P, 2 * HID])
    w2 = sb("w2", [P, 3, P])
    ffn_param = sb("ffn_param", [P, 9])
    vn = sb("vn", [P, 2, 4, P])
    sq = sb("sq", [P, 2, SEQ])
    rn = sb("rn", [P, 2, SEQ])
    swapped = sb("swapped", [P, 2, SEQ])
    cos_part = sb("cos_part", [P, 2, SEQ])
    sin_part = sb("sin_part", [P, 2, SEQ])
    turned = sb("turned", [P, 2, SEQ])
    prob = sb("prob", [P, 2, 8, 64])
    pn = sb("pn", [P, 2, 8, 64])
    oT = sb("oT", [P, 2, SEQ])
    mx = sb("mx", [P, 2, 8])
    rs = sb("rs", [P, 2, 8])
    ri = sb("ri", [P, 2, 8])
    dx = sb("dx", [P, SEQ])
    dsq = sb("dsq", [P, SEQ])
    rstd = sb("rstd", [P, SEQ])
    xn = sb("xn", [P, SEQ])
    gate = sb("gate", [P, SEQ])
    act = sb("act", [P, 2, SEQ])

    w_raw, wv, wo, rope_scale, table = places.w_raw, places.wv, places.wo, places.rope_scale, places.table
    q_blocks, p_blocks, kT, vs = places.q_blocks, places.p_blocks, places.kT, places.vs
    proj_in, wv_in, wo_in, scale_in, table_in = places.proj_in, places.wv_in, places.wo_in, places.scale_in, places.table_in
    pads_zero, ones_ready = places.pads_zero, flow("ones_ready", 0)
    ffn_in = flow("ffn_in", 80)
    vs_in = [flow(f"vs_in_{i}", UNITS // 2 * 32) for i in range(2)]
    high_done, low_done = flow("high_done", UNITS), flow("low_done", UNITS)
    w_high_done, w_split = flow("w_high_done", PAIRS), flow("w_split", PAIRS)
    y_high_done, y_low_done = flow("y_high_done", 2), flow("y_low_done", 2)
    qk_done, sq_done, norm_done, ln_done, r_done = (flow(n, 2 * UNITS) for n in ("qk_done", "sq_done", "norm_done", "ln_done", "r_done"))
    swap_done, sin_done, add_done = (flow(n, 2 * UNITS) for n in ("swap_done", "sin_done", "add_done"))
    rope_done = flow("rope_done", 3 * UNITS)
    v_done, v_copied = flow("v_done", UNITS), flow("v_copied", UNITS)
    score_done, mx_done, sub_done, exp_done, sum_done, rec_done, pn_done, t_done, o_copied, pv_done = (flow(n, UNITS) for n in (
        "score_done", "mx_done", "sub_done", "exp_done", "sum_done", "rec_done", "pn_done", "t_done", "o_copied", "pv_done"))
    pt_copied = flow("pt_copied", 2 * UNITS)
    wo_step = flow("wo_step", UNITS)
    res1_done, res2_done = flow("res1_done", 4), flow("res2_done", 4)
    mean_done, dx_done, dsq_done, var_done, lnv_done, rstd_done, xh_done, xn_done = (flow(n, 2) for n in (
        "mean_done", "dx_done", "dsq_done", "var_done", "lnv_done", "rstd_done", "xh_done", "xn_done"))
    w1_done, gate_done, act_done, w2_step = (flow(n, 6) for n in ("w1_done", "gate_done", "act_done", "w2_step"))

    ROWS = [P, P, HID - 2 * P]

    class Steps:

        def __init__(self, turn, first, last):
            self.turn, self.first, self.last = turn, first, last
            self.range = range(-2 if first else 0, UNITS + 6 if last else UNITS)

        def unit(self, n):
            return (n >= 0 or not self.first) and (n < UNITS or not self.last)

        def resplit(self, job, stage):
            return stage == 5 and (job < 0 or not self.last)

        def stage(self, t):
            job, stage = t // 8 - 1, t % 8
            there = stage < 6 and (job >= 0 or not self.first) and (job < 1 or self.last)
            return (job, stage) if there and t >= 0 else (None, None)

    def all_turns(eng, body):
        body(Steps(0, True, False))
        with eng.Fori(1, LAYERS - 1) as turn:
            body(Steps(turn, False, False))
        body(Steps(LAYERS - 1, False, True))

    block = ctx.enter_context(nc.Block())

    @block.sync
    def _(sp):
        def load_ffn(layer):
            sp.dma_start(w1[:], at_layer(d["w1"], layer)).then_inc(ffn_in.sem, 16)
            for j, rows in enumerate(ROWS):
                sp.dma_start(w2[0:rows, j, :], at_layer(d["w2"], layer)[j * P:j * P + rows, :]).then_inc(ffn_in.sem, 16)
            sp.dma_start(ffn_param[:], at_layer(d["ffn_param"], layer)).then_inc(ffn_in.sem, 16)

        def body(s):
            turn = s.turn
            for t in s.range:
                if t == 0 and not s.first:
                    sp.wait_ge(*wo_step.at(turn, 0))
                    places.load_wo(sp, d, turn, 1)
                if t == 6:
                    if res2_done.any(turn, 0):
                        sp.wait_ge(*res2_done.at(turn, 0))
                    load_ffn(turn)
                if not s.last:
                    if t == 6:
                        sp.wait_ge(*w_split.at(turn, PAIRS))
                        for half in range(2):
                            places.load_qk(sp, d, turn + 1, half)
                    if t == 8:
                        sp.wait_ge(*sin_done.at(turn, 16))
                        places.load_scale(sp, d, turn + 1, 0)
                    if t == 11:
                        sp.wait_ge(*v_done.at(turn, 12))
                        places.load_v(sp, d, turn + 1, 0)
                    if t == 13:
                        sp.wait_ge(*wo_step.at(turn, 12))
                        places.load_wo(sp, d, turn + 1, 0)
                    if t == 15:
                        sp.wait_ge(*v_done.at(turn, 16))
                        places.load_v(sp, d, turn + 1, 1)
                        sp.wait_ge(*sin_done.at(turn, 32))
                        places.load_scale(sp, d, turn + 1, 1)
                n = t + 1
                if t >= -1 and s.unit(n):
                    r = n % 2
                    sp.wait_ge(*v_copied.at(turn, n + 1))
                    sp.dma_start(vs[32:128, r, :, :], vn[0:96, r, :, :]).then_inc(vs_in[r].sem, 16)
                    sp.dma_start(vs[0:32, r, 1:4, :], vn[96:128, r, 0:3, :]).then_inc(vs_in[r].sem, 16)

        all_turns(sp, body)

    @block.tensor
    def _(pe):
        mm = nc.tensor.matmul

        def project(s, n, which):
            b, pair = n // 8 % 2, n % 8
            if which == 0:
                if n % 16 < 8:
                    pe.wait_ge(*w_split.at(s.turn, PAIRS * (n // 16) + pair + 1))
                if n % 8 == 0:
                    pe.wait_ge(*y_high_done.at(s.turn, n // 8 + 1))
            if swap_done.any(s.turn, 2 * (n - 1) + which + 1):
                pe.wait_ge(*swap_done.at(s.turn, 2 * (n - 1) + which + 1))
            cols = slice(P * which, P * which + P)
            mm(QK_BANK[which], w_high[:, pair, cols], y_high[:, b, :], start=True, stop=False)
            mm(QK_BANK[which], w_low[:, pair, cols], y_high[:, b, :], start=False, stop=False)
            if n % 8 == 0:
                pe.wait_ge(*y_low_done.at(s.turn, n // 8 + 1))
            mm(QK_BANK[which], w_high[:, pair, cols], y_low[:, b, :], start=False, stop=True).then_inc(qk_done.sem, 1)

        def head_norm(s, n, which):
            pe.wait_ge(*sq_done.at(s.turn, 2 * n + which + 1))
            if ln_done.any(s.turn, 2 * n + which):
                pe.wait_ge(*ln_done.at(s.turn, 2 * n + which))
            if which == 0:
                mm(NORM_BANK, C["head_ones"], sq[:, 0, :], start=True, stop=True).then_inc(norm_done.sem, 1)
            else:
                pe.wait_ge(*high_done.at(s.turn, n + 1))
                mm(NORM_BANK, head_ones[:], sq_high[:], start=True, stop=False)
                pe.wait_ge(*low_done.at(s.turn, n + 1))
                mm(NORM_BANK, head_ones[:], sq_low[:], start=False, stop=True).then_inc(norm_done.sem, 1)

        def project_v(s, n, here, before):
            b, pair = n // 8 % 2, n % 8
            if v_copied.any(s.turn, n):
                pe.wait_ge(*v_copied.at(s.turn, n))
            if before[1] == 1:
                pe.wait_ge(*lnv_done.at(s.turn, before[0] + 1))
            if here[1] in (2, 3, 4):
                pe.wait_ge(*act_done.at(s.turn, 3 * here[0] + here[1] - 1))
            pe.wait_ge(*wv_in[pair // 4].at(s.turn, 16 * (n // 16) + 16))
            for tile in range(4):
                rows = slice(P * tile, P * tile + P)
                last = mm(V_BANK[:, rows], Y[:, b, rows], wv[:, pair, :], start=True, stop=True)
            last.then_inc(v_done.sem, 1)

        def scores(s, n):
            r = n % 2
            pe.wait_ge(*rope_done.at(s.turn, 3 * n + 3))
            if sub_done.any(s.turn, n):
                pe.wait_ge(*sub_done.at(s.turn, n))
            mm(SCORE_BANK, C["ident16"], C["mask16"], start=True, stop=False, skip_group_check=True)
            for i in range(8):
                for odd in range(2):
                    t0 = 64 * i + WIN * odd
                    last = mm(SCORE_BANK[64 * odd:64 * odd + 64, 64 * i:64 * i + 64],
                              q_blocks[:, r, i, odd].rearrange("p h q -> p (h q)"), kT[:, r, t0:t0 + 64],
                              start=False, stop=(i == 7), skip_group_check=True)
            last.then_inc(score_done.sem, 1)

        def turn_probs(s, n, here):
            r = n % 2
            pe.wait_ge(*vs_in[r].at(s.turn, 32 * (n // 2) + 32))
            pe.wait_ge(*pn_done.at(s.turn, n + 1))
            if o_copied.any(s.turn, n):
                pe.wait_ge(*o_copied.at(s.turn, n))
            job, stage = here
            if stage == 1:
                pe.wait_ge(*dx_done.at(s.turn, job + 1))
            if stage in (2, 3, 4):
                pe.wait_ge(*gate_done.at(s.turn, 3 * job + stage - 1))
            for j in range(4):
                last = nc.tensor.transpose(TURN_BANK[:, P * j:P * j + P], pn[:, r, 2 * j:2 * j + 2, :].rearrange("p i k -> p (i k)"), C["ident"])
            last.then_inc(t_done.sem, 1)

        def values(s, n):
            r = n % 2
            pe.wait_ge(*pt_copied.at(s.turn, 2 * n + 2))
            for j in range(4):
                for odd in range(2):
                    for head in range(2):
                        rows = slice(64 * head, 64 * head + 64)
                        last = mm(TURN_BANK[rows, P * j:P * j + P].rearrange("p (h o q) -> p h o q", h=2, q=WIN)[:, :, odd, :],
                                  (vn if odd else vs)[:, r, j, rows], p_blocks[:, r, j, odd, head].rearrange("p h q -> p (h q)"),
                                  start=True, stop=True)
            last.then_inc(pv_done.sem, 1)

        def out_proj(s, n):
            b, pair = n // 8 % 2, n % 8
            if n >= 0:
                pe.wait_ge(*wo_in[pair // 4].at(s.turn, 16))
            pe.wait_ge(*o_copied.at(s.turn, n + 1))
            mm(OUT_BANK[b], wo[:, pair, :], oT[:, n % 2, :], start=(pair == 0), stop=(pair == 7)).then_inc(wo_step.sem, 1)

        def up(s, t, job, j):
            if j == 0:
                pe.wait_ge(*ffn_in.at(s.turn, 80 * (job + 1) if job < 1 else 80))
                pe.wait_ge(*xn_done.at(s.turn, job + 1))
                pe.wait_ge(*lnv_done.at(s.turn, job + 1))
            pe.wait_ge(*v_copied.at(s.turn, min(t + 1, UNITS) if s.last else t + 1))
            pe.wait_ge(*o_copied.at(s.turn, min(t, UNITS) if s.last else t))
            if act_done.any(s.turn, 3 * job + j):
                pe.wait_ge(*act_done.at(s.turn, 3 * job + j))
            mm(TURN_BANK[0:ROWS[j], :], w1[:, HID + P * j:HID + P * j + ROWS[j]], xn[:], start=True, stop=True)
            mm(V_BANK[0:ROWS[j], :], w1[:, P * j:P * j + ROWS[j]], xn[:], start=True, stop=True).then_inc(w1_done.sem, 1)

        def down(s, job, j):
            pe.wait_ge(*act_done.at(s.turn, 3 * job + j + 1))
            mm(OUT_BANK[job % 2], w2[0:ROWS[j], j, :], act[0:ROWS[j], j % 2, :], start=(j == 0), stop=(j == 2)).then_inc(w2_step.sem, 1)

        def body(s):
            for t in s.range:
                here, before = s.stage(t), s.stage(t - 1)
                job, stage = here
                if s.unit(t + 2):
                    project(s, t + 2, 0)
                    project(s, t + 2, 1)
                    head_norm(s, t + 2, 0)
                if stage == 1:
                    pe.wait_ge(*res1_done.at(s.turn, 2 * job + 2))
                    pe.wait_ge(*o_copied.at(s.turn, min(t, UNITS) if s.last else t))
                    mm(TURN_BANK, C["mean_ones"], Y[:, job % 2, 0:SEQ], start=True, stop=True).then_inc(mean_done.sem, 1)
                if stage in (3, 4, 5):
                    down(s, job, stage - 3)
                if stage in (2, 3, 4):
                    up(s, t, job, stage - 2)
                if t >= -1 and s.unit(t + 1):
                    scores(s, t + 1)
                if s.unit(t + 2):
                    head_norm(s, t + 2, 1)
                if s.unit(t) and t >= 0:
                    turn_probs(s, t, here)
                if t >= -1 and s.unit(t + 1):
                    project_v(s, t + 1, here, before)
                if s.unit(t - 1) and t - 1 >= -1:
                    out_proj(s, t - 1)
                if s.unit(t) and t >= 0:
                    values(s, t)
                if stage == 1:
                    pe.wait_ge(*dsq_done.at(s.turn, job + 1))
                    pe.wait_ge(*v_copied.at(s.turn, t + 2 if s.unit(t + 1) else UNITS))
                    mm(V_BANK, C["mean_ones"], dsq[:], start=True, stop=True).then_inc(var_done.sem, 1)

        pe.wait_ge(pads_zero.sem, 4)
        pe.wait_ge(ones_ready.sem, 1)
        all_turns(pe, body)

    @block.scalar
    def _(ac):
        A = nc.scalar.activation

        def logarithm(s, n, which):
            i = 2 * n + which
            ac.wait_ge(*norm_done.at(s.turn, i + 1))
            if rope_done.any(s.turn, 3 * (n - 1) + 2 + which):
                ac.wait_ge(*rope_done.at(s.turn, 3 * (n - 1) + 2 + which))
            A(rn[:, which, :], NORM_BANK, ACT.Ln, bias=C["tiny"], scale=SS_SCALE).then_inc(ln_done.sem, 1)

        def root(s, n, which):
            ac.wait_ge(*ln_done.at(s.turn, 2 * n + which + 1))
            A(rn[:, which, :], rn[:, which, :], ACT.Exp, bias=C["ln_scale"], scale=-0.5).then_inc(r_done.sem, 1)

        def body(s):
            for t in s.range:
                job, stage = s.stage(t)
                if s.unit(t - 1) and t >= 0:
                    ac.wait_ge(*pv_done.at(s.turn, t))
                    if wo_step.any(s.turn, t - 2):
                        ac.wait_ge(*wo_step.at(s.turn, t - 2))
                    A(oT[:, (t - 1) % 2, :], TURN_BANK, ACT.Copy).then_inc(o_copied.sem, 1)
                if s.unit(t + 2):
                    for which in range(2):
                        ac.wait_ge(*qk_done.at(s.turn, 2 * (t + 2) + which + 1))
                        if norm_done.any(s.turn, 2 * (t + 1) + which + 1):
                            ac.wait_ge(*norm_done.at(s.turn, 2 * (t + 1) + which + 1))
                        if which == 1 and low_done.any(s.turn, t + 2):
                            ac.wait_ge(*low_done.at(s.turn, t + 2))
                        A(sq[:, which, :], QK_BANK[which], ACT.Square).then_inc(sq_done.sem, 1)
                    ac.wait_ge(*sq_done.at(s.turn, 2 * (t + 2) + 2))
                    A(sq_high[:], sq[:, 1, :], ACT.Copy).then_inc(high_done.sem, 1)
                if s.unit(t + 2):
                    logarithm(s, t + 2, 0)
                    root(s, t + 2, 0)
                if stage in (2, 3, 4):
                    j = stage - 2
                    if j == 0:
                        ac.wait_ge(*ffn_in.at(s.turn, 80 * (job + 1) if job < 1 else 80))
                    ac.wait_ge(*w1_done.at(s.turn, 3 * job + j + 1))
                    if act_done.any(s.turn, 3 * job + j):
                        ac.wait_ge(*act_done.at(s.turn, 3 * job + j))
                    A(gate[0:ROWS[j], :], TURN_BANK[0:ROWS[j], :], ACT.Gelu, bias=ffn_param[0:ROWS[j], 5 + j:6 + j]).then_inc(gate_done.sem, 1)
                    nc.scalar.preload_act_table_set("natural_log_exp_and_others")
                if stage == 1:
                    ac.wait_ge(*dx_done.at(s.turn, job + 1))
                    if var_done.any(s.turn, job):
                        ac.wait_ge(*var_done.at(s.turn, job))
                    A(dsq[:], dx[:], ACT.Square).then_inc(dsq_done.sem, 1)
                if s.unit(t + 2):
                    logarithm(s, t + 2, 1)
                if s.unit(t) and t >= 0:
                    ac.wait_ge(*t_done.at(s.turn, t + 1))
                    if pv_done.any(s.turn, t - 1):
                        ac.wait_ge(*pv_done.at(s.turn, t - 1))
                    for half in range(2):
                        rows = slice(64 * half, 64 * half + 64)
                        A(p_blocks[rows, t % 2, :, :, :, half, :].rearrange("p j o h q -> p (j o h) q"),
                          TURN_BANK[rows, :].rearrange("p (n q) -> p n q", q=WIN), ACT.Copy).then_inc(pt_copied.sem, 1)
                if s.resplit(job, stage):
                    ac.wait_ge(*res2_done.at(s.turn, 2 * job + 2))
                    ac.wait_ge(*v_done.at(s.turn, 8 * job + 8))
                    A(y_high[:, job % 2, :], Y[:, job % 2, 0:SEQ], ACT.Copy).then_inc(y_high_done.sem, 1)
                if s.unit(t + 2):
                    root(s, t + 2, 1)
                if t >= -1 and s.unit(t + 1):
                    ac.wait_ge(*v_done.at(s.turn, t + 2))
                    if pv_done.any(s.turn, t):
                        ac.wait_ge(*pv_done.at(s.turn, t))
                    if vs_in[(t + 1) % 2].any(s.turn, 32 * ((t + 1) // 2)):
                        ac.wait_ge(*vs_in[(t + 1) % 2].at(s.turn, 32 * ((t + 1) // 2)))
                    A(vn[:, (t + 1) % 2], V_BANK.rearrange("p (j f) -> p j f", f=P), ACT.Copy).then_inc(v_copied.sem, 1)
                if t >= -1 and s.unit(t + 1):
                    ac.wait_ge(*sub_done.at(s.turn, t + 2))
                    A(prob[:, (t + 1) % 2], prob[:, (t + 1) % 2], ACT.Exp, scale=QK_SCALE).then_inc(exp_done.sem, 1)
                if stage == 1:
                    ac.wait_ge(*var_done.at(s.turn, job + 1))
                    if xh_done.any(s.turn, job):
                        ac.wait_ge(*xh_done.at(s.turn, job))
                    A(rstd[:], V_BANK, ACT.Ln, bias=C["eps"]).then_inc(lnv_done.sem, 1)
                    ac.wait_ge(*lnv_done.at(s.turn, job + 1))
                    A(rstd[:], rstd[:], ACT.Exp, scale=-0.5).then_inc(rstd_done.sem, 1)

        nc.scalar.preload_act_table_set("natural_log_exp_and_others")
        A(head_ones[:], C["head_ones"], ACT.Copy).then_inc(ones_ready.sem, 1)
        for b in range(2):
            A(y_high[:, b, :], Y[:, b, 0:SEQ], ACT.Copy).then_inc(y_high_done.sem, 1)
        ac.wait_ge(pads_zero.sem, 4)
        all_turns(ac, body)

    @block.vector
    def _(dv):
        v = nc.vector

        def high_weights(s, pair, ahead):
            dv.wait_ge(*proj_in[pair // 4].at(s.turn, 16 * ahead + 16))
            if ahead:
                dv.wait_ge(*v_done.at(s.turn, 8 + pair + 1))
            v.tensor_copy(w_high[:, pair, :], w_raw[:, pair, :]).then_inc(w_high_done.sem, 1)

        def rotate(s, n, which):
            i, tab, b = 2 * n + which, 2 * which, n // 8 % 2
            if which == 0 and n % 8 == 0:
                dv.wait_ge(*scale_in[b].at(s.turn, 16 * (n // 16) + 16))
            dv.wait_ge(*sq_done.at(s.turn, i + 1))
            if add_done.any(s.turn, i - 1):
                dv.wait_ge(*add_done.at(s.turn, i - 1))
            if sin_done.any(s.turn, i - 1):
                dv.wait_ge(*sin_done.at(s.turn, i - 1))
            v.scalar_tensor_tensor(cos_part[:, which, :], QK_BANK[which], rope_scale[:, b, tab:tab + 1], table[:, tab, :],
                                   ALU.mult, ALU.mult)
            v.stream_shuffle(swapped[:, which, :], QK_BANK[which], HALF_SWAP).then_inc(swap_done.sem, 1)

        def rotate_sin(s, n, which):
            i, tab, b = 2 * n + which, 2 * which, n // 8 % 2
            dv.wait_ge(*swap_done.at(s.turn, i + 1))
            v.scalar_tensor_tensor(sin_part[:, which, :], swapped[:, which, :], rope_scale[:, b, tab + 1:tab + 2], table[:, tab + 1, :],
                                   ALU.mult, ALU.mult).then_inc(sin_done.sem, 1)

        def rope_last(s, n, which):
            r = n % 2
            dv.wait_ge(*add_done.at(s.turn, 2 * n + which + 1))
            dv.wait_ge(*r_done.at(s.turn, 2 * n + which + 1))
            if score_done.any(s.turn, n - 1):
                dv.wait_ge(*score_done.at(s.turn, n - 1))
            if which == 0:
                for head in range(2):
                    rows = slice(64 * head, 64 * head + 64)
                    v.scalar_tensor_tensor(q_blocks[rows, r, :, :, head, :].rearrange("p i o q -> p (i o) q"),
                                           rn[rows, 0, :].rearrange("p (w q) -> p w q", q=WIN), 1e12,
                                           turned[rows, 0, :].rearrange("p (w q) -> p w q", q=WIN), ALU.min, ALU.mult).then_inc(rope_done.sem, 1)
            else:
                v.scalar_tensor_tensor(kT[:, r, WIN:], rn[:, 1, :], 1e12, turned[:, 1, :], ALU.min, ALU.mult).then_inc(rope_done.sem, 1)

        def residual1(s, job):
            b = job % 2
            dv.wait_ge(*wo_step.at(s.turn, 8 * job + 8))
            for f in range(2):
                dst = Y[64 * f:64 * f + 64, b, f:f + SEQ]
                v.tensor_tensor(dst, OUT_BANK[b][64 * f:64 * f + 64, :], dst, ALU.add).then_inc(res1_done.sem, 1)

        def residual2(s, job):
            b = job % 2
            dv.wait_ge(*w2_step.at(s.turn, 3 * job + 3))
            for f in range(2):
                dst = Y[64 * f:64 * f + 64, b, f:f + SEQ]
                v.scalar_tensor_tensor(dst, OUT_BANK[b][64 * f:64 * f + 64, :], ffn_param[64 * f:64 * f + 64, 8:9], dst,
                                       ALU.add, ALU.add).then_inc(res2_done.sem, 1)

        def body(s):
            for t in s.range:
                job, stage = s.stage(t)
                if stage == 2:
                    dv.wait_ge(*ffn_in.at(s.turn, 80 * (job + 1) if job < 1 else 80))
                    dv.wait_ge(*rstd_done.at(s.turn, job + 1))
                    if w1_done.any(s.turn, 3 * job):
                        dv.wait_ge(*w1_done.at(s.turn, 3 * job))
                    v.tensor_tensor(xn[:], dx[:], rstd[:], ALU.mult).then_inc(xh_done.sem, 1)
                    dv.wait_ge(*xh_done.at(s.turn, job + 1))
                    v.tensor_scalar(xn[:], xn[:], ffn_param[:, 0:1], ffn_param[:, 1:2], ALU.mult, ALU.add).then_inc(xn_done.sem, 1)
                if s.first and t + 3 < PAIRS:
                    high_weights(s, t + 3, 0)
                if t >= PAIRS and not s.last:
                    high_weights(s, t - PAIRS, 1)
                n = t + 2
                if s.unit(n):
                    rotate(s, n, 0)
                    rotate(s, n, 1)
                if stage == 1:
                    dv.wait_ge(*mean_done.at(s.turn, job + 1))
                    if xh_done.any(s.turn, job):
                        dv.wait_ge(*xh_done.at(s.turn, job))
                    if dsq_done.any(s.turn, job):
                        dv.wait_ge(*dsq_done.at(s.turn, job))
                    v.tensor_tensor(dx[:], Y[:, job % 2, 0:SEQ], TURN_BANK, ALU.subtract).then_inc(dx_done.sem, 1)
                if s.unit(n):
                    rotate_sin(s, n, 0)
                    rotate_sin(s, n, 1)
                if stage == 5:
                    residual2(s, job)
                if stage in (2, 3, 4):
                    j = stage - 2
                    rows = ROWS[j]
                    dv.wait_ge(*gate_done.at(s.turn, 3 * job + j + 1))
                    if w2_step.any(s.turn, 3 * job + j - 1):
                        dv.wait_ge(*w2_step.at(s.turn, 3 * job + j - 1))
                    v.scalar_tensor_tensor(act[0:rows, j % 2, :], V_BANK[0:rows, :], ffn_param[0:rows, 2 + j:3 + j], gate[0:rows, :],
                                           ALU.add, ALU.mult).then_inc(act_done.sem, 1)
                n = t + 1
                if t >= -1 and s.unit(n):
                    r = n % 2
                    bank = SCORE_BANK.rearrange("p (i k) -> p i k", k=64)
                    dv.wait_ge(*score_done.at(s.turn, n + 1))
                    if sub_done.any(s.turn, n - 1):
                        dv.wait_ge(*sub_done.at(s.turn, n - 1))
                    v.tensor_reduce(mx[:, r, :], bank, AX, ALU.max).then_inc(mx_done.sem, 1)
                    dv.wait_ge(*mx_done.at(s.turn, n + 1))
                    if pn_done.any(s.turn, n - 1):
                        dv.wait_ge(*pn_done.at(s.turn, n - 1))
                    if sum_done.any(s.turn, n - 1):
                        dv.wait_ge(*sum_done.at(s.turn, n - 1))
                    v.tensor_tensor(prob[:, r], bank, mx[:, r, :].unsqueeze(2).to_broadcast([P, 8, 64]), ALU.subtract).then_inc(sub_done.sem, 1)
                if s.unit(t + 2):
                    rope_last(s, t + 2, 0)
                if s.resplit(job, stage):
                    dv.wait_ge(*y_high_done.at(s.turn, job + 3))
                    v.tensor_tensor(y_low[:, job % 2, :], Y[:, job % 2, 0:SEQ], y_high[:, job % 2, :], ALU.subtract).then_inc(y_low_done.sem, 1)
                if s.unit(t + 2):
                    rope_last(s, t + 2, 1)
                if t >= -1 and s.unit(n):
                    dv.wait_ge(*exp_done.at(s.turn, n + 1))
                    if rec_done.any(s.turn, n - 1):
                        dv.wait_ge(*rec_done.at(s.turn, n - 1))
                    v.tensor_reduce(rs[:, r, :], prob[:, r], AX, ALU.add).then_inc(sum_done.sem, 1)
                    dv.wait_ge(*sum_done.at(s.turn, n + 1))
                    if pn_done.any(s.turn, n - 1):
                        dv.wait_ge(*pn_done.at(s.turn, n - 1))
                    v.reciprocal(ri[:, r, :], rs[:, r, :]).then_inc(rec_done.sem, 1)
                if stage == 0:
                    residual1(s, job)

        for b in range(2):
            dv.wait_ge(y_high_done.sem, b + 1)
            v.tensor_tensor(y_low[:, b, :], Y[:, b, 0:SEQ], y_high[:, b, :], ALU.subtract).then_inc(y_low_done.sem, 1)
        dv.wait_ge(pads_zero.sem, 4)
        dv.wait_ge(table_in.sem, 16)
        high_weights(Steps(0, True, False), 0, 0)
        all_turns(dv, body)

    @block.gpsimd
    def _(pool):
        def low_weights(s, pair, ahead):
            pool.wait_ge(*w_high_done.at(s.turn, PAIRS * ahead + pair + 1))
            nc.gpsimd.tensor_tensor(w_low[:, pair, :], w_raw[:, pair, :], w_high[:, pair, :], ALU.subtract).then_inc(w_split.sem, 1)

        def body(s):
            for t in s.range:
                if s.unit(t) and t >= 0:
                    r = t % 2
                    pool.wait_ge(*rec_done.at(s.turn, t + 1))
                    if t_done.any(s.turn, t - 1):
                        pool.wait_ge(*t_done.at(s.turn, t - 1))
                    nc.gpsimd.tensor_tensor(pn[:, r], prob[:, r], ri[:, r, :].unsqueeze(2).to_broadcast([P, 8, 64]), ALU.mult).then_inc(pn_done.sem, 1)
                if s.unit(t + 2):
                    pool.wait_ge(*high_done.at(s.turn, t + 3))
                    if norm_done.any(s.turn, 2 * (t + 2)):
                        pool.wait_ge(*norm_done.at(s.turn, 2 * (t + 2)))
                    nc.gpsimd.tensor_tensor(sq_low[:], sq[:, 1, :], sq_high[:], ALU.subtract).then_inc(low_done.sem, 1)
                    for which in range(2):
                        n = t + 2
                        pool.wait_ge(*sin_done.at(s.turn, 2 * n + which + 1))
                        if rope_done.any(s.turn, 3 * (n - 1) + 2 + which):
                            pool.wait_ge(*rope_done.at(s.turn, 3 * (n - 1) + 2 + which))
                        nc.gpsimd.tensor_tensor(turned[:, which, :], cos_part[:, which, :], sin_part[:, which, :], ALU.add).then_inc(add_done.sem, 1)
                if s.first and t + 3 < PAIRS:
                    low_weights(s, t + 3, 0)
                if t >= PAIRS and not s.last:
                    low_weights(s, t - PAIRS, 1)

        low_weights(Steps(0, True, False), 0, 0)
        all_turns(pool, body)


def build_last_norm(nc, ctx, x2, Y, out, C):
    def sb(name, shape, dt=F32):
        return ctx.enter_context(nc.sbuf_tensor("la_" + name, shape, dt))

    ps = C["psum"]
    total = sb("total", [P, 2, SEQ])
    centred = sb("centred", [P, 2, SEQ])
    ln = sb("ln", [P, 2, SEQ])
    res = sb("res", [P, 2, SEQ])
    sum_done = Flow(C["sems"].enter_context(nc.semaphore("la_sum_done")), 4)
    stored = Flow(C["sems"].enter_context(nc.semaphore("la_stored")), 32)
    s = C["norm"](2)

    def rows(b):
        return ps[:, b, :], ps[:, 2 + b, :]

    block = ctx.enter_context(nc.Block())

    @block.sync
    def _(sp):
        for b in range(2):
            sp.wait_ge(*s["scaled"].at(s["use"], b + 1))
            sp.dma_start(out[:, b, :], res[:, b, :]).then_inc(stored.sem, 16)
        sp.wait_ge(stored.sem, 32)

    @block.tensor
    def _(pe):
        for b in range(2):
            pe.wait_ge(sum_done.sem, 2 * b + 2)
            normalise(nc, "pe_mean", pe, s, b, total[:, b, :], None, (None, None), rows(b), C)
        for b in range(2):
            normalise(nc, "pe_var", pe, s, b, None, None, (centred, ln), rows(b), C)

    @block.scalar
    def _(ac):
        nc.scalar.preload_act_table_set("natural_log_exp_and_others")
        for b in range(2):
            normalise(nc, "act_square", ac, s, b, None, None, (centred, ln), None, C)
        for b in range(2):
            normalise(nc, "act_rstd", ac, s, b, None, None, (centred, ln), rows(b), C)

    @block.vector
    def _(dv):
        for b in range(2):
            for f in range(2):
                half = slice(64 * f, 64 * f + 64)
                nc.vector.tensor_tensor(total[half, b, :], Y[half, b, f:f + SEQ], x2[half, b, :], ALU.add).then_inc(sum_done.sem, 1)
        dv.wait_ge(sum_done.sem, 4)
        for b in range(2):
            normalise(nc, "dve_centre", dv, s, b, total[:, b, :], None, (centred, ln), rows(b), C)
        for b in range(2):
            normalise(nc, "dve_scale", dv, s, b, None, res[:, b, :], (centred, ln), None, C)


def program(nc, d, out, probes=None):
    d = {**d, "line": nc.dram_tensor("bias_line", (HEADS, SPAN), F32).ap(),
         "gates": nc.dram_tensor("gate_rows", (EXPERTS, BATCH, SEQ), F32).ap()}
    with ExitStack() as ctx:
        def sb(name, shape, dt=F32):
            return ctx.enter_context(nc.sbuf_tensor(name, shape, dt))

        C = {"sems": ctx, "psum": ctx.enter_context(nc.psum_tensor("banks", [P, 8, 512], F32))}
        Y = sb("stream", [P, 2, SEQ + 1])
        x2 = sb("x2", [P, 2, SEQ])
        steps = norm_steps(nc, ctx)
        C["rms"] = rms_steps(nc, ctx)
        C["norm"] = lambda use: {**steps, "use": use}
        consts = dict(ident=sb("ident", [P, P]), ident16=sb("ident16", [P, P], BF16), mask16=sb("mask16", [P, SEQ], BF16),
                      head_ones=sb("head_ones", [P, P]), mean_ones=sb("mean_ones", [P, P]))
        for name, t in consts.items():
            C[name] = t[:]
        fill = sb("fill", [P, 4])
        FILL = (("tiny", 2.0 ** -64), ("eps", 1e-5), ("ln_scale", float(0.5 * np.log(SS_SCALE))), ("one", 1.0))
        for i, (name, _) in enumerate(FILL):
            C[name] = fill[:, i:i + 1]
        C["const_in"] = Flow(C["sems"].enter_context(nc.semaphore("const_in")), 0)
        C["fill"] = Flow(C["sems"].enter_context(nc.semaphore("fill_done")), 0)
        C["const_n"], C["fill_n"] = 16 * (len(consts) + 1), len(FILL)
        probed = ctx.enter_context(nc.semaphore("probed")) if probes else None

        def probe(name, t, n):
            if probes:
                with nc.Block() as block:
                    @block.sync
                    def _(sp):
                        sp.dma_start(probes[name], t[:]).then_inc(probed, 16)
                        sp.wait_ge(probed, 16 * n)

        x = ctx.enter_context(nc.sbuf_tensor("x", [P, 2, SEQ], F32))
        h1 = ctx.enter_context(nc.sbuf_tensor("h1", [P, 2, SEQ], F32))
        x1 = ctx.enter_context(nc.sbuf_tensor("x1", [P, 2, SEQ], F32))
        weights = ExpertWeights(nc, ctx, C)
        with nc.Block() as block:
            @block.sync
            def _(sp):
                sp.dma_start(x[:], d["x"]).then_inc(C["const_in"].sem, 16)
                for name in consts:
                    sp.dma_start(C[name], d["c_" + name]).then_inc(C["const_in"].sem, 16)

            @block.scalar
            def _(ac):
                ac.wait_ge(C["const_in"].sem, C["const_n"])

            @block.vector
            def _(dv):
                for i, (_, value) in enumerate(FILL):
                    nc.vector.memset(fill[:, i:i + 1], value).then_inc(C["fill"].sem, 1)
        with ExitStack() as part:
            build_mamba(nc, part, x, h1, weights, d, C)
        probe("h1", h1, 1)
        cross = CrossPlaces(nc, ctx, C)
        with ExitStack() as part:
            build_moe(nc, part, x, h1, x1, weights, cross, d, C)
        probe("x1", x1, 2)
        stack = StackPlaces(nc, ctx, C)
        with ExitStack() as part:
            build_cross(nc, part, x1, x2, Y, cross, stack, d, C)
        probe("x2", x2, 3)
        with ExitStack() as part:
            build_stack(nc, part, Y, stack, d, C)
        with ExitStack() as part:
            build_last_norm(nc, part, x2, Y, out, C)


def head_rows():
    return [*range(0, 16), *range(32, 48), *range(16, 32), *range(48, 64)]

def stack_constants():
    half = np.arange(0, DH, 2, dtype=np.float32)
    inv_freq = (1.0 / np.float32(10000.0) ** (half / np.float32(DH))).astype(np.float32)
    t = np.arange(SEQ, dtype=np.float32)
    fr = t[:, None] * inv_freq[None, :]
    fr = np.concatenate([fr, fr], -1)
    bs = (half + np.float32(0.4 * DH)) / np.float32(1.4 * DH)
    power = (t - SEQ // 2) / np.float32(WIN // 2)
    sc = (bs[None, :] ** power[:, None]).astype(np.float32)
    sc = np.concatenate([sc, sc], -1)
    sign = np.where(np.arange(DH) < DH // 2, -1.0, 1.0).astype(np.float32)
    cos, sin = np.cos(fr), np.sin(fr) * sign
    rows = head_rows() * 1
    tabs = [cos * sc, sin * sc, cos / sc, sin / sc]
    rope = np.stack([np.tile(x[:, rows].T, (2, 1)) for x in tabs], 1).astype(np.float32)
    i = np.arange(32)[:, None]; j = np.arange(64)[None, :]
    ok = (j >= i) & (j <= i + 32)
    mask = np.tile(np.where(ok, 0.0, -1e30), (4, 8))
    mask[0:64, 0:32] = -1e30
    mask = mask.astype(np.dtype("bfloat16"))
    ho = np.kron(np.eye(2), np.ones((64, 64))).astype(np.float32)
    return dict(rope=rope, c_mask16=mask, c_ident=np.eye(128, dtype=np.float32), c_ident16=np.eye(128).astype(np.dtype("bfloat16")),
                c_head_ones=ho, c_mean_ones=np.full((128, 128), 1 / 128, np.float32))

def stack_inputs(Wqkv, q_scale, k_scale, Wo, ln_g, ln_b, W1, b1, W2, b2):
    rows = np.array(head_rows())
    partner = (rows + 32) % 64
    L = Wqkv.shape[0]
    w = Wqkv.reshape(L, 128, 3, 16, 64)
    pairs = lambda t: t.reshape(L, 128, 8, 128)
    w_qk = np.concatenate([pairs(w[:, :, 0][..., rows]), pairs(w[:, :, 1][..., rows])], -1)
    rs = np.stack([np.tile(x, (1, 2)) for x in (q_scale[:, rows], q_scale[:, partner], k_scale[:, rows], k_scale[:, partner])], -1)
    wo = np.ascontiguousarray(Wo.reshape(L, 8, 128, 128).transpose(0, 2, 1, 3))
    def cols(v):
        o = np.zeros((L, 384), v.dtype); o[:, :HID] = v
        return list(o.reshape(L, 3, 128).transpose(1, 0, 2))
    prm = np.stack([ln_g, ln_b, *cols(b1[:, :HID]), *cols(b1[:, HID:]), b2], -1)
    return dict(w_qk=w_qk, w_v=pairs(w[:, :, 2]), rope_scale=np.ascontiguousarray(rs), wo=wo, w1=W1, w2=W2, ffn_param=np.ascontiguousarray(prm))

def front_inputs(i):
    A = lambda n: i['L0_attn_' + n]
    blocks = lambda v: np.stack([v[0:128], v[128:256]], 1)
    xproj = A('x_proj_w')
    o = {}
    o['x'] = np.ascontiguousarray(i['x'].transpose(2, 0, 1))
    o['rms1'] = A('rms1_w')[:, None]; o['rms2'] = A('rms2_w')[:, None]
    o['in_w'] = A('in_proj_w').reshape(128, 4, 128)
    o['xdt_w'] = blocks(xproj[:, 0:64])
    o['xbc_w'] = np.tile(blocks(xproj[:, 64:96]), (1, 1, 3))
    o['dt_w'] = A('dt_proj_w').reshape(64, 2, 128)
    o['out_w'] = blocks(A('out_proj_w'))
    chan = np.concatenate([A('conv_w')[:, 0, :], A('conv_b')[:, None], A('dt_proj_b')[:, None], A('D_skip')[:, None]], 1)
    o['chan'] = blocks(chan)
    o['a_log'] = blocks(A('A_log'))
    o['router'] = A('router_w')
    o['wg'] = A('Wg'); o['wu'] = A('Wu')
    o['wd'] = A('Wd').reshape(8, 4, 128, 128).transpose(0, 2, 1, 3)
    o['xwq'] = i['L0_xattn_Wq']; o['xwk'] = i['L0_xattn_Wkv'][:, :128]; o['xwv'] = i['L0_xattn_Wkv'][:, 128:]
    o['xwo'] = i['L0_xattn_Wo']; o['rel'] = i['L0_xattn_rel_bias']
    o['ctxT'] = np.tile(i['ctx_1024'][:, ::-1].transpose(2, 0, 1)[:, :, None, :], (1, 1, 4, 1))
    return {k: np.ascontiguousarray(v) for k, v in o.items()}

def buckets(rel):
    nb = 16
    out = (rel > 0).astype(np.int32) * nb
    rel = np.abs(rel)
    me = nb // 2
    rf = np.maximum(rel, 1).astype(np.float32)
    large = me + (np.log(rf / np.float32(me)) / np.float32(np.log(128 / me)) * np.float32(nb - me)).astype(np.int32)
    large = np.minimum(large, nb - 1)
    return out + np.where(rel < me, rel, large)

def front_constants():
    sel = np.zeros((96, 32, 128), np.float32)
    for p in range(96): sel[p, p % 32] = 1
    order = np.broadcast_to(np.arange(8, 0, -1, dtype=np.float32), (128, 8, 8))
    b = buckets(31 - np.arange(544))
    oh = (np.arange(32)[:, None] == b[None]).astype(np.float32)
    ho = np.kron(np.eye(16), np.ones((8, 1))).astype(np.float32)
    qu = np.zeros((128, 16), np.float32)
    for p in range(128):
        qu[p, [h for h in range(16) if h % 4 == p // 32]] = 1
    return dict(select=sel.astype(np.dtype("bfloat16")), order=np.ascontiguousarray(order), onehot=oh, head_of=ho, quarter=qu)


def laid_out(inputs):
    stack = {name[len("L0_ffn_"):]: a for name, a in inputs.items() if name.startswith("L0_ffn_")}
    return {**stack_inputs(**stack), **front_inputs(inputs)}


def shape_constants():
    return {**stack_constants(), **front_constants()}


def kernel(**inputs):
    import concourse.bacc as _bacc
    from concourse.bass_utils import run_bass_kernel_spmd as _run

    inputs = {name: np.asarray(a) for name, a in inputs.items()}
    arrays = {"in_" + name: np.ascontiguousarray(a) for name, a in {**laid_out(inputs), **shape_constants()}.items()}
    nc = _bacc.Bacc("TRN2", target_bir_lowering=False, num_devices=1)
    d = {name[3:]: nc.dram_tensor(name, a.shape, mybir.dt.from_np(a.dtype), kind="ExternalInput").ap() for name, a in arrays.items()}
    out = nc.dram_tensor("out", (P, BATCH, SEQ), F32, kind="ExternalOutput").ap()
    program(nc, d, out)
    got = _run(nc, [arrays], core_ids=[0]).results[0]["out"]
    return np.ascontiguousarray(got.transpose(1, 2, 0))
```
